# Optimizing a Trainium2 kernel written in Bass

```python
import numpy as np
import jax
import jax.numpy as jnp

def _softmax(x, axis=-1):
    return jax.nn.softmax(x, axis=axis)

def _gelu(x):
    return jax.nn.gelu(x, approximate=True)

def _silu(x):
    return jax.nn.silu(x)

def _sigmoid(x):
    return jax.nn.sigmoid(x)

def _layernorm(x, axis=-1, eps=1e-05):
    m = jnp.mean(x, axis=axis, keepdims=True)
    v = jnp.var(x, axis=axis, keepdims=True)
    return (x - m) / jnp.sqrt(v + eps)

def _scatter_add(tgt, idx, src, axis=0):
    return tgt.at[idx].add(src)

def _segment_sum(src, seg, n):
    return jax.ops.segment_sum(src, seg, n)
kernel_name = 'mk_gnn_ffn_d1_gnn_r8_e819bc'

def setup_inputs(seed: int=0):
    np.random.seed(seed)
    _w = jnp.asarray

    def _rec_inputs():
        import jax
        import jax.numpy as jnp
        _gk = jax.random.key(seed)
        x = -0.0002117 + 1 * jax.random.normal(jax.random.fold_in(_gk, 1), (12500, 256), jnp.float32)
        src = jax.random.randint(jax.random.fold_in(_gk, 2), (200000,), 0, 12500, jnp.int32)
        dst = jnp.minimum((12500 * jax.random.uniform(jax.random.fold_in(_gk, 3), (200000,)) ** 2.0).astype(jnp.int32), 99999)
        _o = jnp.argsort(dst, stable=True)
        src = src[_o]
        dst = dst[_o]
        return (x, src, dst)
    x, src, dst = _rec_inputs()

    def _L0_gnn_setup():
        import jax, jax.numpy as jnp
        import numpy as np
        N = 12500
        E = 200000
        D = 256
        BN_EPS = 1e-05
        key = jax.random.key(seed)
        ks = jax.random.split(key, 6)
        node_feats = jax.random.normal(ks[0], (N, D), dtype=jnp.float32)
        src = jax.random.randint(ks[1], (E,), 0, N, dtype=jnp.int64)
        dst = jax.random.randint(ks[2], (E,), 0, N, dtype=jnp.int64)
        eps = jnp.zeros((1,), dtype=jnp.float32)
        W1 = jax.random.normal(ks[3], (D, 2 * D), dtype=jnp.float32) * (1.0 / np.sqrt(D))
        b1 = jnp.zeros((2 * D,), dtype=jnp.float32)
        W2 = jax.random.normal(ks[4], (2 * D, D), dtype=jnp.float32) * (1.0 / np.sqrt(2 * D))
        b2 = jnp.zeros((D,), dtype=jnp.float32)
        gamma = jnp.ones((D,), dtype=jnp.float32)
        beta = jnp.zeros((D,), dtype=jnp.float32)
        return {'node_feats': node_feats, 'src': src, 'dst': dst, 'eps': eps, 'W1': W1, 'b1': b1, 'W2': W2, 'b2': b2, 'gamma': gamma, 'beta': beta}
    _L0_gnn_all = _L0_gnn_setup()
    _L0_gnn_in = {k: v for k, v in _L0_gnn_all.items() if k in ('eps', 'W1', 'b1', 'W2', 'b2', 'gamma', 'beta')}
    del _L0_gnn_all

    def _L0_ffn_setup():
        import math
        import jax, jax.numpy as jnp
        import numpy as np
        CAPACITY_FACTOR = 1.25
        key = jax.random.key(seed)
        ks = jax.random.split(key, 5)
        B, L, D, F, E = (8, 1024, 256, 1024, 8)
        h = jax.random.normal(ks[0], (B, L, D), dtype=jnp.float32)
        gate_w = jax.random.normal(ks[1], (D, E), dtype=jnp.float32) * 0.02
        gate_b = jnp.zeros((E,), dtype=jnp.float32)
        w1 = jax.random.normal(ks[2], (E, D, F), dtype=jnp.float32) * (1.0 / math.sqrt(D))
        b1 = jnp.zeros((E, F), dtype=jnp.float32)
        w2 = jax.random.normal(ks[3], (E, F, D), dtype=jnp.float32) * (1.0 / math.sqrt(F))
        b2 = jnp.zeros((E, D), dtype=jnp.float32)
        return {'h': h, 'gate_w': gate_w, 'gate_b': gate_b, 'w1': w1, 'b1': b1, 'w2': w2, 'b2': b2}
    _L0_ffn_all = _L0_ffn_setup()
    _L0_ffn_in = {k: v for k, v in _L0_ffn_all.items() if k in ('gate_w', 'gate_b', 'w1', 'b1', 'w2', 'b2')}
    del _L0_ffn_all
    return {'x': x, 'src': src, 'dst': dst, 'L0_gnn_eps': _L0_gnn_in['eps'], 'L0_gnn_W1': _L0_gnn_in['W1'], 'L0_gnn_b1': _L0_gnn_in['b1'], 'L0_gnn_W2': _L0_gnn_in['W2'], 'L0_gnn_b2': _L0_gnn_in['b2'], 'L0_gnn_gamma': _L0_gnn_in['gamma'], 'L0_gnn_beta': _L0_gnn_in['beta'], 'L0_ffn_gate_w': _L0_ffn_in['gate_w'], 'L0_ffn_gate_b': _L0_ffn_in['gate_b'], 'L0_ffn_w1': _L0_ffn_in['w1'], 'L0_ffn_b1': _L0_ffn_in['b1'], 'L0_ffn_w2': _L0_ffn_in['w2'], 'L0_ffn_b2': _L0_ffn_in['b2']}

def reference(x, src, dst, L0_gnn_eps, L0_gnn_W1, L0_gnn_b1, L0_gnn_W2, L0_gnn_b2, L0_gnn_gamma, L0_gnn_beta, L0_ffn_gate_w, L0_ffn_gate_b, L0_ffn_w1, L0_ffn_b1, L0_ffn_w2, L0_ffn_b2):
    import jax
    import jax.numpy as jnp

    def _L0_gnn_ref(node_feats, src, dst, eps, W1, b1, W2, b2, gamma, beta):
        import jax, jax.numpy as jnp
        import numpy as np
        N = 12500
        E = 200000
        D = 256
        BN_EPS = 1e-05
        n = node_feats.shape[0]
        neigh = jax.ops.segment_sum(node_feats[src], dst, num_segments=n)
        h = (1.0 + eps) * node_feats + neigh
        h = jax.nn.relu(h @ W1 + b1) @ W2 + b2
        mean = jnp.mean(h, axis=0)
        var = jnp.mean(jnp.square(h - mean), axis=0)
        h = (h - mean) * jax.lax.rsqrt(var + BN_EPS) * gamma + beta
        return h

    def _L0_ffn_ref(h, gate_w, gate_b, w1, b1, w2, b2):
        import math
        import jax, jax.numpy as jnp
        import numpy as np
        CAPACITY_FACTOR = 1.25
        B, L, D = h.shape
        E = gate_w.shape[1]
        T = B * L
        C = max(1, math.ceil(CAPACITY_FACTOR * T / E))
        x = h.reshape(T, D)
        logits = x @ gate_w + gate_b
        probs = jax.nn.softmax(logits, axis=-1)
        idx = jnp.argmax(probs, axis=-1)
        prb = jnp.take_along_axis(probs, idx[:, None], axis=1)[:, 0]
        one_hot = jax.nn.one_hot(idx, E, dtype=jnp.float32)
        pos = (jnp.cumsum(one_hot, axis=0) * one_hot).sum(-1).astype(jnp.int32) - 1
        kept = pos < C
        pos_safe = jnp.where(kept, pos, C)
        buf = jnp.zeros((E, C, D), dtype=h.dtype).at[idx, pos_safe].set(x, mode='drop')
        hmid = jax.nn.relu(jnp.einsum('ecd,edf->ecf', buf, w1) + b1[:, None, :])
        ybuf = jnp.einsum('ecf,efd->ecd', hmid, w2) + b2[:, None, :]
        pos_g = jnp.minimum(pos, C - 1)
        y_tok = ybuf[idx, pos_g] * (prb * kept)[:, None]
        y = y_tok.reshape(B, L, D)
        y = jnp.nan_to_num(y, nan=0.0, posinf=10000.0, neginf=-10000.0)
        return y
    x = x + _L0_gnn_ref(_layernorm(x, axis=-1), src, dst, L0_gnn_eps, L0_gnn_W1, L0_gnn_b1, L0_gnn_W2, L0_gnn_b2, L0_gnn_gamma, L0_gnn_beta)
    x = x + _L0_ffn_ref(_layernorm(x, axis=-1)[None], L0_ffn_gate_w, L0_ffn_gate_b, L0_ffn_w1, L0_ffn_b1, L0_ffn_w2, L0_ffn_b2)[0]
    return x

_drawn_inputs = setup_inputs


def setup_inputs(seed=0):
    import zlib

    import numpy as np

    out = dict(_drawn_inputs(seed))
    spreads = {'L0_gnn_b1': (0.0, 0.408),
     'L0_gnn_b2': (0.0, 0.8),
     'L0_gnn_gamma': (1.0, 0.2),
     'L0_gnn_beta': (0.0, 0.1),
     'L0_ffn_gate_b': (0.0, 0.1),
     'L0_ffn_b1': (0.0, 0.8),
     'L0_ffn_b2': (0.0, 0.613)}
    factors = {}
    for name, (base, spread) in spreads.items():
        noise = np.random.default_rng([zlib.crc32(name.encode()), seed]).standard_normal(out[name].shape)
        drawn = base * np.exp(spread * noise) if base else spread * noise
        out[name] = jnp.asarray(drawn.astype(out[name].dtype))
    for name, factor in factors.items():
        out[name] = (out[name] * factor).astype(out[name].dtype)
    return out
```

```python
from contextlib import ExitStack

import numpy as np

import concourse.bass as bass
from concourse import mybir

ALU = mybir.AluOpType
ACT = mybir.ActivationFunctionType
AX = mybir.AxisListType
RMAX = bass.bass_isa.ReduceOp.max
F32 = mybir.dt.float32
F16 = mybir.dt.float16
I32 = mybir.dt.int32
U32 = mybir.dt.uint32
U8 = mybir.dt.uint8

P = 128
N = 12500
D = 256
NE = 200000
NX = 8
F = 1024
CAP = -(-5 * N // (4 * NX))
DK = D // P
H1 = 2 * D
H1C = H1 // P
FC = F // P
QT = 4
QN = QT * P
NQ = -(-N // QN)
NB = NQ * QT
ET = -(-NE // P)
EFULL = NE // P
ETAIL = NE - EFULL * P
GT = 8
RG = 4
NG = -(-ET // (GT * RG)) * RG
EP = NG * GT
PAD_DST = NB * P - QN + 255
SLOTS = QN * -(-CAP // QN)
SG = SLOTS // QN
ROW = D + 12
R5 = 5
LOW = 2048.0
EPS = 1e-5
BIG = 3.4028234663852886e38
SKIP = float(1 << 24)

assert NQ % R5 == 0 and NG % RG == 0 and D == 2 * P and PAD_DST >= N


def walk(engine, stages, count, ring):
    def step(s):
        for stage, lag in stages:
            if 0 <= s - lag < count:
                stage(s - lag, (s - lag) % ring, (s - lag) // ring)

    for s in range(ring):
        step(s)
    with engine.Fori(1, count // ring - 1) as it:
        for j in range(ring):
            for stage, lag in stages:
                stage(it * ring + j - lag, (j - lag) % ring, it if j >= lag else it - 1)
    for s in range(count - ring, count + max(lag for _, lag in stages)):
        step(s)


def wait_count(engine, sem, value, register, step=1):
    if isinstance(value, int):
        engine.wait_ge(sem, value)
    else:
        engine.wait_ge(sem, register)
        engine.reg_add(register, register, step)


def counter(engine, name, start):
    register = engine.alloc_register(name)
    engine.reg_mov(register, start)
    return register


def at(q, n=1):
    return bass.ds(q * n, n)


def kernel_program(nc, x, src, dst, src_tail, dst_tail, eps, W1, b1, W2, b2, gamma, beta, gate_w, gate_b,
                   w1, xb1, w2, xb2, out):
    table = nc.dram_tensor("table", (NB * P, 2 * D), F16, kind="Internal").ap()
    buf = nc.dram_tensor("slot_rows", (NX * SLOTS, ROW), F32, kind="Internal").ap()
    with ExitStack() as whole:
        def keep(name, shape, dt):
            return whole.enter_context(nc.sbuf_tensor(name, shape, dt))

        ident = keep("ident", [P, P], F32)
        onesf = keep("onesf", [P, P], F32)
        epsc = keep("epsc", [P, 1], F32)

        with ExitStack() as gnn:
            def hold(name, shape, dt):
                return gnn.enter_context(nc.sbuf_tensor(name, shape, dt))

            nodes = hold("nodes", [P, NQ, QT * D], F32)
            src_all = hold("src_all", [P, EP], I32)
            dst_all = hold("dst_all", [P, EP], F32)
            ctl = hold("ctl", [P, NG], I32)
            base = hold("base", [P, NB], F32)
            iota = hold("iota", [P, P], F16)
            stats = hold("stats", [P, DK, NQ * 6], F32)
            W1s = hold("W1s", [P, DK, H1], F32)
            W2s = hold("W2s", [P, H1C, D], F32)
            b1s = hold("b1s", [P, H1C], F32)
            b2s = hold("b2s", [P, DK], F32)
            gam = hold("gam", [P, DK], F32)
            bet = hold("bet", [P, DK], F32)
            stage_norm(nc, x, src, dst, src_tail, dst_tail, eps, W1, b1, W2, b2, gamma, beta, table,
                       ident, onesf, epsc, nodes, src_all, dst_all, ctl, base, iota, W1s, W2s, b1s, b2s, gam, bet)
            stage_edges(nc, table, buf, ident, nodes, src_all, dst_all, ctl, base, iota, stats, W1s, W2s, b1s, b2s)
            stage_route(nc, x, gate_w, gate_b, buf, out, ident, onesf, epsc, nodes, stats, gam, bet)
        stage_experts(nc, buf, w1, xb1, w2, xb2, out, ident)


def stage_norm(nc, x, src, dst, src_tail, dst_tail, eps, W1, b1, W2, b2, gamma, beta, table,
               ident, onesf, epsc, nodes, src_all, dst_all, ctl, base, iota, W1s, W2s, b1s, b2s, gam, bet):
    with ExitStack() as ctx:
        def sb(name, shape, dt):
            return ctx.enter_context(nc.sbuf_tensor(name, shape, dt))

        def sem(name):
            return ctx.enter_context(nc.semaphore(name))

        xin = sb("n_xin", [P, R5, QT, D], F32)
        pair = sb("n_pair", [P, R5, QT, 2 * D], F16)
        st = sb("n_st", [P, R5, QT, 6], F32)
        mv = sb("n_mv", [P, R5, QT, 2], F32)
        sd = sb("n_sd", [P, R5, QT], F32)
        off = sb("n_off", [P, R5, QT], F32)
        epsl = sb("n_epsl", [P, 1], F32)
        rsl = sb("n_rsl", [P, R5, QT], F32)
        selfs = sb("n_selfs", [P, 1], F32)
        epsb = sb("n_epsb", [P, 1], F32)
        dsti = sb("n_dsti", [P, EP], I32)
        ext = sb("n_ext", [P, 2, NG], F32)
        low_of = sb("n_low_of", [P, NG], F32)
        allx = sb("n_allx", [P, 2, NG], F32)
        blki = sb("n_blki", [P, 2, NG], I32)
        blks = sb("n_blks", [P, 2, NG], I32)
        sfx = sb("n_sfx", [P, 2, NG + 128], F32)
        sfi = sb("n_sfi", [P, NG], I32)
        sfs = sb("n_sfs", [P, NG], I32)
        packed = sb("n_packed", [P, 2, NG], F32)

        s_x = [sem(f"n_x{j}") for j in range(R5)]
        s_tab = [sem(f"n_tab{j}") for j in range(R5)]
        s_pad, s_src, s_dst, s_w, s_eps = sem("n_pad"), sem("n_src"), sem("n_dst"), sem("n_w"), sem("n_eps_in")
        s_self, s_epsc, s_const, s_id = sem("n_self"), sem("n_epsc"), sem("n_const"), sem("n_id")
        s_stat, s_var, s_std, s_rst, s_xn = sem("n_stat"), sem("n_var"), sem("n_std"), sem("n_rst"), sem("n_xn")
        s_hi, s_term, s_lo = sem("n_hi"), sem("n_term"), sem("n_lo")
        s_ext, s_all, s_rng = sem("n_ext_s"), sem("n_all"), sem("n_rng")

        with nc.Block() as block:
            @block.sync
            def _(sp):
                def load(q, j, rnd):
                    if not (isinstance(rnd, int) and rnd == 0):
                        sp.wait_ge(s_lo, q - R5 + 1)
                        sp.wait_ge(s_term, q - R5 + 1)
                    if isinstance(q, int) and q == NQ - 1:
                        sp.dma_start(xin[:, j, 0, :], x[q * QN:q * QN + P, :]).then_inc(s_x[j], 16)
                        sp.dma_start(xin[0:N - q * QN - P, j, 1, :], x[q * QN + P:N, :]).then_inc(s_x[j], 16)
                    else:
                        sp.dma_start(xin[:, j, :, :],
                                     x[at(q, QN), :].rearrange("(t p) d -> p t d", p=P)).then_inc(s_x[j], 16)

                def store(q, j, rnd):
                    sp.wait_ge(s_lo, q + 1)
                    sp.dma_start(table[at(q, QN), :].rearrange("(t p) d -> p t d", p=P),
                                 pair[:, j, :, :]).then_inc(s_tab[j], 16)

                sp.dma_start(epsb[:, :], eps.unsqueeze(0).broadcast_to((P, 1))).then_inc(s_eps, 16)
                for q in range(2):
                    load(q, q, 0)
                sp.wait_ge(s_pad, 2)
                sp.dma_start(dsti[:, 0:EFULL], dst).then_inc(s_dst, 16)
                sp.dma_start(dsti[0:ETAIL, EFULL:EFULL + 1], dst_tail).then_inc(s_dst, 16)
                for q in range(2, R5):
                    load(q, q, 0)
                sp.dma_start(src_all[:, 0:EFULL], src).then_inc(s_src, 16)
                sp.dma_start(src_all[0:ETAIL, EFULL:EFULL + 1], src_tail).then_inc(s_src, 16)
                with sp.Fori(1, NQ // R5 - 1) as it:
                    for j in range(R5):
                        store(it * R5 + j - R5, j, it - 1)
                        load(it * R5 + j, j, it)
                for q in range(NQ - R5, NQ):
                    store(q - R5, q % R5, q // R5 - 1)
                    load(q, q % R5, q // R5)
                for q in range(NQ - R5, NQ):
                    store(q, q % R5, q // R5)
                for j in range(R5):
                    sp.wait_ge(s_tab[j], 16 * (NQ // R5))
                sp.wait_ge(s_src, 32)

            @block.gpsimd
            def _(pool):
                nc.gpsimd.memset(src_all[:, EFULL:EP], 0).then_inc(s_pad, 1)
                nc.gpsimd.memset(dsti[:, EFULL:EP], PAD_DST).then_inc(s_pad, 1)
                nc.gpsimd.memset(epsl[:, :], EPS / LOW**2).then_inc(s_epsc, 1)
                nc.gpsimd.memset(epsc[:, :], EPS).then_inc(s_const, 1)
                nc.gpsimd.memset(ident[:, :], 0.0).then_inc(s_id, 1)
                nc.gpsimd.memset(onesf[:, :], 1.0).then_inc(s_const, 1)
                nc.gpsimd.iota(base[:, :], pattern=[[P, NB]], base=0, channel_multiplier=0,
                               allow_small_or_imprecise_dtypes=True).then_inc(s_const, 1)
                nc.gpsimd.iota(iota[:, :], pattern=[[1, P]], base=0, channel_multiplier=0,
                               allow_small_or_imprecise_dtypes=True).then_inc(s_const, 1)
                pool.wait_ge(s_id, 1)
                nc.gpsimd.affine_select(out=ident[:, :], in_=ident[:, :], compare_op=ALU.not_equal, fill=1.0,
                                        base=0, pattern=[[-1, P]], channel_multiplier=1).then_inc(s_id, 1)

                def term(q, j, rnd):
                    wait_count(pool, s_xn, q + 1, normed)
                    nc.gpsimd.tensor_tensor(nodes[:, at(q), :].rearrange("p a b -> p (a b)"),
                                            xin[:, j, :, :].rearrange("p t d -> p (t d)"),
                                            selfs[:, 0:1].broadcast_to((P, QT * D)), ALU.mult).then_inc(s_term, 1)

                def extremes(q, j, rnd):
                    if isinstance(q, int) and q == R5 - 1:
                        pool.wait_ge(s_ext, 3)
                        nc.gpsimd.partition_all_reduce(allx[:, :, :].rearrange("p a g -> p (a g)"),
                                                       ext[:, :, :].rearrange("p a g -> p (a g)"), P,
                                                       RMAX).then_inc(s_all, 1)

                normed = counter(pool, "n_normed", R5 + 1)
                pool.wait_ge(s_self, 1)
                walk(pool, [(term, 0), (extremes, 0)], NQ, R5)
                pool.wait_ge(s_id, 2)
                pool.wait_ge(s_const, 4)

            @block.scalar
            def _(act):
                act.dma_start(W1s[:, :, :], W1.rearrange("(k p) f -> p k f", p=P)).then_inc(s_w, 16)
                act.dma_start(W2s[:, :, :], W2.rearrange("(k p) f -> p k f", p=P)).then_inc(s_w, 16)
                with nc.allow_non_contiguous_dma(reason="small vectors"):
                    for tile, vector in ((b1s, b1), (b2s, b2), (gam, gamma), (bet, beta)):
                        act.dma_start(tile[:, :], vector.rearrange("(c p) -> p c", p=P)).then_inc(s_w, 16)

                def std(q, j, rnd):
                    act.wait_ge(s_var, q + 1)
                    nc.scalar.activation(sd[:, j, :], mv[:, j, :, 1], ACT.Sqrt, scale=1.0 / LOW**2,
                                         bias=epsl[:, 0:1]).then_inc(s_std, 1)

                def parts(q, j, rnd):
                    act.wait_ge(s_rst, q * 2 + 2)
                    for t in range(QT):
                        ins = nc.scalar.activation(xin[:, j, t, :], xin[:, j, t, :], ACT.Identity,
                                                   bias=off[:, j, t:t + 1], scale=rsl[:, j, t:t + 1])
                    ins.then_inc(s_xn, 1)
                    if not (isinstance(rnd, int) and rnd == 0):
                        act.wait_ge(s_tab[j], rnd * 16)
                    act.wait_ge(s_xn, q + 1)
                    nc.scalar.activation(pair[:, j, :, 0:D], xin[:, j, :, :], ACT.Identity,
                                         scale=1.0 / LOW).then_inc(s_hi, 1)

                act.wait_ge(s_epsc, 1)
                walk(act, [(std, 0), (parts, 1)], NQ, R5)
                act.wait_ge(s_w, 96)

            @block.vector
            def _(dve):
                dve.wait_ge(s_eps, 16)
                nc.vector.tensor_scalar(selfs[:, :], epsb[:, :], 1.0, 1.0 / LOW, ALU.add,
                                        ALU.mult).then_inc(s_self, 1)

                stat_seen = counter(dve, "n_stat_seen", R5 + 1)

                def stat(q, j, rnd):
                    if isinstance(q, int) and q == NQ - 1:
                        dve.wait_ge(s_x[j], 16 * rnd + 32)
                    else:
                        dve.wait_ge(s_x[j], rnd * 16 + 16)
                    for t in range(QT):
                        ins = nc.vector.bn_stats(st[:, j, t, :], xin[:, j, t, :])
                    ins.then_inc(s_stat, 1)
                    wait_count(dve, s_stat, q + 1, stat_seen)
                    for t in range(QT):
                        ins = nc.vector.bn_aggr(mv[:, j, t, :], st[:, j, t, :])
                    ins.then_inc(s_var, 1)

                def norm(q, j, rnd):
                    dve.wait_ge(s_std, q + 1)
                    nc.vector.reciprocal(rsl[:, j, :], sd[:, j, :]).then_inc(s_rst, 1)
                    dve.wait_ge(s_rst, q * 2 + 1)
                    nc.vector.scalar_tensor_tensor(out=off[:, j, :], in0=mv[:, j, :, 0], scalar=-1.0,
                                                   in1=rsl[:, j, :], op0=ALU.mult, op1=ALU.mult).then_inc(s_rst, 1)

                def low(q, j, rnd):
                    dve.wait_ge(s_hi, q + 1)
                    nc.vector.scalar_tensor_tensor(
                        out=pair[:, j, :, D:2 * D], in0=pair[:, j, :, 0:D], scalar=-LOW, in1=xin[:, j, :, :],
                        op0=ALU.mult, op1=ALU.add).then_inc(s_lo, 1)

                def ranges(q, j, rnd):
                    if not isinstance(q, int):
                        return
                    if q == 3:
                        dve.wait_ge(s_dst, 32)
                        nc.vector.tensor_copy(dst_all[:, :], dsti[:, :]).then_inc(s_rng, 1)
                        dve.wait_ge(s_rng, 1)
                        by_group = dst_all[:, :].rearrange("p (g t) -> p g t", t=GT)
                        nc.vector.tensor_reduce(low_of[:, :], by_group, AX.X, ALU.min).then_inc(s_ext, 1)
                        nc.vector.tensor_reduce(ext[:, 1, :], by_group, AX.X, ALU.max).then_inc(s_ext, 1)
                        dve.wait_ge(s_ext, 2)
                        nc.vector.tensor_scalar(ext[:, 0, :], low_of[:, :], -1.0, None, ALU.mult).then_inc(s_ext, 1)
                    if q == NQ - R5:
                        link = [1]

                        def then(ins):
                            link[0] += 1
                            ins.then_inc(s_rng, 1)
                            dve.wait_ge(s_rng, link[0])

                        dve.wait_ge(s_all, 1)
                        nc.vector.tensor_scalar(blki[:, 0, :], allx[:, 0, :], -1.0, None, ALU.mult).then_inc(s_rng, 1)
                        nc.vector.tensor_copy(blki[:, 1, :], allx[:, 1, :]).then_inc(s_rng, 1)
                        link[0] += 2
                        dve.wait_ge(s_rng, link[0])
                        then(nc.vector.tensor_scalar(blks[:, :, :], blki[:, :, :], 7, None, ALU.arith_shift_right))
                        then(nc.vector.memset(sfx[:, :, :], float(NB)))
                        then(nc.vector.tensor_copy(sfx[:, 0, 0:NG - 1], blks[:, 0, 1:NG]))
                        for k in range(8):
                            then(nc.vector.tensor_tensor(sfx[:, (k + 1) % 2, 0:NG], sfx[:, k % 2, 0:NG],
                                                         sfx[:, k % 2, 1 << k:(1 << k) + NG], ALU.min))
                        then(nc.vector.tensor_copy(sfi[:, :], sfx[:, 0, 0:NG]))
                        then(nc.vector.tensor_scalar(sfs[:, :], sfi[:, :], 2, None, ALU.arith_shift_right))
                        then(nc.vector.tensor_scalar(packed[:, 0, :], blks[:, 1, :], 128.0, 128.0, ALU.mult, ALU.add))
                        then(nc.vector.scalar_tensor_tensor(out=packed[:, 1, :], in0=sfs[:, :], scalar=16384.0,
                                                            in1=packed[:, 0, :], op0=ALU.mult, op1=ALU.add))
                        nc.vector.tensor_tensor(ctl[:, :], packed[:, 1, :], blks[:, 0, :], ALU.add)

                walk(dve, [(stat, 0), (norm, 1), (low, 2), (ranges, 0)], NQ, R5)


def stage_edges(nc, table, buf, ident, nodes, src_all, dst_all, ctl, base, iota, stats, W1s, W2s, b1s, b2s):
    with ExitStack() as ctx:
        def sb(name, shape, dt):
            return ctx.enter_context(nc.sbuf_tensor(name, shape, dt))

        def psum(name, shape, dt):
            return ctx.enter_context(nc.psum_tensor(name, shape, dt))

        def sem(name):
            return ctx.enter_context(nc.semaphore(name))

        ZR = 8
        got = sb("e_got", [P, RG, GT, 2 * D], F16)
        idx = sb("e_idx", [P, RG, GT], I32)
        rel = sb("e_rel", [P, GT], F16)
        hot = sb("e_hot", [P, 2, GT, P], F16)
        part = sb("e_part", [P, D], F32)
        hrow = sb("e_hrow", [P, QT, D], F32)
        hT = sb("e_hT", [P, DK, QN], F32)
        mid = sb("e_mid", [P, H1C, QN], F32)
        zero = sb("e_zero", [P, ZR * ROW], F32)
        sums = psum("e_sums", [P, 2, 2 * D], F32)
        turned = psum("e_turned", [P, DK, QN], F32)
        up = psum("e_up", [P, 2, QN], F32)
        down = psum("e_down", [P, DK, QN], F32)

        s_flush = sem("e_flush")
        s_free, s_idx, s_zero, s_zeroed = sem("e_free"), sem("e_idx_s"), sem("e_zero_s"), sem("e_zeroed")
        s_got = [sem(f"e_got{r}") for r in range(RG)]
        s_rel, s_hot, s_sum, s_part, s_add = sem("e_rel_s"), sem("e_hot_s"), sem("e_sum"), sem("e_part_s"), sem("e_add")
        s_hrow, s_turn, s_hT, s_up, s_mid, s_down, s_h2, s_stat = (
            sem("e_hrow_s"), sem("e_turn"), sem("e_hT_s"), sem("e_up_s"), sem("e_mid_s"), sem("e_down_s"),
            sem("e_h2"), sem("e_stat"))

        blocks_of = nodes[:, :, :].rearrange("p q (t d) -> p (q t) d", d=D)

        with nc.Block() as block:
            @block.sync
            def _(sp):
                sp.wait_ge(s_zero, 1)
                with sp.Fori(0, NX * SLOTS // (P * ZR)) as c:
                    sp.wait_ge(s_got[0], c * (16 * GT) + 16 * GT)
                    sp.dma_start(buf[at(c, P * ZR), :].rearrange("(p r) d -> p (r d)", p=P),
                                 zero[:, :]).then_inc(s_zeroed, 16)
                sp.wait_ge(s_zeroed, 16 * (NX * SLOTS // (P * ZR)))

            @block.gpsimd
            def _(pool):
                free = pool.alloc_register("free")
                have = pool.alloc_register("have")
                pool.reg_mov(free, 1)
                pool.reg_mov(have, 1)
                nc.gpsimd.memset(zero[:, :], 0.0).then_inc(s_zero, 1)
                with pool.Fori(0, NG // RG) as it:
                    for r in range(RG):
                        pool.wait_ge(s_free, free)
                        pool.reg_add(free, free, 1)
                        nc.gpsimd.tensor_copy(idx[:, r, :], src_all[:, at(it * RG + r, GT)]).then_inc(s_idx, 1)
                        pool.wait_ge(s_idx, have)
                        pool.reg_add(have, have, 1)
                        for t in range(GT):
                            pool.indirect_dma_start(
                                got[:, r, t, :], None, table,
                                bass.IndirectOffsetOnAxis(ap=idx[:, r, t:t + 1], axis=0)).then_inc(s_got[r], 16)

            @block.tensor
            def _(pe):
                turn = pe.alloc_register("turn")
                done = pe.alloc_register("done")
                pe.reg_mov(turn, 1)
                pe.reg_mov(done, 0)
                pe.sem_inc(s_free, RG)

                def mlp(q):
                    pe.wait_ge(s_hrow, q + 1)
                    for k in range(DK):
                        for t in range(QT):
                            ins = nc.tensor.transpose(turned[:, k, t * P:(t + 1) * P],
                                                      hrow[:, t, k * P:(k + 1) * P], ident[:, :])
                    ins.then_inc(s_turn, 1)
                    pe.wait_ge(s_hT, q + 1)
                    for c in range(H1C):
                        if c >= 2:
                            pe.wait_ge(s_mid, q * H1C + c - 1)
                        for k in range(DK):
                            ins = nc.tensor.matmul(up[:, c % 2, :], W1s[:, k, c * P:(c + 1) * P], hT[:, k, :],
                                                   start=(k == 0), stop=(k == DK - 1))
                        ins.then_inc(s_up, 1)
                    pe.wait_ge(s_mid, q * H1C + H1C)
                    for c in range(DK):
                        for k in range(H1C):
                            ins = nc.tensor.matmul(down[:, c, :], W2s[:, k, c * P:(c + 1) * P], mid[:, k, :],
                                                   start=(k == 0), stop=(k == H1C - 1))
                    ins.then_inc(s_down, 1)

                with pe.Fori(0, NG // RG) as it:
                    for r in range(RG):
                        word = pe.value_load(ctl[0:1, at(it * RG + r)], min_val=0, max_val=1 << 20)
                        first = pe.snap(word % 128)
                        end = pe.snap((word // 128) % 128)
                        whole = pe.snap(word // 16384)
                        pe.wait_ge(s_got[r], it * (16 * GT) + 16 * GT)
                        with pe.Fori(first, end):
                            half = pe.snap(turn) % 2
                            pe.wait_ge(s_hot, turn)
                            pe.wait_ge(s_add, turn)
                            pe.reg_add(turn, turn, 1)
                            for t in range(GT):
                                ins = nc.tensor.matmul(sums[:, half, :], hot[:, half, t, :], got[:, r, t, :],
                                                       start=(t == 0), stop=(t == GT - 1))
                            ins.then_inc(s_sum, 1)
                        pe.wait_ge(s_sum, turn)
                        pe.sem_inc(s_free, 1)
                        with pe.If(pe.snap(done) < whole):
                            with pe.Fori(done, whole) as quad_no:
                                mlp(nc.s_assert_within(quad_no, 0, NQ - 1, skip_runtime_bounds_check_because="stage_norm packs it"))
                        pe.reg_mov(done, whole)

            @block.scalar
            def _(act):
                def mlp(q):
                    act.wait_ge(s_turn, q + 1)
                    nc.scalar.activation(hT[:, :, :], turned[:, :, :], ACT.Identity).then_inc(s_hT, 1)
                    for c in range(H1C):
                        act.wait_ge(s_up, q * H1C + c + 1)
                        nc.scalar.activation(mid[:, c, :], up[:, c % 2, :], ACT.Relu,
                                             bias=b1s[:, c:c + 1]).then_inc(s_mid, 1)
                    act.wait_ge(s_down, q + 1)
                    for c in range(DK):
                        nc.scalar.activation(
                            nodes[:, at(q), c * QN:(c + 1) * QN].rearrange("p a b -> p (a b)"), down[:, c, :],
                            ACT.Identity, bias=b2s[:, c:c + 1]).then_inc(s_h2, 1)

                with act.Fori(0, NQ) as q:
                    mlp(q)

            @block.vector
            def _(dve):
                turn = dve.alloc_register("turn")
                done = dve.alloc_register("done")
                last = dve.alloc_register("last")
                flushed = dve.alloc_register("flushed")
                dve.reg_mov(turn, 1)
                dve.reg_mov(done, 0)
                dve.reg_mov(last, 0)
                dve.reg_mov(flushed, 1)
                nc.vector.memset(sums[:, :, :], 0.0).then_inc(s_sum, 1)
                dve.wait_ge(s_sum, 1)
                dve.sem_inc(s_add, 1)

                def add_sums(half, b, s_first, s_second, first_count):
                    row = blocks_of[:, b, :].rearrange("p a d -> p (a d)")
                    nc.vector.scalar_tensor_tensor(
                        out=part[:, :], in0=sums[:, half, D:2 * D], scalar=1.0 / LOW, in1=row,
                        op0=ALU.mult, op1=ALU.add).then_inc(s_first, 1)
                    dve.wait_ge(s_first, first_count)
                    return nc.vector.tensor_tensor(row, sums[:, half, 0:D], part[:, :], ALU.add).then_inc(s_second, 1)

                def block_no(register):
                    return at(nc.s_assert_within(dve.snap(register), 0, NB - 1,
                                                 skip_runtime_bounds_check_because="stage_norm packs it"))

                with dve.Fori(0, NG // RG) as it:
                    for r in range(RG):
                        word = dve.value_load(ctl[0:1, at(it * RG + r)], min_val=0, max_val=1 << 20)
                        first = dve.snap(word % 128)
                        end = dve.snap((word // 128) % 128)
                        whole = dve.snap(word // 16384)
                        with dve.Fori(first, end) as number:
                            half, other = dve.snap(dve.snap(turn) % 2), dve.snap((dve.snap(turn) + 1) % 2)
                            b, before = block_no(number), block_no(last)
                            nc.vector.tensor_scalar(rel[:, :], dst_all[:, at(it * RG + r, GT)], base[:, b],
                                                    None, ALU.subtract).then_inc(s_rel, 1)
                            dve.wait_ge(s_rel, turn)
                            nc.vector.tensor_tensor(
                                hot[:, half, :, :], iota[:, :].unsqueeze(1).broadcast_to((P, GT, P)),
                                rel[:, :].unsqueeze(2).broadcast_to((P, GT, P)), ALU.is_equal).then_inc(s_hot, 1)
                            dve.wait_ge(s_sum, turn)
                            add_sums(other, before, s_part, s_add, turn)
                            dve.reg_mov(last, number)
                            dve.reg_add(turn, turn, 1)
                        with dve.If(dve.snap(done) < whole):
                            half = dve.snap((dve.snap(turn) + 1) % 2)
                            before = block_no(last)
                            dve.wait_ge(s_sum, turn)
                            dve.wait_ge(s_add, turn)
                            add_sums(half, before, s_flush, s_flush, flushed)
                            dve.reg_add(flushed, flushed, 1)
                            dve.wait_ge(s_flush, flushed)
                            dve.reg_add(flushed, flushed, 1)
                            with dve.Fori(done, whole) as number:
                                q = nc.s_assert_within(number, 0, NQ - 1,
                                                       skip_runtime_bounds_check_because="stage_norm packs it")
                                nc.vector.tensor_scalar(hrow[:, :, :].rearrange("p t d -> p (t d)"),
                                                        nodes[:, at(q), :].rearrange("p a b -> p (a b)"),
                                                        1.0, None, ALU.mult).then_inc(s_hrow, 1)
                                dve.wait_ge(s_turn, q + 1)
                            nc.vector.memset(sums[:, :, :], 0.0)
                        dve.reg_mov(done, whole)
                with dve.Fori(0, NQ - 1) as q:
                    dve.wait_ge(s_h2, q * DK + DK)
                    for c in range(DK):
                        nc.vector.bn_stats(stats[:, c, at(q, 6)],
                                           nodes[:, at(q), c * QN:(c + 1) * QN].rearrange("p a b -> p (a b)"))
                dve.wait_ge(s_h2, NQ * DK)
                for c in range(DK):
                    nc.vector.bn_stats(stats[:, c, (NQ - 1) * 6:NQ * 6],
                                       nodes[:, NQ - 1, c * QN:c * QN + N - (NQ - 1) * QN])


def stage_route(nc, x, gate_w, gate_b, buf, out, ident, onesf, epsc, nodes, stats, gam, bet):
    with ExitStack() as ctx:
        def sb(name, shape, dt):
            return ctx.enter_context(nc.sbuf_tensor(name, shape, dt))

        def psum(name, shape, dt):
            return ctx.enter_context(nc.psum_tensor(name, shape, dt))

        def sem(name):
            return ctx.enter_context(nc.semaphore(name))

        bnv = sb("r_bnv", [P, DK, 2], F32)
        bns = sb("r_bns", [P, DK], F32)
        bnr = sb("r_bnr", [P, DK], F32)
        scale = sb("r_scale", [P, DK], F32)
        ms = sb("r_ms", [P, DK], F32)
        shift = sb("r_shift", [P, DK], F32)
        gw = sb("r_gw", [P, DK, NX], F32)
        gb = sb("r_gb", [P, NX], F32)
        tri = sb("r_tri", [P, P], F32)
        rev = sb("r_rev", [P, NX], F32)
        node1 = sb("r_node1", [P, NB], F32)
        xin = sb("r_xin", [P, R5, QT, D], F32)
        row = sb("r_row", [P, R5, QT, ROW], F32)
        hbn = sb("r_hbn", [P, DK, QN], F32)
        xn = sb("r_xn", [P, QT, D], F32)
        xT = sb("r_xT", [P, DK, QN], F32)
        st = sb("r_st", [P, R5, QT, 6], F32)
        mv = sb("r_mv", [P, R5, QT, 2], F32)
        sd = sb("r_sd", [P, R5, QT], F32)
        lg = sb("r_lg", [P, QT, NX], F32)
        mx = sb("r_mx", [P, QT], F32)
        cand = sb("r_cand", [P, QT, NX], F32)
        best = sb("r_best", [P, QT], F32)
        hot = sb("r_hot", [P, QT, NX], F32)
        seen = sb("r_seen", [P, QT + 1, NX], F32)
        mine = sb("r_mine", [P, QT, NX], F32)
        pos = sb("r_pos", [P, QT], F32)
        slot = sb("r_slot", [P, QT], F32)
        over = sb("r_over", [P, QT], F32)
        slot2 = sb("r_slot2", [P, QT], F32)
        pad = sb("r_pad", [P, QT], F32)
        slots = sb("r_slots", [P, R5, QT], I32)
        turned = psum("r_turned", [P, QT, D], F32)
        back = psum("r_back", [P, DK, QN], F32)
        logit = psum("r_logit", [P, QT, NX], F32)
        count = psum("r_count", [P, QT, NX], F32)

        s_gw, s_const, s_tri, s_rows, s_bn = sem("r_gw_s"), sem("r_const"), sem("r_tri_s"), sem("r_rows"), sem("r_bn")
        s_bnsd = sem("r_bnsd")
        s_x = [sem(f"r_x{j}") for j in range(R5)]
        s_out = [sem(f"r_out{j}") for j in range(R5)]
        s_scat = [sem(f"r_scat{j}") for j in range(R5)]
        s_hbn, s_turn, s_x2, s_var, s_std, s_rstd, s_xn, s_back, s_xT, s_logit = (
            sem("r_hbn_s"), sem("r_turn"), sem("r_x2_s"), sem("r_var"), sem("r_std"), sem("r_rstd"), sem("r_xn_s"),
            sem("r_back_s"), sem("r_xT_s"), sem("r_logit_s"))
        s_stat, s_hotv, s_hot, s_count, s_slotv, s_slot, s_node = (
            sem("r_stat"), sem("r_hotv"), sem("r_hot_s"), sem("r_count_s"), sem("r_slotv"), sem("r_slot_s"),
            sem("r_node_s"))

        with nc.Block() as block:
            @block.sync
            def _(sp):
                sp.dma_start(gw[:, :, :], gate_w.rearrange("(k p) e -> p k e", p=P)).then_inc(s_gw, 16)
                sp.dma_start(gb[:, :], gate_b.unsqueeze(0).broadcast_to((P, NX))).then_inc(s_gw, 16)

                def load(q, j, rnd):
                    if not (isinstance(rnd, int) and rnd == 0):
                        sp.wait_ge(s_x2, q - R5 + 1)
                    if isinstance(q, int) and q == NQ - 1:
                        sp.dma_start(xin[:, j, 0, :], x[q * QN:q * QN + P, :]).then_inc(s_x[j], 16)
                        sp.dma_start(xin[0:N - q * QN - P, j, 1, :], x[q * QN + P:N, :]).then_inc(s_x[j], 16)
                    else:
                        sp.dma_start(xin[:, j, :, :],
                                     x[at(q, QN), :].rearrange("(t p) d -> p t d", p=P)).then_inc(s_x[j], 16)

                def store(q, j, rnd):
                    sp.wait_ge(s_x2, q + 1)
                    if isinstance(q, int) and q == NQ - 1:
                        sp.dma_start(out[q * QN:q * QN + P, :], row[:, j, 0, 0:D]).then_inc(s_out[j], 16)
                        sp.dma_start(out[q * QN + P:N, :], row[0:N - q * QN - P, j, 1, 0:D]).then_inc(s_out[j], 16)
                    else:
                        sp.dma_start(out[at(q, QN), :].rearrange("(t p) d -> p t d", p=P),
                                     row[:, j, :, 0:D]).then_inc(s_out[j], 16)

                walk(sp, [(load, 0), (store, 3)], NQ, R5)
                for j in range(R5):
                    sp.wait_ge(s_out[j], 16 * (NQ // R5) + (16 if j == (NQ - 1) % R5 else 0))

            @block.gpsimd
            def _(pool):
                ready = counter(pool, "r_ready", R5 + 1)
                nc.gpsimd.memset(row[:, :, :, D + 3:D + 4], 0.0).then_inc(s_rows, 1)
                nc.gpsimd.memset(seen[:, :, :], 0.0).then_inc(s_const, 1)
                nc.gpsimd.iota(rev[:, :], pattern=[[-1, NX]], base=NX, channel_multiplier=0,
                               allow_small_or_imprecise_dtypes=True).then_inc(s_const, 1)
                nc.gpsimd.iota(node1[:, :], pattern=[[P, NB]], base=1, channel_multiplier=1,
                               allow_small_or_imprecise_dtypes=True).then_inc(s_const, 1)
                nc.gpsimd.affine_select(out=tri[:, :], in_=onesf[:, :], compare_op=ALU.is_ge, fill=0.0,
                                        base=0, pattern=[[1, P]], channel_multiplier=-1).then_inc(s_tri, 1)
                bound = pool.to_reg(NX * SLOTS - 1)

                def scatter(q, j, rnd):
                    wait_count(pool, s_slot, q + 1, ready)
                    for t in range(QT):
                        pool.indirect_dma_start(
                            buf, bass.IndirectOffsetOnAxis(ap=slots[:, j, t:t + 1], axis=0), row[:, j, t, :], None,
                            bounds_check=bound, oob_is_err=False).then_inc(s_scat[j], 16)

                pool.wait_ge(s_rows, 1)
                walk(pool, [(scatter, 0)], NQ, R5)
                for j in range(R5):
                    pool.wait_ge(s_scat[j], 16 * QT * (NQ // R5))

            @block.tensor
            def _(pe):
                def turn(q, j, rnd):
                    pe.wait_ge(s_hbn, q + 1)
                    if not (isinstance(q, int) and q == 0):
                        pe.wait_ge(s_x2, q)
                    for t in range(QT):
                        for k in range(DK):
                            ins = nc.tensor.transpose(turned[:, t, k * P:(k + 1) * P],
                                                      hbn[:, k, t * P:(t + 1) * P], ident[:, :])
                    ins.then_inc(s_turn, 1)

                def turn_back(q, j, rnd):
                    pe.wait_ge(s_xn, q + 1)
                    if not (isinstance(q, int) and q == 0):
                        pe.wait_ge(s_xT, q)
                    for k in range(DK):
                        for t in range(QT):
                            ins = nc.tensor.transpose(back[:, k, t * P:(t + 1) * P],
                                                      xn[:, t, k * P:(k + 1) * P], ident[:, :])
                    ins.then_inc(s_back, 1)

                def gate(q, j, rnd):
                    pe.wait_ge(s_xT, q + 1)
                    if not (isinstance(q, int) and q == 0):
                        pe.wait_ge(s_hot, q)
                    for t in range(QT):
                        for k in range(DK):
                            ins = nc.tensor.matmul(logit[:, t, :], xT[:, k, t * P:(t + 1) * P], gw[:, k, :],
                                                   start=(k == 0), stop=(k == DK - 1))
                    ins.then_inc(s_logit, 1)

                def counts(q, j, rnd):
                    pe.wait_ge(s_hot, q + 1)
                    if not (isinstance(q, int) and q == 0):
                        pe.wait_ge(s_slot, q)
                    nc.tensor.matmul(count[:, :, :], tri[:, :], hot[:, :, :], start=True, stop=False)
                    nc.tensor.matmul(count[:, :, :], onesf[:, :], seen[:, 0:QT, :],
                                     start=False, stop=True).then_inc(s_count, 1)

                pe.wait_ge(s_gw, 32)
                pe.wait_ge(s_tri, 1)
                walk(pe, [(counts, 4), (turn, 1), (gate, 3), (turn_back, 2)], NQ, R5)

            @block.scalar
            def _(act):
                act.wait_ge(s_bn, 1)
                nc.scalar.activation(bns[:, :], bnv[:, :, 1], ACT.Sqrt, bias=epsc[:, 0:1]).then_inc(s_bnsd, 1)
                act.wait_ge(s_bn, 2)

                def norm(q, j, rnd):
                    if not (isinstance(q, int) and q == 0):
                        act.wait_ge(s_turn, q)
                    for k in range(DK):
                        ins = nc.scalar.activation(
                            hbn[:, k, :], nodes[:, at(q), k * QN:(k + 1) * QN].rearrange("p a b -> p (a b)"),
                            ACT.Identity, bias=shift[:, k:k + 1], scale=scale[:, k:k + 1])
                    ins.then_inc(s_hbn, 1)

                def rows(q, j, rnd):
                    act.wait_ge(s_rstd, q * 2 + 2)
                    if not (isinstance(q, int) and q == 0):
                        act.wait_ge(s_back, q)
                    for t in range(QT):
                        ins = nc.scalar.activation(xn[:, t, :], row[:, j, t, 0:D], ACT.Identity,
                                                   bias=row[:, j, t, D + 1:D + 2], scale=row[:, j, t, D:D + 1])
                    ins.then_inc(s_xn, 1)

                def std(q, j, rnd):
                    act.wait_ge(s_var, q + 1)
                    nc.scalar.activation(sd[:, j, :], mv[:, j, :, 1], ACT.Sqrt, bias=epsc[:, 0:1]).then_inc(s_std, 1)

                def columns(q, j, rnd):
                    act.wait_ge(s_back, q + 1)
                    if not (isinstance(q, int) and q == 0):
                        act.wait_ge(s_logit, q)
                    nc.scalar.activation(xT[:, :, :], back[:, :, :], ACT.Identity).then_inc(s_xT, 1)

                walk(act, [(columns, 3), (rows, 2), (norm, 0), (std, 1)], NQ, R5)

            @block.vector
            def _(dve):
                for k in range(DK):
                    ins = nc.vector.bn_aggr(bnv[:, k, :], stats[:, k, :])
                ins.then_inc(s_bn, 1)
                dve.wait_ge(s_bnsd, 1)
                nc.vector.reciprocal(bnr[:, :], bns[:, :]).then_inc(s_node, 1)
                dve.wait_ge(s_node, 1)
                nc.vector.tensor_tensor(scale[:, :], bnr[:, :], gam[:, :], ALU.mult).then_inc(s_node, 1)
                dve.wait_ge(s_node, 2)
                nc.vector.tensor_tensor(ms[:, :], bnv[:, :, 0], scale[:, :], ALU.mult).then_inc(s_node, 1)
                dve.wait_ge(s_node, 3)
                nc.vector.tensor_tensor(shift[:, :], bet[:, :], ms[:, :], ALU.subtract).then_inc(s_bn, 1)
                dve.wait_ge(s_gw, 32)
                dve.wait_ge(s_const, 3)
                dve.wait_ge(s_rows, 1)

                stat_seen = counter(dve, "r_stat_seen", R5)

                def add(q, j, rnd):
                    dve.wait_ge(s_turn, q + 1)
                    if isinstance(q, int) and q == NQ - 1:
                        dve.wait_ge(s_x[j], 16 * rnd + 32)
                    else:
                        dve.wait_ge(s_x[j], rnd * 16 + 16)
                    if not (isinstance(rnd, int) and rnd == 0):
                        dve.wait_ge(s_out[j], rnd * 16)
                        dve.wait_ge(s_scat[j], rnd * (16 * QT))
                    nc.vector.tensor_tensor(row[:, j, :, 0:D], turned[:, :, :], xin[:, j, :, :],
                                            ALU.add).then_inc(s_x2, 1)
                    dve.wait_ge(s_x2, q + 1)
                    for t in range(QT):
                        ins = nc.vector.bn_stats(st[:, j, t, :], row[:, j, t, 0:D])
                    ins.then_inc(s_stat, 1)
                    wait_count(dve, s_stat, q + 1, stat_seen)
                    for t in range(QT):
                        ins = nc.vector.bn_aggr(mv[:, j, t, :], st[:, j, t, :])
                    ins.then_inc(s_var, 1)

                def norm(q, j, rnd):
                    dve.wait_ge(s_std, q + 1)
                    nc.vector.reciprocal(row[:, j, :, D], sd[:, j, :]).then_inc(s_rstd, 1)
                    dve.wait_ge(s_rstd, q * 2 + 1)
                    nc.vector.scalar_tensor_tensor(out=row[:, j, :, D + 1], in0=mv[:, j, :, 0], scalar=-1.0,
                                                   in1=row[:, j, :, D], op0=ALU.mult, op1=ALU.mult
                                                   ).then_inc(s_rstd, 1)

                def pick(q, j, rnd):
                    CH = 10

                    def then(k, ins):
                        ins.then_inc(s_hotv, 1)
                        dve.wait_ge(s_hotv, q * CH + k)

                    dve.wait_ge(s_logit, q + 1)
                    if not (isinstance(q, int) and q == 0):
                        dve.wait_ge(s_count, q)
                    then(1, nc.vector.tensor_tensor(lg[:, :, :], logit[:, :, :],
                                                    gb[:, :].unsqueeze(1).broadcast_to((P, QT, NX)), ALU.add))
                    then(2, nc.vector.tensor_reduce(mx[:, :], lg[:, :, :], AX.X, ALU.max))
                    then(3, nc.vector.tensor_tensor(row[:, j, :, D + 4:ROW], lg[:, :, :],
                                                    mx[:, :].unsqueeze(2).broadcast_to((P, QT, NX)), ALU.subtract))
                    then(4, nc.vector.scalar_tensor_tensor(
                        out=cand[:, :, :], in0=row[:, j, :, D + 4:ROW], scalar=0.0,
                        in1=rev[:, :].unsqueeze(1).broadcast_to((P, QT, NX)), op0=ALU.is_ge, op1=ALU.mult))
                    then(5, nc.vector.tensor_reduce(best[:, :], cand[:, :, :], AX.X, ALU.max))
                    nc.vector.tensor_tensor(hot[:, :, :], rev[:, :].unsqueeze(1).broadcast_to((P, QT, NX)),
                                            best[:, :].unsqueeze(2).broadcast_to((P, QT, NX)),
                                            ALU.is_equal).then_inc(s_hotv, 1)
                    then(7, nc.vector.tensor_copy(seen[:, 0, :], seen[:, QT, :]))
                    for t in range(QT - 1):
                        then(8 + t, nc.vector.tensor_tensor(seen[:, t + 1, :], seen[:, t, :], hot[:, t, :], ALU.add))
                    nc.vector.tensor_tensor(seen[:, QT, :], seen[:, QT - 1, :], hot[:, QT - 1, :],
                                            ALU.add).then_inc(s_hot, 1)

                def place(q, j, rnd):
                    CH = 7

                    def then(k, ins):
                        ins.then_inc(s_slotv, 1)
                        dve.wait_ge(s_slotv, q * CH + k)

                    dve.wait_ge(s_count, q + 1)
                    dve.wait_ge(s_hot, q + 1)
                    then(1, nc.vector.tensor_tensor(mine[:, :, :], count[:, :, :], hot[:, :, :], ALU.mult))
                    then(2, nc.vector.tensor_reduce(pos[:, :], mine[:, :, :], AX.X, ALU.add))
                    then(3, nc.vector.scalar_tensor_tensor(out=slot[:, :], in0=best[:, :], scalar=-float(SLOTS),
                                                           in1=pos[:, :], op0=ALU.mult, op1=ALU.add))
                    nc.vector.tensor_scalar(over[:, :], pos[:, :], float(CAP), SKIP, ALU.is_gt,
                                            ALU.mult).then_inc(s_slotv, 1)
                    then(5, nc.vector.tensor_scalar(pad[:, :], node1[:, at(q, QT)], float(N), SKIP, ALU.is_gt,
                                                    ALU.mult))
                    nc.vector.tensor_scalar(row[:, j, :, D + 2], node1[:, at(q, QT)], 1.0, None,
                                            ALU.mult).then_inc(s_slotv, 1)
                    then(7, nc.vector.scalar_tensor_tensor(out=slot2[:, :], in0=slot[:, :],
                                                           scalar=float(NX * SLOTS - 1), in1=over[:, :],
                                                           op0=ALU.add, op1=ALU.add))
                    nc.vector.tensor_tensor(slots[:, j, :], slot2[:, :], pad[:, :], ALU.add).then_inc(s_slot, 1)

                walk(dve, [(place, 4), (add, 1), (pick, 3), (norm, 1)], NQ, R5)


def stage_experts(nc, buf, w1, xb1, w2, xb2, out, ident):
    with ExitStack() as ctx:
        def sb(name, shape, dt):
            return ctx.enter_context(nc.sbuf_tensor(name, shape, dt))

        def psum(name, shape, dt):
            return ctx.enter_context(nc.psum_tensor(name, shape, dt))

        def sem(name):
            return ctx.enter_context(nc.semaphore(name))

        NS = NX * SG
        R8 = 2 * SG
        RR = 4
        w1s = sb("x_w1s", [P, 2, DK, F], F32)
        w2s = sb("x_w2s", [P, 2, FC, D], F32)
        b1s = sb("x_b1s", [P, 2, FC], F32)
        b2s = sb("x_b2s", [P, 2, D], F32)
        row = sb("x_row", [P, RR, QT, ROW], F32)
        xn = sb("x_xn", [P, QT, D], F32)
        xT = sb("x_xT", [P, 2, DK, QN], F32)
        mid = sb("x_mid", [P, FC, QN], F32)
        ex = sb("x_ex", [P, QT, NX], F32)
        tot = sb("x_tot", [P, QT], F32)
        prob = sb("x_prob", [P, RR, QT], F32)
        gone = sb("x_gone", [P, QT], F32)
        node = sb("x_node", [P, RR, QT], F32)
        nodei = sb("x_nodei", [P, RR, QT], I32)
        yb = sb("x_yb", [P, QT, D], F32)
        y = sb("x_y", [P, QT, D], F32)
        up1 = sb("x_up1", [P, QT, D], F32)
        dn1 = sb("x_dn1", [P, QT, D], F32)
        fine = sb("x_fine", [P, QT, D], I32)
        res = sb("x_res", [P, RR, QT, D], F32)
        turned = psum("x_turned", [P, DK, QN], F32)
        up = psum("x_up", [P, 2, QN], F32)
        down = psum("x_down", [P, QT, D], F32)

        s_row = [sem(f"x_row{j}") for j in range(RR)]
        s_scat = [sem(f"x_scat{j}") for j in range(RR)]
        s_w = [sem(f"x_w{j}") for j in range(2)]
        s_xn, s_turn, s_xT, s_up, s_mid, s_down, s_exp, s_meta, s_yv, s_res = (
            sem("x_xn_s"), sem("x_turn"), sem("x_xT_s"), sem("x_up_s"), sem("x_mid_s"), sem("x_down_s"),
            sem("x_exp"), sem("x_meta"), sem("x_yv"), sem("x_res_s"))

        with nc.Block() as block:
            @block.sync
            def _(sp):
                def weights(s, j, rnd):
                    if j % SG:
                        return
                    e = s // SG if isinstance(s, int) else rnd * 2 + j // SG
                    h = (j // SG + 1) % 2
                    if isinstance(s, int) and e + 1 >= NX:
                        return
                    if isinstance(s, int) and e == 0:
                        fetch(0, 0)
                    if not (isinstance(s, int) and e == 0):
                        sp.wait_ge(s_down, s * 1)
                        sp.wait_ge(s_res, s * 1)
                    fetch(e + 1, h)

                def fetch(e, h):
                    sp.dma_start(w1s[:, h, :, :],
                                 w1[at(e), :, :].rearrange("a (k p) f -> p (a k) f", p=P)).then_inc(s_w[h], 16)
                    sp.dma_start(w2s[:, h, :, :],
                                 w2[at(e), :, :].rearrange("a (k p) d -> p (a k) d", p=P)).then_inc(s_w[h], 16)
                    with nc.allow_non_contiguous_dma(reason="small vector"):
                        sp.dma_start(b1s[:, h, :], xb1[at(e), :].rearrange("a (c p) -> p (a c)", p=P)).then_inc(s_w[h], 16)
                    sp.dma_start(b2s[:, h, :], xb2[at(e), :].broadcast_to((P, D))).then_inc(s_w[h], 16)

                def load(s, j, rnd):
                    if not (isinstance(s, int) and s < RR):
                        sp.wait_ge(s_res, s - RR + 1)
                    sp.dma_start(row[:, j % RR, :, :],
                                 buf[at(s, QN), :].rearrange("(t p) d -> p t d", p=P)).then_inc(s_row[j % RR], 16)

                walk(sp, [(load, 0), (weights, SG - 1)], NS, R8)

            @block.gpsimd
            def _(pool):
                ready = counter(pool, "x_ready", R8 + 1)
                bound = pool.to_reg(N - 1)

                def scatter(s, j, rnd):
                    wait_count(pool, s_res, s + 1, ready)
                    for t in range(QT):
                        pool.indirect_dma_start(
                            out, bass.IndirectOffsetOnAxis(ap=nodei[:, j % RR, t:t + 1], axis=0),
                            res[:, j % RR, t, :], None, bounds_check=bound,
                            oob_is_err=False).then_inc(s_scat[j % RR], 16)

                walk(pool, [(scatter, 0)], NS, R8)
                for j in range(RR):
                    pool.wait_ge(s_scat[j], 16 * QT * (NS // RR))

            @block.tensor
            def _(pe):
                def turn(s, j, rnd):
                    pe.wait_ge(s_xn, s + 1)
                    if not (isinstance(s, int) and s == 0):
                        pe.wait_ge(s_xT, s)
                    for k in range(DK):
                        for t in range(QT):
                            ins = nc.tensor.transpose(turned[:, k, t * P:(t + 1) * P],
                                                      xn[:, t, k * P:(k + 1) * P], ident[:, :])
                    ins.then_inc(s_turn, 1)

                def products(s, j, rnd):
                    h = j // SG
                    if j % SG == 0:
                        pe.wait_ge(s_w[h], rnd * 64 + 64)
                    pe.wait_ge(s_xT, s + 1)
                    for c in range(FC):
                        if not (isinstance(s, int) and s == 0 and c < 2):
                            pe.wait_ge(s_mid, s * FC + c - 1)
                        for k in range(DK):
                            ins = nc.tensor.matmul(up[:, c % 2, :], w1s[:, h, k, c * P:(c + 1) * P],
                                                   xT[:, j % 2, k, :], start=(k == 0), stop=(k == DK - 1))
                        ins.then_inc(s_up, 1)
                    pe.wait_ge(s_mid, s * FC + FC)
                    if not (isinstance(s, int) and s == 0):
                        pe.wait_ge(s_yv, s * 7 - 6)
                    for t in range(QT):
                        for k in range(FC):
                            ins = nc.tensor.matmul(down[:, t, :], mid[:, k, t * P:(t + 1) * P], w2s[:, h, k, :],
                                                   start=(k == 0), stop=(k == FC - 1))
                    ins.then_inc(s_down, 1)

                walk(pe, [(turn, 0), (products, 1)], NS, R8)

            @block.scalar
            def _(act):
                def columns(s, j, rnd):
                    act.wait_ge(s_turn, s + 1)
                    if not (isinstance(s, int) and s < 2):
                        act.wait_ge(s_down, s - 1)
                    nc.scalar.activation(xT[:, j % 2, :, :], turned[:, :, :], ACT.Identity).then_inc(s_xT, 1)

                def expo(s, j, rnd):
                    act.wait_ge(s_row[j % RR], (s // RR) * 16 + 16 if isinstance(s, int)
                                else (rnd * (R8 // RR) + j // RR) * 16 + 16)
                    if not (isinstance(s, int) and s == 0):
                        act.wait_ge(s_meta, s * 3)
                    nc.scalar.activation(ex[:, :, :], row[:, j % RR, :, D + 4:ROW], ACT.Exp).then_inc(s_exp, 1)

                def hidden(s, j, rnd):
                    h = j // SG
                    if not (isinstance(s, int) and s == 0):
                        act.wait_ge(s_down, s)
                    if j % SG == 0:
                        act.wait_ge(s_w[h], rnd * 64 + 64)
                    for c in range(FC):
                        act.wait_ge(s_up, s * FC + c + 1)
                        nc.scalar.activation(mid[:, c, :], up[:, c % 2, :], ACT.Relu,
                                             bias=b1s[:, h, c:c + 1]).then_inc(s_mid, 1)

                walk(act, [(expo, 0), (columns, 0), (hidden, 1)], NS, R8)

            @block.vector
            def _(dve):
                def norm(s, j, rnd):
                    dve.wait_ge(s_row[j % RR], (s // RR) * 16 + 16 if isinstance(s, int)
                                else (rnd * (R8 // RR) + j // RR) * 16 + 16)
                    if not (isinstance(s, int) and s == 0):
                        dve.wait_ge(s_turn, s)
                    for t in range(QT):
                        ins = nc.vector.tensor_scalar(xn[:, t, :], row[:, j % RR, t, 0:D], row[:, j % RR, t, D:D + 1],
                                                      row[:, j % RR, t, D + 1:D + 2], ALU.mult, ALU.add)
                    ins.then_inc(s_xn, 1)

                def meta(s, j, rnd):
                    dve.wait_ge(s_exp, s + 1)
                    if not (isinstance(s, int) and s < RR):
                        dve.wait_ge(s_scat[j % RR], (s // RR) * (16 * QT) if isinstance(s, int)
                                    else (rnd * (R8 // RR) + j // RR) * (16 * QT))
                    nc.vector.tensor_reduce(tot[:, :], ex[:, :, :], AX.X, ALU.add).then_inc(s_meta, 1)
                    nc.vector.tensor_scalar(gone[:, :], row[:, j % RR, :, D + 2], 0.5, SKIP, ALU.is_lt,
                                            ALU.mult).then_inc(s_meta, 1)
                    dve.wait_ge(s_meta, s * 3 + 2)
                    nc.vector.reciprocal(prob[:, j % RR, :], tot[:, :])
                    nc.vector.scalar_tensor_tensor(out=nodei[:, j % RR, :], in0=row[:, j % RR, :, D + 2], scalar=-1.0,
                                                   in1=gone[:, :], op0=ALU.add, op1=ALU.add).then_inc(s_meta, 1)

                guard_seen = counter(dve, "x_guard_seen", (R8 - 2) * 7 + 6)

                def finish(s, j, rnd):
                    r = j % RR

                    def then(k, ins):
                        ins.then_inc(s_yv, 1)
                        dve.wait_ge(s_yv, s * 7 + k)

                    dve.wait_ge(s_down, s + 1)
                    dve.wait_ge(s_w[j // SG], rnd * 64 + 64)
                    then(1, nc.vector.tensor_tensor(
                        yb[:, :, :], down[:, :, :],
                        b2s[:, j // SG, :].unsqueeze(1).broadcast_to((P, QT, D)), ALU.add))
                    then(2, nc.vector.tensor_tensor(y[:, :, :], yb[:, :, :],
                                                    prob[:, r, :].unsqueeze(2).broadcast_to((P, QT, D)), ALU.mult))
                    nc.vector.tensor_scalar(up1[:, :, :], y[:, :, :], 0.0, 1e4, ALU.is_gt, ALU.mult).then_inc(s_yv, 1)
                    nc.vector.tensor_scalar(dn1[:, :, :], y[:, :, :], 0.0, -1e4, ALU.is_lt, ALU.mult).then_inc(s_yv, 1)
                    then(5, nc.vector.tensor_scalar(fine[:, :, :], y[:, :, :], 0.0, 0.0, ALU.mult, ALU.is_equal))
                    nc.vector.tensor_tensor(up1[:, :, :], up1[:, :, :], dn1[:, :, :], ALU.add).then_inc(s_yv, 1)
                    wait_count(dve, s_yv, s * 7 + 6, guard_seen, 7)
                    then(7, nc.vector.copy_predicated(up1[:, :, :], fine[:, :, :], y[:, :, :]))
                    nc.vector.tensor_tensor(res[:, r, :, :], up1[:, :, :], row[:, r, :, 0:D], ALU.add).then_inc(s_res, 1)

                walk(dve, [(norm, 0), (meta, 0), (finish, 2)], NS, R8)


def kernel(x, src, dst, L0_gnn_eps, L0_gnn_W1, L0_gnn_b1, L0_gnn_W2, L0_gnn_b2, L0_gnn_gamma, L0_gnn_beta,
           L0_ffn_gate_w, L0_ffn_gate_b, L0_ffn_w1, L0_ffn_b1, L0_ffn_w2, L0_ffn_b2):
    import concourse.bacc as bacc
    from concourse.bass_utils import run_bass_kernel_spmd

    def edge_tiles(a):
        a = np.asarray(a)
        return np.ascontiguousarray(a[:EFULL * P].reshape(EFULL, P).T), np.ascontiguousarray(a[EFULL * P:, None])

    src_full, src_tail = edge_tiles(src)
    dst_full, dst_tail = edge_tiles(dst)
    arrays = {
        "x": x, "src": src_full, "dst": dst_full, "src_tail": src_tail, "dst_tail": dst_tail, "eps": L0_gnn_eps,
        "W1": L0_gnn_W1, "b1": L0_gnn_b1, "W2": L0_gnn_W2, "b2": L0_gnn_b2, "gamma": L0_gnn_gamma,
        "beta": L0_gnn_beta, "gate_w": L0_ffn_gate_w, "gate_b": L0_ffn_gate_b, "w1": L0_ffn_w1, "xb1": L0_ffn_b1,
        "w2": L0_ffn_w2, "xb2": L0_ffn_b2,
    }
    nc = bacc.Bacc("TRN2", target_bir_lowering=False, num_devices=1)
    ins, aps = {}, {}
    for name, a in arrays.items():
        a = np.ascontiguousarray(a)
        ins[f"in_{name}"] = a
        aps[name] = nc.dram_tensor(f"in_{name}", a.shape, mybir.dt.from_np(a.dtype), kind="ExternalInput").ap()
    out = nc.dram_tensor("out", (N, D), F32, kind="ExternalOutput").ap()
    kernel_program(nc, out=out, **aps)
    return run_bass_kernel_spmd(nc, [ins], core_ids=[0]).results[0]["out"]
```

```python
from contextlib import ExitStack

import numpy as np

import concourse.bass as bass
from concourse import mybir

ALU = mybir.AluOpType
ACT = mybir.ActivationFunctionType
AX = mybir.AxisListType
RMAX = bass.bass_isa.ReduceOp.max
F32 = mybir.dt.float32
F16 = mybir.dt.float16
I32 = mybir.dt.int32
U32 = mybir.dt.uint32
U8 = mybir.dt.uint8

P = 128
N = 12500
D = 256
NE = 200000
NX = 8
F = 1024
CAP = -(-5 * N // (4 * NX))
DK = D // P
H1 = 2 * D
H1C = H1 // P
FC = F // P
QT = 4
QN = QT * P
NQ = -(-N // QN)
NB = NQ * QT
ET = -(-NE // P)
EFULL = NE // P
ETAIL = NE - EFULL * P
GT = 8
RG = 4
NG = -(-ET // (GT * RG)) * RG
EP = NG * GT
PAD_DST = NB * P - QN + 255
SLOTS = QN * -(-CAP // QN)
SG = SLOTS // QN
ROW = D + 12
R5 = 5
X_SCALE, W_SCALE, MID_SCALE = 2.0 ** 10, 2.0 ** 8, 2.0 ** 4
EPS = 1e-5
BIG = 3.4028234663852886e38
SKIP = float(1 << 24)

assert NQ % R5 == 0 and NG % RG == 0 and D == 2 * P and PAD_DST >= N


def walk(engine, stages, count, ring):
    def step(s):
        for stage, lag in stages:
            if 0 <= s - lag < count:
                stage(s - lag, (s - lag) % ring, (s - lag) // ring)

    for s in range(ring):
        step(s)
    with engine.Fori(1, count // ring - 1) as it:
        for j in range(ring):
            for stage, lag in stages:
                stage(it * ring + j - lag, (j - lag) % ring, it if j >= lag else it - 1)
    for s in range(count - ring, count + max(lag for _, lag in stages)):
        step(s)


def wait_count(engine, sem, value, register, step=1):
    if isinstance(value, int):
        engine.wait_ge(sem, value)
    else:
        engine.wait_ge(sem, register)
        engine.reg_add(register, register, step)


def counter(engine, name, start):
    register = engine.alloc_register(name)
    engine.reg_mov(register, start)
    return register


def at(q, n=1):
    return bass.ds(q * n, n)


def kernel_program(nc, x, src, dst, src_tail, dst_tail, eps, W1, b1, W2, b2, gamma, beta, gate_w, gate_b,
                   w1, xb1, w2, xb2, out):
    table = nc.dram_tensor("table", (NB * P, 2 * D), F16, kind="Internal").ap()
    buf = nc.dram_tensor("slot_rows", (NX * SLOTS, ROW), F32, kind="Internal").ap()
    with ExitStack() as whole:
        def keep(name, shape, dt):
            return whole.enter_context(nc.sbuf_tensor(name, shape, dt))

        ident = keep("ident", [P, P], F32)
        onesf = keep("onesf", [P, P], F32)
        epsc = keep("epsc", [P, 1], F32)

        with ExitStack() as gnn:
            def hold(name, shape, dt):
                return gnn.enter_context(nc.sbuf_tensor(name, shape, dt))

            nodes = hold("nodes", [P, NQ, QT * D], F32)
            src_all = hold("src_all", [P, EP], I32)
            dst_all = hold("dst_all", [P, EP], F32)
            ctl = hold("ctl", [P, NG + 1], I32)
            base = hold("base", [P, NB], F32)
            iota = hold("iota", [P, P], F16)
            stats = hold("stats", [P, DK, NQ * 6], F32)
            W1s = hold("W1s", [P, DK, H1], F32)
            W2s = hold("W2s", [P, H1C, D], F32)
            b1s = hold("b1s", [P, H1C], F32)
            b2s = hold("b2s", [P, DK], F32)
            gam = hold("gam", [P, DK], F32)
            bet = hold("bet", [P, DK], F32)
            stage_norm(nc, x, src, dst, src_tail, dst_tail, eps, W1, b1, W2, b2, gamma, beta, table,
                       ident, onesf, epsc, nodes, src_all, dst_all, ctl, base, iota, W1s, W2s, b1s, b2s, gam, bet)
            stage_edges(nc, table, buf, ident, nodes, src_all, dst_all, ctl, base, iota, stats, W1s, W2s, b1s, b2s)
            stage_route(nc, x, gate_w, gate_b, buf, out, ident, onesf, epsc, nodes, stats, gam, bet)
        stage_experts(nc, buf, w1, xb1, w2, xb2, out, ident)


def stage_norm(nc, x, src, dst, src_tail, dst_tail, eps, W1, b1, W2, b2, gamma, beta, table,
               ident, onesf, epsc, nodes, src_all, dst_all, ctl, base, iota, W1s, W2s, b1s, b2s, gam, bet):
    with ExitStack() as ctx:
        def sb(name, shape, dt):
            return ctx.enter_context(nc.sbuf_tensor(name, shape, dt))

        def sem(name):
            return ctx.enter_context(nc.semaphore(name))

        xin = sb("n_xin", [P, R5, QT, D], F32)
        pair = sb("n_pair", [P, R5, QT, 2 * D], F16)
        st = sb("n_st", [P, R5, QT, 6], F32)
        mv = sb("n_mv", [P, R5, QT, 2], F32)
        sd = sb("n_sd", [P, R5, QT], F32)
        off = sb("n_off", [P, R5, QT], F32)
        epsl = sb("n_epsl", [P, 1], F32)
        rsl = sb("n_rsl", [P, R5, QT], F32)
        selfs = sb("n_selfs", [P, 1], F32)
        epsb = sb("n_epsb", [P, 1], F32)
        dsti = sb("n_dsti", [P, EP], I32)
        ext = sb("n_ext", [P, 2, NG], F32)
        low_of = sb("n_low_of", [P, NG], F32)
        allx = sb("n_allx", [P, 2, NG], F32)
        blki = sb("n_blki", [P, 2, NG], I32)
        blks = sb("n_blks", [P, 2, NG], I32)
        sfx = sb("n_sfx", [P, 2, NG + 128], F32)
        sfi = sb("n_sfi", [P, NG], I32)
        sfs = sb("n_sfs", [P, NG], I32)
        packed = sb("n_packed", [P, 2, NG], F32)

        s_x = [sem(f"n_x{j}") for j in range(R5)]
        s_tab = [sem(f"n_tab{j}") for j in range(R5)]
        s_pad, s_src, s_dst, s_w, s_eps = sem("n_pad"), sem("n_src"), sem("n_dst"), sem("n_w"), sem("n_eps_in")
        s_self, s_epsc, s_const, s_id = sem("n_self"), sem("n_epsc"), sem("n_const"), sem("n_id")
        s_stat, s_var, s_std, s_rst, s_xn = sem("n_stat"), sem("n_var"), sem("n_std"), sem("n_rst"), sem("n_xn")
        s_hi, s_term, s_lo = sem("n_hi"), sem("n_term"), sem("n_lo")
        s_ext, s_all, s_rng = sem("n_ext_s"), sem("n_all"), sem("n_rng")

        with nc.Block() as block:
            @block.sync
            def _(sp):
                def load(q, j, rnd):
                    if not (isinstance(rnd, int) and rnd == 0):
                        sp.wait_ge(s_lo, q - R5 + 1)
                        sp.wait_ge(s_term, q - R5 + 1)
                    if isinstance(q, int) and q == NQ - 1:
                        sp.dma_start(xin[:, j, 0, :], x[q * QN:q * QN + P, :]).then_inc(s_x[j], 16)
                        sp.dma_start(xin[0:N - q * QN - P, j, 1, :], x[q * QN + P:N, :]).then_inc(s_x[j], 16)
                    else:
                        sp.dma_start(xin[:, j, :, :],
                                     x[at(q, QN), :].rearrange("(t p) d -> p t d", p=P)).then_inc(s_x[j], 16)

                def store(q, j, rnd):
                    sp.wait_ge(s_lo, q + 1)
                    sp.dma_start(table[at(q, QN), :].rearrange("(t p) d -> p t d", p=P),
                                 pair[:, j, :, :]).then_inc(s_tab[j], 16)

                sp.dma_start(epsb[:, :], eps.unsqueeze(0).broadcast_to((P, 1))).then_inc(s_eps, 16)
                for q in range(2):
                    load(q, q, 0)
                sp.wait_ge(s_pad, 2)
                sp.dma_start(dsti[:, 0:EFULL], dst).then_inc(s_dst, 16)
                sp.dma_start(dsti[0:ETAIL, EFULL:EFULL + 1], dst_tail).then_inc(s_dst, 16)
                for q in range(2, R5):
                    load(q, q, 0)
                sp.dma_start(src_all[:, 0:EFULL], src).then_inc(s_src, 16)
                sp.dma_start(src_all[0:ETAIL, EFULL:EFULL + 1], src_tail).then_inc(s_src, 16)
                with sp.Fori(1, NQ // R5 - 1) as it:
                    for j in range(R5):
                        store(it * R5 + j - R5, j, it - 1)
                        load(it * R5 + j, j, it)
                for q in range(NQ - R5, NQ):
                    store(q - R5, q % R5, q // R5 - 1)
                    load(q, q % R5, q // R5)
                for q in range(NQ - R5, NQ):
                    store(q, q % R5, q // R5)
                for j in range(R5):
                    sp.wait_ge(s_tab[j], 16 * (NQ // R5))
                sp.wait_ge(s_src, 32)

            @block.gpsimd
            def _(pool):
                nc.gpsimd.memset(src_all[:, EFULL:EP], 0).then_inc(s_pad, 1)
                nc.gpsimd.memset(ctl[:, NG:NG + 1], 0)
                nc.gpsimd.memset(dsti[:, EFULL:EP], PAD_DST).then_inc(s_pad, 1)
                nc.gpsimd.memset(epsl[:, :], EPS / X_SCALE**2).then_inc(s_epsc, 1)
                nc.gpsimd.memset(epsc[:, :], EPS).then_inc(s_const, 1)
                nc.gpsimd.memset(ident[:, :], 0.0).then_inc(s_id, 1)
                nc.gpsimd.memset(onesf[:, :], 1.0).then_inc(s_const, 1)
                nc.gpsimd.iota(base[:, :], pattern=[[P, NB]], base=0, channel_multiplier=0,
                               allow_small_or_imprecise_dtypes=True).then_inc(s_const, 1)
                nc.gpsimd.iota(iota[:, :], pattern=[[1, P]], base=0, channel_multiplier=0,
                               allow_small_or_imprecise_dtypes=True).then_inc(s_const, 1)
                pool.wait_ge(s_id, 1)
                nc.gpsimd.affine_select(out=ident[:, :], in_=ident[:, :], compare_op=ALU.not_equal, fill=1.0,
                                        base=0, pattern=[[-1, P]], channel_multiplier=1).then_inc(s_id, 1)

                def term(q, j, rnd):
                    wait_count(pool, s_xn, q + 1, normed)
                    nc.gpsimd.tensor_tensor(nodes[:, at(q), :].rearrange("p a b -> p (a b)"),
                                            xin[:, j, :, :].rearrange("p t d -> p (t d)"),
                                            selfs[:, 0:1].broadcast_to((P, QT * D)), ALU.mult).then_inc(s_term, 1)

                def extremes(q, j, rnd):
                    if isinstance(q, int) and q == R5 - 1:
                        pool.wait_ge(s_ext, 3)
                        nc.gpsimd.partition_all_reduce(allx[:, :, :].rearrange("p a g -> p (a g)"),
                                                       ext[:, :, :].rearrange("p a g -> p (a g)"), P,
                                                       RMAX).then_inc(s_all, 1)

                normed = counter(pool, "n_normed", R5 + 1)
                pool.wait_ge(s_self, 1)
                walk(pool, [(term, 0), (extremes, 0)], NQ, R5)
                pool.wait_ge(s_id, 2)
                pool.wait_ge(s_const, 4)

            @block.scalar
            def _(act):
                act.dma_start(W1s[:, :, :], W1.rearrange("(k p) f -> p k f", p=P)).then_inc(s_w, 16)
                act.dma_start(W2s[:, :, :], W2.rearrange("(k p) f -> p k f", p=P)).then_inc(s_w, 16)
                with nc.allow_non_contiguous_dma(reason="small vectors"):
                    for tile, vector in ((b1s, b1), (b2s, b2), (gam, gamma), (bet, beta)):
                        act.dma_start(tile[:, :], vector.rearrange("(c p) -> p c", p=P)).then_inc(s_w, 16)

                def std(q, j, rnd):
                    act.wait_ge(s_var, q + 1)
                    nc.scalar.activation(sd[:, j, :], mv[:, j, :, 1], ACT.Sqrt, scale=1.0 / X_SCALE**2,
                                         bias=epsl[:, 0:1]).then_inc(s_std, 1)

                def parts(q, j, rnd):
                    act.wait_ge(s_rst, q * 2 + 2)
                    for t in range(QT):
                        ins = nc.scalar.activation(xin[:, j, t, :], xin[:, j, t, :], ACT.Identity,
                                                   bias=off[:, j, t:t + 1], scale=rsl[:, j, t:t + 1])
                    ins.then_inc(s_xn, 1)
                    if not (isinstance(rnd, int) and rnd == 0):
                        act.wait_ge(s_tab[j], rnd * 16)
                    act.wait_ge(s_xn, q + 1)
                    nc.scalar.activation(pair[:, j, :, 0:D], xin[:, j, :, :], ACT.Identity).then_inc(s_hi, 1)

                act.wait_ge(s_epsc, 1)
                walk(act, [(std, 0), (parts, 1)], NQ, R5)
                act.wait_ge(s_w, 96)

            @block.vector
            def _(dve):
                dve.wait_ge(s_eps, 16)
                nc.vector.tensor_scalar(selfs[:, :], epsb[:, :], 1.0, 1.0 / X_SCALE, ALU.add,
                                        ALU.mult).then_inc(s_self, 1)

                stat_seen = counter(dve, "n_stat_seen", R5 + 1)

                def stat(q, j, rnd):
                    if isinstance(q, int) and q == NQ - 1:
                        dve.wait_ge(s_x[j], 16 * rnd + 32)
                    else:
                        dve.wait_ge(s_x[j], rnd * 16 + 16)
                    for t in range(QT):
                        ins = nc.vector.bn_stats(st[:, j, t, :], xin[:, j, t, :])
                    ins.then_inc(s_stat, 1)
                    wait_count(dve, s_stat, q + 1, stat_seen)
                    for t in range(QT):
                        ins = nc.vector.bn_aggr(mv[:, j, t, :], st[:, j, t, :])
                    ins.then_inc(s_var, 1)

                def norm(q, j, rnd):
                    dve.wait_ge(s_std, q + 1)
                    nc.vector.reciprocal(rsl[:, j, :], sd[:, j, :]).then_inc(s_rst, 1)
                    dve.wait_ge(s_rst, q * 2 + 1)
                    nc.vector.scalar_tensor_tensor(out=off[:, j, :], in0=mv[:, j, :, 0], scalar=-1.0,
                                                   in1=rsl[:, j, :], op0=ALU.mult, op1=ALU.mult).then_inc(s_rst, 1)

                def low(q, j, rnd):
                    dve.wait_ge(s_hi, q + 1)
                    nc.vector.tensor_tensor(pair[:, j, :, D:2 * D], xin[:, j, :, :], pair[:, j, :, 0:D],
                                            ALU.subtract).then_inc(s_lo, 1)

                def ranges(q, j, rnd):
                    if not isinstance(q, int):
                        return
                    if q == 3:
                        dve.wait_ge(s_dst, 32)
                        nc.vector.tensor_copy(dst_all[:, :], dsti[:, :]).then_inc(s_rng, 1)
                        dve.wait_ge(s_rng, 1)
                        by_group = dst_all[:, :].rearrange("p (g t) -> p g t", t=GT)
                        nc.vector.tensor_reduce(low_of[:, :], by_group, AX.X, ALU.min).then_inc(s_ext, 1)
                        nc.vector.tensor_reduce(ext[:, 1, :], by_group, AX.X, ALU.max).then_inc(s_ext, 1)
                        dve.wait_ge(s_ext, 2)
                        nc.vector.tensor_scalar(ext[:, 0, :], low_of[:, :], -1.0, None, ALU.mult).then_inc(s_ext, 1)
                    if q == NQ - R5:
                        link = [1]

                        def then(ins):
                            link[0] += 1
                            ins.then_inc(s_rng, 1)
                            dve.wait_ge(s_rng, link[0])

                        dve.wait_ge(s_all, 1)
                        nc.vector.tensor_scalar(blki[:, 0, :], allx[:, 0, :], -1.0, None, ALU.mult).then_inc(s_rng, 1)
                        nc.vector.tensor_copy(blki[:, 1, :], allx[:, 1, :]).then_inc(s_rng, 1)
                        link[0] += 2
                        dve.wait_ge(s_rng, link[0])
                        then(nc.vector.tensor_scalar(blks[:, :, :], blki[:, :, :], 7, None, ALU.arith_shift_right))
                        then(nc.vector.memset(sfx[:, :, :], float(NB)))
                        then(nc.vector.tensor_copy(sfx[:, 0, 0:NG - 1], blks[:, 0, 1:NG]))
                        for k in range(8):
                            then(nc.vector.tensor_tensor(sfx[:, (k + 1) % 2, 0:NG], sfx[:, k % 2, 0:NG],
                                                         sfx[:, k % 2, 1 << k:(1 << k) + NG], ALU.min))
                        then(nc.vector.tensor_copy(sfi[:, :], sfx[:, 0, 0:NG]))
                        then(nc.vector.tensor_scalar(sfs[:, :], sfi[:, :], 2, None, ALU.arith_shift_right))
                        then(nc.vector.tensor_scalar(packed[:, 0, :], blks[:, 1, :], 128.0, 128.0, ALU.mult, ALU.add))
                        then(nc.vector.scalar_tensor_tensor(out=packed[:, 1, :], in0=sfs[:, :], scalar=16384.0,
                                                            in1=packed[:, 0, :], op0=ALU.mult, op1=ALU.add))
                        nc.vector.tensor_tensor(ctl[:, 0:NG], packed[:, 1, :], blks[:, 0, :], ALU.add)

                walk(dve, [(stat, 0), (norm, 1), (low, 2), (ranges, 0)], NQ, R5)


def stage_edges(nc, table, buf, ident, nodes, src_all, dst_all, ctl, base, iota, stats, W1s, W2s, b1s, b2s):
    with ExitStack() as ctx:
        def sb(name, shape, dt):
            return ctx.enter_context(nc.sbuf_tensor(name, shape, dt))

        def psum(name, shape, dt):
            return ctx.enter_context(nc.psum_tensor(name, shape, dt))

        def sem(name):
            return ctx.enter_context(nc.semaphore(name))

        HR = 4
        LAG = 2
        ZR = 8
        got = sb("e_got", [P, RG, GT, 2 * D], F16)
        idx = sb("e_idx", [P, RG, GT], I32)
        hot = sb("e_hot", [P, HR, GT, P], F16)
        hrow = sb("e_hrow", [P, QT, D], F32)
        hT = sb("e_hT", [P, DK, QN], F32)
        mid = sb("e_mid", [P, H1C, QN], F32)
        zero = sb("e_zero", [P, ZR * ROW], F32)
        sums = psum("e_sums", [P, HR, 2 * D], F32)
        turned = psum("e_turned", [P, DK, QN], F32)
        up = psum("e_up", [P, 2, QN], F32)

        s_flush = sem("e_flush")
        s_free, s_zero, s_zeroed = sem("e_free"), sem("e_zero_s"), sem("e_zeroed")
        s_idx = [sem(f"e_idx{h}") for h in range(2)]
        s_got = [sem(f"e_got{r}") for r in range(RG)]
        s_hot, s_sum, s_add = sem("e_hot_s"), sem("e_sum"), sem("e_add")
        s_hrow, s_turn, s_hT, s_up, s_mid, s_down, s_h2 = (
            sem("e_hrow_s"), sem("e_turn"), sem("e_hT_s"), sem("e_up_s"), sem("e_mid_s"), sem("e_down_s"),
            sem("e_h2"))

        blocks_of = nodes[:, :, :].rearrange("p q (t d) -> p (q t) d", d=D)

        with nc.Block() as block:
            @block.sync
            def _(sp):
                ZERO = NX * SLOTS // (P * ZR)

                def indices(n, h):
                    sp.dma_start(idx[:, 2 * h:2 * h + 2, :],
                                 src_all[:, at(n * 2 + h, 2 * GT)]).then_inc(s_idx[h], 16)

                def next_indices(it):
                    for h in range(2):
                        for r in range(2 * h, 2 * h + 2):
                            sp.wait_ge(s_got[r], it * (16 * GT) + 16 * GT)
                        indices(it + 1, h)

                for h in range(2):
                    indices(0, h)
                sp.wait_ge(s_zero, 1)
                with sp.Fori(0, ZERO) as it:
                    next_indices(it)
                    sp.dma_start(buf[at(it, P * ZR), :].rearrange("(p r) d -> p (r d)", p=P),
                                 zero[:, :]).then_inc(s_zeroed, 16)
                with sp.Fori(ZERO, NG // RG - 1) as it:
                    next_indices(it)
                sp.wait_ge(s_zeroed, 16 * ZERO)

            @block.gpsimd
            def _(pool):
                free = counter(pool, "free", 1)
                have = [counter(pool, f"have{h}", 16) for h in range(2)]
                nc.gpsimd.memset(zero[:, :], 0.0).then_inc(s_zero, 1)
                with pool.Fori(0, NG // RG):
                    for r in range(RG):
                        if r % 2 == 0:
                            pool.wait_ge(s_idx[r // 2], have[r // 2])
                            pool.reg_add(have[r // 2], have[r // 2], 16)
                        pool.wait_ge(s_free, free)
                        pool.reg_add(free, free, 1)
                        for t in range(GT):
                            pool.indirect_dma_start(
                                got[:, r, t, :], None, table,
                                bass.IndirectOffsetOnAxis(ap=idx[:, r, t:t + 1], axis=0)).then_inc(s_got[r], 16)

            @block.tensor
            def _(pe):
                turn = pe.alloc_register("turn")
                done = pe.alloc_register("done")
                pe.reg_mov(turn, 1)
                made = pe.alloc_register("made")
                pe.reg_mov(done, 0)
                pe.reg_mov(made, 0)
                pe.sem_inc(s_free, RG)

                pe.sem_inc(s_turn, 1)

                def transposes(q):
                    pe.wait_ge(s_hrow, q + 1)
                    for k in range(DK):
                        for t in range(QT):
                            ins = nc.tensor.transpose(turned[:, k, t * P:(t + 1) * P],
                                                      hrow[:, t, k * P:(k + 1) * P], ident[:, :])
                    ins.then_inc(s_turn, 1)

                def products(q):
                    pe.wait_ge(s_hT, q + 1)
                    for c in range(H1C):
                        if c >= 2:
                            pe.wait_ge(s_mid, q * H1C + c - 1)
                        for k in range(DK):
                            ins = nc.tensor.matmul(up[:, c % 2, :], W1s[:, k, c * P:(c + 1) * P], hT[:, k, :],
                                                   start=(k == 0), stop=(k == DK - 1))
                        ins.then_inc(s_up, 1)
                    pe.wait_ge(s_mid, q * H1C + H1C)
                    for c in range(DK):
                        for k in range(H1C):
                            ins = nc.tensor.matmul(up[:, c, :], W2s[:, k, c * P:(c + 1) * P], mid[:, k, :],
                                                   start=(k == 0), stop=(k == H1C - 1))
                    ins.then_inc(s_down, 1)

                def quad(number):
                    return nc.s_assert_within(number, 0, NQ - 1,
                                              skip_runtime_bounds_check_because="stage_norm packs it")

                first, end, whole = (pe.alloc_register(n) for n in ("first", "end", "whole"))

                def load_word(number):
                    return pe.value_load(ctl[0:1, number], min_val=0, max_val=1 << 20)

                def unpack(word):
                    pe.reg_mov(first, pe.snap(word % 128))
                    pe.reg_mov(end, pe.snap((word // 128) % 128))
                    pe.reg_mov(whole, pe.snap(word // 16384))

                unpack(load_word(at(0)))
                with pe.Fori(0, NG // RG) as it:
                    for r in range(RG):
                        with pe.Fori(first, end):
                            place = pe.snap(turn) % HR
                            pe.wait_ge(s_got[r], it * (16 * GT) + 16 * GT)
                            pe.wait_ge(s_hot, turn)
                            pe.wait_ge(s_add, turn)
                            pe.reg_add(turn, turn, 1)
                            for t in range(GT):
                                for part in range(2):
                                    ins = nc.tensor.matmul(sums[:, place, 0:D], hot[:, place, t, :],
                                                           got[:, r, t, part * D:(part + 1) * D],
                                                           start=(t == 0 and part == 0),
                                                           stop=(t == GT - 1 and part == 1))
                            ins.then_inc(s_sum, 1)
                        word = load_word(at(it * RG + (r + 1)))
                        pe.wait_ge(s_sum, pe.snap(pe.snap(turn) + 1))
                        pe.sem_inc(s_free, 1)
                        with pe.If(pe.snap(done) < pe.snap(whole)):
                            with pe.Fori(done, whole) as number:
                                with pe.If(number > 0):
                                    products(quad(pe.snap(made)))
                                    pe.reg_add(made, made, 1)
                                transposes(quad(number))
                        pe.reg_mov(done, whole)
                        unpack(word)
                products(NQ - 1)

            @block.scalar
            def _(act):
                def mlp(q):
                    act.wait_ge(s_turn, q + 2)
                    nc.scalar.activation(hT[:, :, :], turned[:, :, :], ACT.Identity).then_inc(s_hT, 1)
                    for c in range(H1C):
                        act.wait_ge(s_up, q * H1C + c + 1)
                        nc.scalar.activation(mid[:, c, :], up[:, c % 2, :], ACT.Relu,
                                             bias=b1s[:, c:c + 1]).then_inc(s_mid, 1)
                    act.wait_ge(s_down, q + 1)
                    for c in range(DK):
                        nc.scalar.activation(
                            nodes[:, at(q), c * QN:(c + 1) * QN].rearrange("p a b -> p (a b)"), up[:, c, :],
                            ACT.Identity, bias=b2s[:, c:c + 1]).then_inc(s_h2, 1)

                with act.Fori(0, NQ) as q:
                    mlp(q)

            @block.vector
            def _(dve):
                turn = dve.alloc_register("turn")
                done = dve.alloc_register("done")
                last = dve.alloc_register("last")
                older = dve.alloc_register("older")
                flushed = dve.alloc_register("flushed")
                dve.reg_mov(turn, 1)
                dve.reg_mov(done, 0)
                measured = dve.alloc_register("measured")
                dve.reg_mov(last, 0)
                dve.reg_mov(older, 0)
                dve.reg_mov(measured, 0)
                dve.reg_mov(flushed, 1)
                nc.vector.memset(sums[:, :, 0:D], 0.0).then_inc(s_sum, LAG)
                dve.wait_ge(s_sum, LAG)
                dve.sem_inc(s_add, 1)

                def place_of(back):
                    return dve.snap(dve.snap(turn) + (HR - back)) % HR

                def add_sums(back, b):
                    place = dve.snap(place_of(back))
                    row = blocks_of[:, b, :].rearrange("p a d -> p (a d)")
                    return nc.vector.scalar_tensor_tensor(out=row, in0=sums[:, place, 0:D], scalar=1.0 / X_SCALE,
                                                          in1=row, op0=ALU.mult, op1=ALU.add)

                def batch_stats(q, width=QN):
                    dve.wait_ge(s_h2, q * DK + DK)
                    for c in range(DK):
                        nc.vector.bn_stats(stats[:, c, at(q, 6)], nodes[:, at(q), c * QN:c * QN + width].rearrange(
                            "p a b -> p (a b)"))

                def quad(number):
                    return nc.s_assert_within(number, 0, NQ - 1,
                                              skip_runtime_bounds_check_because="stage_norm packs it")

                def block_no(register):
                    return at(nc.s_assert_within(dve.snap(register), 0, NB - 1,
                                                 skip_runtime_bounds_check_because="stage_norm packs it"))

                with dve.Fori(0, NG // RG) as it:
                    for r in range(RG):
                        word = dve.value_load(ctl[0:1, at(it * RG + r)], min_val=0, max_val=1 << 20)
                        first = dve.snap(word % 128)
                        end = dve.snap((word // 128) % 128)
                        whole = dve.snap(word // 16384)
                        with dve.Fori(first, end) as number:
                            place = dve.snap(place_of(0))
                            b, before = block_no(number), block_no(older)
                            nc.vector.scalar_tensor_tensor(
                                out=hot[:, place, :, :],
                                in0=dst_all[:, at(it * RG + r, GT)].unsqueeze(2).broadcast_to((P, GT, P)),
                                scalar=base[:, b], in1=iota[:, :].unsqueeze(1).broadcast_to((P, GT, P)),
                                op0=ALU.subtract, op1=ALU.is_equal).then_inc(s_hot, 1)
                            dve.wait_ge(s_sum, turn)
                            dve.wait_ge(s_add, turn)
                            add_sums(LAG, before).then_inc(s_add, 1)
                            dve.reg_mov(older, last)
                            dve.reg_mov(last, number)
                            dve.reg_add(turn, turn, 1)
                        with dve.If(dve.snap(done) < whole):
                            before, newest = block_no(older), block_no(last)
                            dve.wait_ge(s_sum, dve.snap(dve.snap(turn) + 1))
                            dve.wait_ge(s_add, turn)

                            def then(ins):
                                ins.then_inc(s_flush, 1)
                                dve.wait_ge(s_flush, flushed)
                                dve.reg_add(flushed, flushed, 1)

                            then(add_sums(2, before))
                            then(add_sums(1, newest))
                            nc.vector.memset(sums[:, :, 0:D], 0.0).then_inc(s_flush, 1)
                            open_block = dve.snap(whole * QT)
                            dve.reg_mov(last, open_block)
                            dve.reg_mov(older, open_block)
                            with dve.Fori(done, whole) as number:
                                q = quad(number)
                                dve.wait_ge(s_turn, q + 1)
                                nc.vector.tensor_scalar(hrow[:, :, :].rearrange("p t d -> p (t d)"),
                                                        nodes[:, at(q), :].rearrange("p a b -> p (a b)"),
                                                        1.0, None, ALU.mult).then_inc(s_hrow, 1)
                                with dve.If(number > 1):
                                    batch_stats(quad(dve.snap(measured)))
                                    dve.reg_add(measured, measured, 1)
                            dve.wait_ge(s_flush, flushed)
                            dve.reg_add(flushed, flushed, 1)
                        dve.reg_mov(done, whole)
                batch_stats(NQ - 2)
                batch_stats(NQ - 1, N - (NQ - 1) * QN)


def stage_route(nc, x, gate_w, gate_b, buf, out, ident, onesf, epsc, nodes, stats, gam, bet):
    with ExitStack() as ctx:
        def sb(name, shape, dt):
            return ctx.enter_context(nc.sbuf_tensor(name, shape, dt))

        def psum(name, shape, dt):
            return ctx.enter_context(nc.psum_tensor(name, shape, dt))

        def sem(name):
            return ctx.enter_context(nc.semaphore(name))

        bnv = sb("r_bnv", [P, DK, 2], F32)
        bns = sb("r_bns", [P, DK], F32)
        bnr = sb("r_bnr", [P, DK], F32)
        scale = sb("r_scale", [P, DK], F32)
        ms = sb("r_ms", [P, DK], F32)
        shift = sb("r_shift", [P, DK], F32)
        gw = sb("r_gw", [P, DK, NX], F32)
        gb = sb("r_gb", [P, NX], F32)
        tri = sb("r_tri", [P, P], F32)
        rev = sb("r_rev", [P, NX], F32)
        node1 = sb("r_node1", [P, NB], F32)
        xin = sb("r_xin", [P, R5, QT, D], F32)
        row = sb("r_row", [P, R5, QT, ROW], F32)
        hbn = sb("r_hbn", [P, DK, QN], F32)
        xn = sb("r_xn", [P, QT, D], F32)
        xT = sb("r_xT", [P, DK, QN], F32)
        st = sb("r_st", [P, R5, QT, 6], F32)
        mv = sb("r_mv", [P, R5, QT, 2], F32)
        sd = sb("r_sd", [P, R5, QT], F32)
        lg = sb("r_lg", [P, QT, NX], F32)
        mx = sb("r_mx", [P, QT], F32)
        cand = sb("r_cand", [P, QT, NX], F32)
        best = sb("r_best", [P, QT], F32)
        hot = sb("r_hot", [P, QT, NX], F32)
        seen = sb("r_seen", [P, QT + 1, NX], F32)
        mine = sb("r_mine", [P, QT, NX], F32)
        pos = sb("r_pos", [P, QT], F32)
        slot = sb("r_slot", [P, QT], F32)
        over = sb("r_over", [P, QT], F32)
        slot2 = sb("r_slot2", [P, QT], F32)
        pad = sb("r_pad", [P, QT], F32)
        slots = sb("r_slots", [P, R5, QT], I32)
        turned = psum("r_turned", [P, QT, D], F32)
        back = psum("r_back", [P, DK, QN], F32)
        logit = psum("r_logit", [P, QT, NX], F32)
        count = psum("r_count", [P, QT, NX], F32)

        s_gw, s_const, s_tri, s_rows, s_bn = sem("r_gw_s"), sem("r_const"), sem("r_tri_s"), sem("r_rows"), sem("r_bn")
        s_bnsd = sem("r_bnsd")
        s_x = [sem(f"r_x{j}") for j in range(R5)]
        s_out = [sem(f"r_out{j}") for j in range(R5)]
        s_scat = [sem(f"r_scat{j}") for j in range(R5)]
        s_hbn, s_turn, s_x2, s_var, s_std, s_rstd, s_xn, s_back, s_xT, s_logit = (
            sem("r_hbn_s"), sem("r_turn"), sem("r_x2_s"), sem("r_var"), sem("r_std"), sem("r_rstd"), sem("r_xn_s"),
            sem("r_back_s"), sem("r_xT_s"), sem("r_logit_s"))
        s_stat, s_hotv, s_hot, s_count, s_slotv, s_slot, s_node = (
            sem("r_stat"), sem("r_hotv"), sem("r_hot_s"), sem("r_count_s"), sem("r_slotv"), sem("r_slot_s"),
            sem("r_node_s"))

        with nc.Block() as block:
            @block.sync
            def _(sp):
                sp.dma_start(gw[:, :, :], gate_w.rearrange("(k p) e -> p k e", p=P)).then_inc(s_gw, 16)
                sp.dma_start(gb[:, :], gate_b.unsqueeze(0).broadcast_to((P, NX))).then_inc(s_gw, 16)

                def load(q, j, rnd):
                    if not (isinstance(rnd, int) and rnd == 0):
                        sp.wait_ge(s_x2, q - R5 + 1)
                    if isinstance(q, int) and q == NQ - 1:
                        sp.dma_start(xin[:, j, 0, :], x[q * QN:q * QN + P, :]).then_inc(s_x[j], 16)
                        sp.dma_start(xin[0:N - q * QN - P, j, 1, :], x[q * QN + P:N, :]).then_inc(s_x[j], 16)
                    else:
                        sp.dma_start(xin[:, j, :, :],
                                     x[at(q, QN), :].rearrange("(t p) d -> p t d", p=P)).then_inc(s_x[j], 16)

                def store(q, j, rnd):
                    sp.wait_ge(s_x2, q + 1)
                    if isinstance(q, int) and q == NQ - 1:
                        sp.dma_start(out[q * QN:q * QN + P, :], row[:, j, 0, 0:D]).then_inc(s_out[j], 16)
                        sp.dma_start(out[q * QN + P:N, :], row[0:N - q * QN - P, j, 1, 0:D]).then_inc(s_out[j], 16)
                    else:
                        sp.dma_start(out[at(q, QN), :].rearrange("(t p) d -> p t d", p=P),
                                     row[:, j, :, 0:D]).then_inc(s_out[j], 16)

                walk(sp, [(load, 0), (store, 3)], NQ, R5)
                for j in range(R5):
                    sp.wait_ge(s_out[j], 16 * (NQ // R5) + (16 if j == (NQ - 1) % R5 else 0))

            @block.gpsimd
            def _(pool):
                ready = counter(pool, "r_ready", R5 + 1)
                nc.gpsimd.memset(row[:, :, :, D + 3:D + 4], 0.0).then_inc(s_rows, 1)
                nc.gpsimd.memset(seen[:, :, :], 0.0).then_inc(s_const, 1)
                nc.gpsimd.iota(rev[:, :], pattern=[[-1, NX]], base=NX, channel_multiplier=0,
                               allow_small_or_imprecise_dtypes=True).then_inc(s_const, 1)
                nc.gpsimd.iota(node1[:, :], pattern=[[P, NB]], base=1, channel_multiplier=1,
                               allow_small_or_imprecise_dtypes=True).then_inc(s_const, 1)
                nc.gpsimd.affine_select(out=tri[:, :], in_=onesf[:, :], compare_op=ALU.is_ge, fill=0.0,
                                        base=0, pattern=[[1, P]], channel_multiplier=-1).then_inc(s_tri, 1)
                bound = pool.to_reg(NX * SLOTS - 1)

                def scatter(q, j, rnd):
                    wait_count(pool, s_slot, q + 1, ready)
                    for t in range(QT):
                        pool.indirect_dma_start(
                            buf, bass.IndirectOffsetOnAxis(ap=slots[:, j, t:t + 1], axis=0), row[:, j, t, :], None,
                            bounds_check=bound, oob_is_err=False).then_inc(s_scat[j], 16)

                pool.wait_ge(s_rows, 1)
                walk(pool, [(scatter, 0)], NQ, R5)
                for j in range(R5):
                    pool.wait_ge(s_scat[j], 16 * QT * (NQ // R5))

            @block.tensor
            def _(pe):
                def turn(q, j, rnd):
                    pe.wait_ge(s_hbn, q + 1)
                    if not (isinstance(q, int) and q == 0):
                        pe.wait_ge(s_x2, q)
                    for t in range(QT):
                        for k in range(DK):
                            ins = nc.tensor.transpose(turned[:, t, k * P:(k + 1) * P],
                                                      hbn[:, k, t * P:(t + 1) * P], ident[:, :])
                    ins.then_inc(s_turn, 1)

                def turn_back(q, j, rnd):
                    pe.wait_ge(s_xn, q + 1)
                    if not (isinstance(q, int) and q == 0):
                        pe.wait_ge(s_xT, q)
                    for k in range(DK):
                        for t in range(QT):
                            ins = nc.tensor.transpose(back[:, k, t * P:(t + 1) * P],
                                                      xn[:, t, k * P:(k + 1) * P], ident[:, :])
                    ins.then_inc(s_back, 1)

                def gate(q, j, rnd):
                    pe.wait_ge(s_xT, q + 1)
                    if not (isinstance(q, int) and q == 0):
                        pe.wait_ge(s_hot, q)
                    for t in range(QT):
                        for k in range(DK):
                            ins = nc.tensor.matmul(logit[:, t, :], xT[:, k, t * P:(t + 1) * P], gw[:, k, :],
                                                   start=(k == 0), stop=(k == DK - 1))
                    ins.then_inc(s_logit, 1)

                def counts(q, j, rnd):
                    pe.wait_ge(s_hot, q + 1)
                    if not (isinstance(q, int) and q == 0):
                        pe.wait_ge(s_slot, q)
                    nc.tensor.matmul(count[:, :, :], tri[:, :], hot[:, :, :], start=True, stop=False)
                    nc.tensor.matmul(count[:, :, :], onesf[:, :], seen[:, 0:QT, :],
                                     start=False, stop=True).then_inc(s_count, 1)

                pe.wait_ge(s_gw, 32)
                pe.wait_ge(s_tri, 1)
                walk(pe, [(counts, 4), (turn, 1), (gate, 3), (turn_back, 2)], NQ, R5)

            @block.scalar
            def _(act):
                act.wait_ge(s_bn, 1)
                nc.scalar.activation(bns[:, :], bnv[:, :, 1], ACT.Sqrt, bias=epsc[:, 0:1]).then_inc(s_bnsd, 1)
                act.wait_ge(s_bn, 2)

                def norm(q, j, rnd):
                    if not (isinstance(q, int) and q == 0):
                        act.wait_ge(s_turn, q)
                    for k in range(DK):
                        ins = nc.scalar.activation(
                            hbn[:, k, :], nodes[:, at(q), k * QN:(k + 1) * QN].rearrange("p a b -> p (a b)"),
                            ACT.Identity, bias=shift[:, k:k + 1], scale=scale[:, k:k + 1])
                    ins.then_inc(s_hbn, 1)

                def rows(q, j, rnd):
                    act.wait_ge(s_rstd, q * 2 + 2)
                    if not (isinstance(q, int) and q == 0):
                        act.wait_ge(s_back, q)
                    for t in range(QT):
                        ins = nc.scalar.activation(xn[:, t, :], row[:, j, t, 0:D], ACT.Identity,
                                                   bias=row[:, j, t, D + 1:D + 2], scale=row[:, j, t, D:D + 1])
                    ins.then_inc(s_xn, 1)

                def std(q, j, rnd):
                    act.wait_ge(s_var, q + 1)
                    nc.scalar.activation(sd[:, j, :], mv[:, j, :, 1], ACT.Sqrt, bias=epsc[:, 0:1]).then_inc(s_std, 1)

                def columns(q, j, rnd):
                    act.wait_ge(s_back, q + 1)
                    if not (isinstance(q, int) and q == 0):
                        act.wait_ge(s_logit, q)
                    nc.scalar.activation(xT[:, :, :], back[:, :, :], ACT.Identity).then_inc(s_xT, 1)

                walk(act, [(columns, 3), (rows, 2), (norm, 0), (std, 1)], NQ, R5)

            @block.vector
            def _(dve):
                for k in range(DK):
                    ins = nc.vector.bn_aggr(bnv[:, k, :], stats[:, k, :])
                ins.then_inc(s_bn, 1)
                dve.wait_ge(s_bnsd, 1)
                nc.vector.reciprocal(bnr[:, :], bns[:, :]).then_inc(s_node, 1)
                dve.wait_ge(s_node, 1)
                nc.vector.tensor_tensor(scale[:, :], bnr[:, :], gam[:, :], ALU.mult).then_inc(s_node, 1)
                dve.wait_ge(s_node, 2)
                nc.vector.tensor_tensor(ms[:, :], bnv[:, :, 0], scale[:, :], ALU.mult).then_inc(s_node, 1)
                dve.wait_ge(s_node, 3)
                nc.vector.tensor_tensor(shift[:, :], bet[:, :], ms[:, :], ALU.subtract).then_inc(s_bn, 1)
                dve.wait_ge(s_gw, 32)
                dve.wait_ge(s_const, 3)
                dve.wait_ge(s_rows, 1)

                stat_seen = counter(dve, "r_stat_seen", R5)

                def add(q, j, rnd):
                    dve.wait_ge(s_turn, q + 1)
                    if isinstance(q, int) and q == NQ - 1:
                        dve.wait_ge(s_x[j], 16 * rnd + 32)
                    else:
                        dve.wait_ge(s_x[j], rnd * 16 + 16)
                    if not (isinstance(rnd, int) and rnd == 0):
                        dve.wait_ge(s_out[j], rnd * 16)
                        dve.wait_ge(s_scat[j], rnd * (16 * QT))
                    nc.vector.tensor_tensor(row[:, j, :, 0:D], turned[:, :, :], xin[:, j, :, :],
                                            ALU.add).then_inc(s_x2, 1)
                    dve.wait_ge(s_x2, q + 1)
                    for t in range(QT):
                        ins = nc.vector.bn_stats(st[:, j, t, :], row[:, j, t, 0:D])
                    ins.then_inc(s_stat, 1)
                    wait_count(dve, s_stat, q + 1, stat_seen)
                    for t in range(QT):
                        ins = nc.vector.bn_aggr(mv[:, j, t, :], st[:, j, t, :])
                    ins.then_inc(s_var, 1)

                def norm(q, j, rnd):
                    dve.wait_ge(s_std, q + 1)
                    nc.vector.reciprocal(row[:, j, :, D], sd[:, j, :]).then_inc(s_rstd, 1)
                    dve.wait_ge(s_rstd, q * 2 + 1)
                    nc.vector.scalar_tensor_tensor(out=row[:, j, :, D + 1], in0=mv[:, j, :, 0], scalar=-1.0,
                                                   in1=row[:, j, :, D], op0=ALU.mult, op1=ALU.mult
                                                   ).then_inc(s_rstd, 1)

                def pick(q, j, rnd):
                    CH = 10

                    def then(k, ins):
                        ins.then_inc(s_hotv, 1)
                        dve.wait_ge(s_hotv, q * CH + k)

                    dve.wait_ge(s_logit, q + 1)
                    if not (isinstance(q, int) and q == 0):
                        dve.wait_ge(s_count, q)
                    then(1, nc.vector.tensor_tensor(lg[:, :, :], logit[:, :, :],
                                                    gb[:, :].unsqueeze(1).broadcast_to((P, QT, NX)), ALU.add))
                    then(2, nc.vector.tensor_reduce(mx[:, :], lg[:, :, :], AX.X, ALU.max))
                    then(3, nc.vector.tensor_tensor(row[:, j, :, D + 4:ROW], lg[:, :, :],
                                                    mx[:, :].unsqueeze(2).broadcast_to((P, QT, NX)), ALU.subtract))
                    then(4, nc.vector.scalar_tensor_tensor(
                        out=cand[:, :, :], in0=row[:, j, :, D + 4:ROW], scalar=0.0,
                        in1=rev[:, :].unsqueeze(1).broadcast_to((P, QT, NX)), op0=ALU.is_ge, op1=ALU.mult))
                    then(5, nc.vector.tensor_reduce(best[:, :], cand[:, :, :], AX.X, ALU.max))
                    nc.vector.tensor_tensor(hot[:, :, :], rev[:, :].unsqueeze(1).broadcast_to((P, QT, NX)),
                                            best[:, :].unsqueeze(2).broadcast_to((P, QT, NX)),
                                            ALU.is_equal).then_inc(s_hotv, 1)
                    then(7, nc.vector.tensor_copy(seen[:, 0, :], seen[:, QT, :]))
                    for t in range(QT - 1):
                        then(8 + t, nc.vector.tensor_tensor(seen[:, t + 1, :], seen[:, t, :], hot[:, t, :], ALU.add))
                    nc.vector.tensor_tensor(seen[:, QT, :], seen[:, QT - 1, :], hot[:, QT - 1, :],
                                            ALU.add).then_inc(s_hot, 1)

                def place(q, j, rnd):
                    CH = 7

                    def then(k, ins):
                        ins.then_inc(s_slotv, 1)
                        dve.wait_ge(s_slotv, q * CH + k)

                    dve.wait_ge(s_count, q + 1)
                    dve.wait_ge(s_hot, q + 1)
                    then(1, nc.vector.tensor_tensor(mine[:, :, :], count[:, :, :], hot[:, :, :], ALU.mult))
                    then(2, nc.vector.tensor_reduce(pos[:, :], mine[:, :, :], AX.X, ALU.add))
                    then(3, nc.vector.scalar_tensor_tensor(out=slot[:, :], in0=best[:, :], scalar=-float(SLOTS),
                                                           in1=pos[:, :], op0=ALU.mult, op1=ALU.add))
                    nc.vector.tensor_scalar(over[:, :], pos[:, :], float(CAP), SKIP, ALU.is_gt,
                                            ALU.mult).then_inc(s_slotv, 1)
                    then(5, nc.vector.tensor_scalar(pad[:, :], node1[:, at(q, QT)], float(N), SKIP, ALU.is_gt,
                                                    ALU.mult))
                    nc.vector.tensor_scalar(row[:, j, :, D + 2], node1[:, at(q, QT)], 1.0, None,
                                            ALU.mult).then_inc(s_slotv, 1)
                    then(7, nc.vector.scalar_tensor_tensor(out=slot2[:, :], in0=slot[:, :],
                                                           scalar=float(NX * SLOTS - 1), in1=over[:, :],
                                                           op0=ALU.add, op1=ALU.add))
                    nc.vector.tensor_tensor(slots[:, j, :], slot2[:, :], pad[:, :], ALU.add).then_inc(s_slot, 1)

                walk(dve, [(place, 4), (add, 1), (pick, 3), (norm, 1)], NQ, R5)


def stage_experts(nc, buf, w1, xb1, w2, xb2, out, ident):
    with ExitStack() as ctx:
        def sb(name, shape, dt):
            return ctx.enter_context(nc.sbuf_tensor(name, shape, dt))

        def psum(name, shape, dt):
            return ctx.enter_context(nc.psum_tensor(name, shape, dt))

        def sem(name):
            return ctx.enter_context(nc.semaphore(name))

        NS = NX * SG
        R8 = 2 * SG
        RR = 4
        MB = 4
        w1f = sb("x_w1f", [P, DK, F], F32)
        w2f = sb("x_w2f", [P, FC, D], F32)
        b1f = sb("x_b1f", [P, FC], F32)
        w1h = sb("x_w1h", [P, 2, DK, F], F16)
        w1l = sb("x_w1l", [P, 2, DK, F], F16)
        w2h = sb("x_w2h", [P, 2, FC, D], F16)
        w2l = sb("x_w2l", [P, 2, FC, D], F16)
        b1s = sb("x_b1s", [P, 2, FC], F32)
        b2s = sb("x_b2s", [P, 2, D], F32)
        row = sb("x_row", [P, RR, QT, ROW], F32)
        xn = sb("x_xn", [P, QT, D], F32)
        xTh = sb("x_xTh", [P, 2, DK, QN], F16)
        xTl = sb("x_xTl", [P, 2, DK, QN], F16)
        midf = sb("x_midf", [P, MB, QN], F32)
        midh = sb("x_midh", [P, 2, FC, QN], F16)
        midl = sb("x_midl", [P, 2, FC, QN], F16)
        ex = sb("x_ex", [P, QT, NX], F32)
        tot = sb("x_tot", [P, QT], F32)
        prob = sb("x_prob", [P, RR, QT], F32)
        gone = sb("x_gone", [P, QT], F32)
        nodei = sb("x_nodei", [P, RR, QT], I32)
        yb = sb("x_yb", [P, QT, D], F32)
        y = sb("x_y", [P, QT, D], F32)
        up1 = sb("x_up1", [P, QT, D], F32)
        dn1 = sb("x_dn1", [P, QT, D], F32)
        fine = sb("x_fine", [P, QT, D], I32)
        res = sb("x_res", [P, RR, QT, D], F32)
        first_row = sb("x_first_row", [1, NX, SG], F32)
        taken = sb("x_taken", [1, NX, SG], F32)
        groups = sb("x_groups", [1, NX // 2, 2], F32)
        words = sb("x_words", [1, NX // 2], I32)
        turned = psum("x_turned", [P, DK, QN], F32)
        up = psum("x_up", [P, MB, QN], F32)
        down = psum("x_down", [P, QT, D], F32)

        s_row = [sem(f"x_row{j}") for j in range(RR)]
        s_scat = [sem(f"x_scat{j}") for j in range(RR)]
        s_zero, s_first, s_groups, s_w, s_whi, s_split = (
            sem("x_zero"), sem("x_first"), sem("x_groups_s"), sem("x_w"), sem("x_whi"), sem("x_split"))
        s_xn, s_turn, s_xT, s_xlo, s_up, s_mid, s_mlo, s_down, s_exp, s_meta, s_yv, s_res = (
            sem("x_xn_s"), sem("x_turn"), sem("x_xT_s"), sem("x_xlo"), sem("x_up_s"), sem("x_mid_s"), sem("x_mlo"),
            sem("x_down_s"), sem("x_exp"), sem("x_meta"), sem("x_yv"), sem("x_res_s"))

        def expert(j, rnd):
            return rnd * 2 + j // SG

        def landed(j, rnd):
            return rnd * (R8 // RR) + j // RR + 1

        def group_counts(engine):
            word = engine.alloc_register("round_word")
            engine.wait_ge(s_groups, 3)

            def take(s, j, rnd):
                if j == 0:
                    engine.reg_mov(word, engine.value_load(words[0:1, at(rnd)], min_val=0, max_val=63))

            def branch(own, j, work, skip):
                if j == 0:
                    engine.reg_mov(own, word)
                used = engine.snap(engine.snap(own) % 8) if j < SG else engine.snap(engine.snap(own) // 8)
                with engine.If(used > j % SG):
                    work()
                with engine.Else():
                    skip()

            return take, branch

        with nc.Block() as block:
            @block.sync
            def _(sp):
                def weights(s, j, rnd):
                    e = expert(j, rnd)
                    if j % SG or (isinstance(s, int) and e + 1 >= NX):
                        return
                    if isinstance(s, int) and e == 0:
                        sp.wait_ge(s_split, 1)
                    else:
                        sp.wait_ge(s_res, e * SG)
                    fetch(e + 1, (j // SG + 1) % 2)

                def fetch(e, h):
                    sp.dma_start(w1f[:, :, :], w1[at(e), :, :].rearrange("a (k p) f -> p (a k) f", p=P)).then_inc(s_w, 16)
                    sp.dma_start(w2f[:, :, :], w2[at(e), :, :].rearrange("a (k p) d -> p (a k) d", p=P)).then_inc(s_w, 16)
                    with nc.allow_non_contiguous_dma(reason="small vector"):
                        sp.dma_start(b1f[:, :], xb1[at(e), :].rearrange("a (c p) -> p (a c)", p=P)).then_inc(s_w, 16)
                    sp.dma_start(b2s[:, h, :], xb2[at(e), :].broadcast_to((P, D))).then_inc(s_w, 16)

                def load(s, j, rnd):
                    if not (isinstance(s, int) and s < RR):
                        sp.wait_ge(s_res, s - RR + 1)
                    sp.dma_start(row[:, j % RR, :, :],
                                 buf[at(s, QN), :].rearrange("(t p) d -> p t d", p=P)).then_inc(s_row[j % RR], 16)

                with nc.allow_non_contiguous_dma(reason="one word of the first slot of each group"):
                    sp.dma_start(first_row[:, :, :], buf.rearrange("(e g n) d -> n e g d", g=SG, n=QN)[0:1, :, :, D + 2]
                                 ).then_inc(s_first, 16)
                fetch(0, 0)
                walk(sp, [(load, 0), (weights, 3)], NS, R8)

            @block.gpsimd
            def _(pool):
                take, branch = group_counts(pool)
                lows = pool.alloc_register("lows_word")
                ready = counter(pool, "x_ready", R8 + 1 - 3)
                bound = pool.to_reg(N - 1)

                def low_hidden(s, j, rnd):
                    def work():
                        if not (isinstance(s, int) and s < 2):
                            pool.wait_ge(s_down, s - 1)
                        for c in range(FC):
                            pool.wait_ge(s_mid, s * FC + c + 1)
                            nc.gpsimd.tensor_tensor(midl[:, j % 2, c, :], midf[:, c % MB, :], midh[:, j % 2, c, :],
                                                    ALU.subtract).then_inc(s_mlo, 1)

                    def skip():
                        if not (isinstance(s, int) and s == 0):
                            pool.wait_ge(s_mlo, s * FC)
                        pool.sem_inc(s_mlo, FC)

                    branch(lows, j, work, skip)

                def scatter(s, j, rnd):
                    r = j % RR
                    wait_count(pool, s_res, s + 1, ready)
                    for t in range(QT):
                        pool.indirect_dma_start(
                            out, bass.IndirectOffsetOnAxis(ap=nodei[:, r, t:t + 1], axis=0),
                            res[:, r, t, :], None, bounds_check=bound, oob_is_err=False).then_inc(s_scat[r], 16)

                nc.gpsimd.memset(res[:, :, :, :], 0.0).then_inc(s_zero, 1)
                walk(pool, [(take, 0), (low_hidden, 1), (scatter, 3)], NS, R8)
                for j in range(RR):
                    pool.wait_ge(s_scat[j], 16 * QT * (NS // RR))

            @block.tensor
            def _(pe):
                take, branch = group_counts(pe)
                ups = pe.alloc_register("ups_word")
                downs = pe.alloc_register("downs_word")

                def turn(s, j, rnd):
                    pe.wait_ge(s_xn, s + 1)
                    if not (isinstance(s, int) and s == 0):
                        pe.wait_ge(s_xlo, s)
                    for k in range(DK):
                        for t in range(QT):
                            ins = nc.tensor.transpose(turned[:, k, t * P:(t + 1) * P],
                                                      xn[:, t, k * P:(k + 1) * P], ident[:, :])
                    ins.then_inc(s_turn, 1)

                def product_up(s, j, rnd):
                    h = j // SG

                    def work():
                        pe.wait_ge(s_split, expert(j, rnd) + 1)
                        pe.wait_ge(s_xlo, s + 1)
                        for c in range(FC):
                            cols = slice(c * P, (c + 1) * P)
                            if not (isinstance(s, int) and s == 0 and c < MB):
                                pe.wait_ge(s_mid, s * FC + c + 1 - MB)
                            passes = [(w, x, k) for k in range(DK) for w, x in ((w1h, xTh), (w1h, xTl), (w1l, xTh))]
                            for n, (w, x, k) in enumerate(passes):
                                ins = nc.tensor.matmul(up[:, c % MB, :], w[:, h, k, cols], x[:, j % 2, k, :],
                                                       start=(n == 0), stop=(n == len(passes) - 1))
                            ins.then_inc(s_up, 1)

                    def skip():
                        if not (isinstance(s, int) and s == 0):
                            pe.wait_ge(s_up, s * FC)
                        pe.sem_inc(s_up, FC)

                    branch(ups, j, work, skip)

                def product_down(s, j, rnd):
                    h = j // SG

                    def work():
                        pe.wait_ge(s_mlo, s * FC + FC)
                        if not (isinstance(s, int) and s == 0):
                            pe.wait_ge(s_yv, s * 7 - 6)
                        for t in range(QT):
                            rows = slice(t * P, (t + 1) * P)
                            passes = [(m, w, k) for k in range(FC)
                                      for m, w in ((midh, w2h), (midh, w2l), (midl, w2h))]
                            for n, (m, w, k) in enumerate(passes):
                                ins = nc.tensor.matmul(down[:, t, :], m[:, j % 2, k, rows], w[:, h, k, :],
                                                       start=(n == 0), stop=(n == len(passes) - 1))
                        ins.then_inc(s_down, 1)

                    def skip():
                        if not (isinstance(s, int) and s == 0):
                            pe.wait_ge(s_down, s)
                        pe.sem_inc(s_down, 1)

                    branch(downs, j, work, skip)

                walk(pe, [(take, 0), (turn, 0), (product_up, 1), (product_down, 2)], NS, R8)

            @block.scalar
            def _(act):
                take, branch = group_counts(act)
                mids = act.alloc_register("mids_word")

                def columns(s, j, rnd):
                    act.wait_ge(s_turn, s + 1)
                    if not (isinstance(s, int) and s < 2):
                        act.wait_ge(s_up, s * FC - FC)
                    nc.scalar.activation(xTh[:, j % 2, :, :], turned[:, :, :], ACT.Identity,
                                         scale=X_SCALE).then_inc(s_xT, 1)

                def expo(s, j, rnd):
                    act.wait_ge(s_row[j % RR], landed(j, rnd) * 16)
                    if not (isinstance(s, int) and s == 0):
                        act.wait_ge(s_meta, s * 3)
                    nc.scalar.activation(ex[:, :, :], row[:, j % RR, :, D + 4:ROW], ACT.Exp).then_inc(s_exp, 1)

                def hidden(s, j, rnd):
                    h = j // SG

                    def work():
                        if not (isinstance(s, int) and s < 2):
                            act.wait_ge(s_down, s - 1)
                        act.wait_ge(s_split, expert(j, rnd) + 1)
                        for c in range(FC):
                            act.wait_ge(s_up, s * FC + c + 1)
                            if not (isinstance(s, int) and s == 0 and c < MB):
                                act.wait_ge(s_mlo, s * FC + c + 1 - MB)
                            for m in (midf[:, c % MB, :], midh[:, j % 2, c, :]):
                                ins = nc.scalar.activation(m, up[:, c % MB, :], ACT.Relu, bias=b1s[:, h, c:c + 1],
                                                           scale=MID_SCALE / (X_SCALE * W_SCALE))
                            ins.then_inc(s_mid, 1)

                    def skip():
                        if not (isinstance(s, int) and s == 0):
                            act.wait_ge(s_mid, s * FC)
                        act.sem_inc(s_mid, FC)

                    branch(mids, j, work, skip)

                def split(s, j, rnd):
                    e = expert(j, rnd) + 1
                    if j % SG or (isinstance(s, int) and e >= NX):
                        return
                    if not (isinstance(s, int) and e == 1):
                        act.wait_ge(s_down, (e - 1) * SG)
                    high_weights(e, (j // SG + 1) % 2)

                def high_weights(e, h):
                    act.wait_ge(s_w, e * 64 + 64)
                    nc.scalar.activation(w1h[:, h, :, :], w1f[:, :, :], ACT.Identity, scale=W_SCALE)
                    nc.scalar.activation(w2h[:, h, :, :], w2f[:, :, :], ACT.Identity, scale=W_SCALE
                                         ).then_inc(s_whi, 1)

                high_weights(0, 0)
                walk(act, [(take, 0), (expo, 0), (columns, 0), (hidden, 1), (split, 3)], NS, R8)

            @block.vector
            def _(dve):
                dve.wait_ge(s_first, 16)
                nc.vector.tensor_scalar(taken[:, :, :], first_row[:, :, :], 0.5, None, ALU.is_gt).then_inc(s_groups, 1)
                dve.wait_ge(s_groups, 1)
                nc.vector.tensor_reduce(groups[:, :, :].rearrange("p a b -> p (a b)"), taken[:, :, :], AX.X,
                                        ALU.add).then_inc(s_groups, 1)
                dve.wait_ge(s_groups, 2)
                nc.vector.scalar_tensor_tensor(out=words[:, :], in0=groups[:, :, 1], scalar=8.0, in1=groups[:, :, 0],
                                               op0=ALU.mult, op1=ALU.add).then_inc(s_groups, 1)
                take, branch = group_counts(dve)
                ends = dve.alloc_register("ends_word")

                def norm(s, j, rnd):
                    dve.wait_ge(s_row[j % RR], landed(j, rnd) * 16)
                    if not (isinstance(s, int) and s == 0):
                        dve.wait_ge(s_turn, s)
                    for t in range(QT):
                        ins = nc.vector.tensor_scalar(xn[:, t, :], row[:, j % RR, t, 0:D], row[:, j % RR, t, D:D + 1],
                                                      row[:, j % RR, t, D + 1:D + 2], ALU.mult, ALU.add)
                    ins.then_inc(s_xn, 1)

                def split(s, j, rnd):
                    e = expert(j, rnd) + 1
                    if j % SG or (isinstance(s, int) and e >= NX):
                        return
                    low_weights(e, (j // SG + 1) % 2)

                def low_weights(e, h):
                    dve.wait_ge(s_whi, e + 1)
                    nc.vector.tensor_scalar(b1s[:, h, :], b1f[:, :], MID_SCALE, None, ALU.mult)
                    nc.vector.scalar_tensor_tensor(out=w1l[:, h, :, :], in0=w1f[:, :, :], scalar=W_SCALE,
                                                   in1=w1h[:, h, :, :], op0=ALU.mult, op1=ALU.subtract)
                    nc.vector.scalar_tensor_tensor(out=w2l[:, h, :, :], in0=w2f[:, :, :], scalar=W_SCALE,
                                                   in1=w2h[:, h, :, :], op0=ALU.mult, op1=ALU.subtract
                                                   ).then_inc(s_split, 1)

                def low_columns(s, j, rnd):
                    dve.wait_ge(s_xT, s + 1)
                    nc.vector.scalar_tensor_tensor(out=xTl[:, j % 2, :, :], in0=turned[:, :, :], scalar=X_SCALE,
                                                   in1=xTh[:, j % 2, :, :], op0=ALU.mult, op1=ALU.subtract
                                                   ).then_inc(s_xlo, 1)

                def meta(s, j, rnd):
                    dve.wait_ge(s_exp, s + 1)
                    if not (isinstance(s, int) and s < RR):
                        dve.wait_ge(s_scat[j % RR], (landed(j, rnd) - 1) * (16 * QT))
                    nc.vector.tensor_reduce(tot[:, :], ex[:, :, :], AX.X, ALU.add).then_inc(s_meta, 1)
                    nc.vector.tensor_scalar(gone[:, :], row[:, j % RR, :, D + 2], 0.5, SKIP, ALU.is_lt,
                                            ALU.mult).then_inc(s_meta, 1)
                    dve.wait_ge(s_meta, s * 3 + 2)
                    nc.vector.reciprocal(prob[:, j % RR, :], tot[:, :])
                    nc.vector.scalar_tensor_tensor(out=nodei[:, j % RR, :], in0=row[:, j % RR, :, D + 2], scalar=-1.0,
                                                   in1=gone[:, :], op0=ALU.add, op1=ALU.add).then_inc(s_meta, 1)

                guard_seen = counter(dve, "x_guard_seen", (R8 - 3) * 7 + 6)

                def finish(s, j, rnd):
                    r = j % RR

                    def then(k, ins):
                        ins.then_inc(s_yv, 1)
                        dve.wait_ge(s_yv, s * 7 + k)

                    def work():
                        dve.wait_ge(s_down, s + 1)
                        dve.wait_ge(s_w, expert(j, rnd) * 64 + 64)
                        then(1, nc.vector.scalar_tensor_tensor(
                            out=yb[:, :, :], in0=down[:, :, :], scalar=1.0 / (MID_SCALE * W_SCALE),
                            in1=b2s[:, j // SG, :].unsqueeze(1).broadcast_to((P, QT, D)), op0=ALU.mult, op1=ALU.add))
                        then(2, nc.vector.tensor_tensor(y[:, :, :], yb[:, :, :],
                                                        prob[:, r, :].unsqueeze(2).broadcast_to((P, QT, D)), ALU.mult))
                        nc.vector.tensor_scalar(up1[:, :, :], y[:, :, :], 0.0, 1e4, ALU.is_gt, ALU.mult).then_inc(s_yv, 1)
                        nc.vector.tensor_scalar(dn1[:, :, :], y[:, :, :], 0.0, -1e4, ALU.is_lt, ALU.mult).then_inc(s_yv, 1)
                        then(5, nc.vector.tensor_scalar(fine[:, :, :], y[:, :, :], 0.0, 0.0, ALU.mult, ALU.is_equal))
                        nc.vector.tensor_tensor(up1[:, :, :], up1[:, :, :], dn1[:, :, :], ALU.add).then_inc(s_yv, 1)
                        wait_count(dve, s_yv, s * 7 + 6, guard_seen, 7)
                        then(7, nc.vector.copy_predicated(up1[:, :, :], fine[:, :, :], y[:, :, :]))
                        nc.vector.tensor_tensor(res[:, r, :, :], up1[:, :, :], row[:, r, :, 0:D],
                                                ALU.add).then_inc(s_res, 1)

                    def skip():
                        if not isinstance(s, int):
                            dve.reg_add(guard_seen, guard_seen, 7)
                        if not (isinstance(s, int) and s == 0):
                            dve.wait_ge(s_yv, s * 7)
                            dve.wait_ge(s_res, s)
                        dve.sem_inc(s_yv, 7)
                        dve.sem_inc(s_res, 1)

                    branch(ends, j, work, skip)

                low_weights(0, 0)
                dve.wait_ge(s_zero, 1)
                walk(dve, [(take, 0), (norm, 0), (meta, 0), (finish, 3), (low_columns, 0), (split, 3)], NS, R8)


def kernel(x, src, dst, L0_gnn_eps, L0_gnn_W1, L0_gnn_b1, L0_gnn_W2, L0_gnn_b2, L0_gnn_gamma, L0_gnn_beta,
           L0_ffn_gate_w, L0_ffn_gate_b, L0_ffn_w1, L0_ffn_b1, L0_ffn_w2, L0_ffn_b2):
    import concourse.bacc as bacc
    from concourse.bass_utils import run_bass_kernel_spmd

    def edge_tiles(a):
        a = np.asarray(a)
        return np.ascontiguousarray(a[:EFULL * P].reshape(EFULL, P).T), np.ascontiguousarray(a[EFULL * P:, None])

    src_full, src_tail = edge_tiles(src)
    dst_full, dst_tail = edge_tiles(dst)
    arrays = {
        "x": x, "src": src_full, "dst": dst_full, "src_tail": src_tail, "dst_tail": dst_tail, "eps": L0_gnn_eps,
        "W1": L0_gnn_W1, "b1": L0_gnn_b1, "W2": L0_gnn_W2, "b2": L0_gnn_b2, "gamma": L0_gnn_gamma,
        "beta": L0_gnn_beta, "gate_w": L0_ffn_gate_w, "gate_b": L0_ffn_gate_b, "w1": L0_ffn_w1, "xb1": L0_ffn_b1,
        "w2": L0_ffn_w2, "xb2": L0_ffn_b2,
    }
    nc = bacc.Bacc("TRN2", target_bir_lowering=False, num_devices=1)
    ins, aps = {}, {}
    for name, a in arrays.items():
        a = np.ascontiguousarray(a)
        ins[f"in_{name}"] = a
        aps[name] = nc.dram_tensor(f"in_{name}", a.shape, mybir.dt.from_np(a.dtype), kind="ExternalInput").ap()
    out = nc.dram_tensor("out", (N, D), F32, kind="ExternalOutput").ap()
    kernel_program(nc, out=out, **aps)
    return run_bass_kernel_spmd(nc, [ins], core_ids=[0]).results[0]["out"]
```

```python
from contextlib import ExitStack

import numpy as np

import concourse.bass as bass
from concourse import mybir

ALU = mybir.AluOpType
ACT = mybir.ActivationFunctionType
AX = mybir.AxisListType
RMAX = bass.bass_isa.ReduceOp.max
F32 = mybir.dt.float32
F16 = mybir.dt.float16
I32 = mybir.dt.int32
U32 = mybir.dt.uint32
U8 = mybir.dt.uint8

P = 128
N = 12500
D = 256
NE = 200000
NX = 8
F = 1024
CAP = -(-5 * N // (4 * NX))
DK = D // P
H1 = 2 * D
H1C = H1 // P
FC = F // P
QT = 4
QN = QT * P
NQ = -(-N // QN)
NB = NQ * QT
ET = -(-NE // P)
EFULL = NE // P
ETAIL = NE - EFULL * P
GT = 8
RG = 4
NG = -(-ET // (GT * RG)) * RG
EP = NG * GT
PAD_DST = NB * P - QN + 255
SLOTS = QN * -(-CAP // QN)
SG = SLOTS // QN
ROW = D + 12
R5 = 5
X_SCALE, W_SCALE, MID_SCALE = 2.0 ** 10, 2.0 ** 8, 2.0 ** 4
EPS = 1e-5
BIG = 3.4028234663852886e38
SKIP = float(1 << 24)

assert NQ % R5 == 0 and NG % RG == 0 and D == 2 * P and PAD_DST >= N


def walk(engine, stages, count, ring):
    def step(s):
        for stage, lag in stages:
            if 0 <= s - lag < count:
                stage(s - lag, (s - lag) % ring, (s - lag) // ring)

    for s in range(ring):
        step(s)
    with engine.Fori(1, count // ring - 1) as it:
        for j in range(ring):
            for stage, lag in stages:
                stage(it * ring + j - lag, (j - lag) % ring, it if j >= lag else it - 1)
    for s in range(count - ring, count + max(lag for _, lag in stages)):
        step(s)


def wait_count(engine, sem, value, register, step=1):
    if isinstance(value, int):
        engine.wait_ge(sem, value)
    else:
        engine.wait_ge(sem, register)
        engine.reg_add(register, register, step)


def counter(engine, name, start):
    register = engine.alloc_register(name)
    engine.reg_mov(register, start)
    return register


def at(q, n=1):
    return bass.ds(q * n, n)


def kernel_program(nc, x, src, dst, src_tail, dst_tail, eps, W1, b1, W2, b2, gamma, beta, gate_w, gate_b,
                   w1, xb1, w2, xb2, out):
    table = nc.dram_tensor("table", (NB * P, 2 * D), F16, kind="Internal").ap()
    buf = nc.dram_tensor("slot_rows", (NX * SLOTS, ROW), F32, kind="Internal").ap()
    with ExitStack() as whole:
        def keep(name, shape, dt):
            return whole.enter_context(nc.sbuf_tensor(name, shape, dt))

        ident = keep("ident", [P, P], F32)
        epsc = keep("epsc", [P, 1], F32)

        with ExitStack() as gnn:
            def hold(name, shape, dt):
                return gnn.enter_context(nc.sbuf_tensor(name, shape, dt))

            nodes = hold("nodes", [P, NQ, QT * D], F32)
            src_all = hold("src_all", [P, EP], I32)
            dst_all = hold("dst_all", [P, EP], F32)
            ctl = hold("ctl", [P, NG + 1], I32)
            base = hold("base", [P, NB], F32)
            iota = hold("iota", [P, P], F16)
            stats = hold("stats", [P, DK, NQ * 6], F32)
            W1s = hold("W1s", [P, DK, H1], F32)
            W2s = hold("W2s", [P, H1C, D], F32)
            b1s = hold("b1s", [P, H1C], F32)
            b2s = hold("b2s", [P, DK], F32)
            gam = hold("gam", [P, DK], F32)
            bet = hold("bet", [P, DK], F32)
            stage_norm(nc, x, src, dst, src_tail, dst_tail, eps, W1, b1, W2, b2, gamma, beta, table,
                       ident, epsc, nodes, src_all, dst_all, ctl, base, iota, W1s, W2s, b1s, b2s, gam, bet)
            stage_edges(nc, table, buf, ident, nodes, src_all, dst_all, ctl, base, iota, stats, W1s, W2s, b1s, b2s)
            stage_route(nc, x, gate_w, gate_b, buf, out, ident, epsc, nodes, stats, gam, bet)
        stage_experts(nc, buf, w1, xb1, w2, xb2, out, ident)


def stage_norm(nc, x, src, dst, src_tail, dst_tail, eps, W1, b1, W2, b2, gamma, beta, table,
               ident, epsc, nodes, src_all, dst_all, ctl, base, iota, W1s, W2s, b1s, b2s, gam, bet):
    with ExitStack() as ctx:
        def sb(name, shape, dt):
            return ctx.enter_context(nc.sbuf_tensor(name, shape, dt))

        def sem(name):
            return ctx.enter_context(nc.semaphore(name))

        xin = sb("n_xin", [P, R5, QT, D], F32)
        pair = sb("n_pair", [P, R5, QT, 2 * D], F16)
        st = sb("n_st", [P, R5, QT, 6], F32)
        mv = sb("n_mv", [P, R5, QT, 2], F32)
        sd = sb("n_sd", [P, R5, QT], F32)
        off = sb("n_off", [P, R5, QT], F32)
        epsl = sb("n_epsl", [P, 1], F32)
        rsl = sb("n_rsl", [P, R5, QT], F32)
        selfs = sb("n_selfs", [P, 1], F32)
        epsb = sb("n_epsb", [P, 1], F32)
        dsti = sb("n_dsti", [P, EP], I32)
        ext = sb("n_ext", [P, 2, NG], F32)
        low_of = sb("n_low_of", [P, NG], F32)
        allx = sb("n_allx", [P, 2, NG], F32)
        blki = sb("n_blki", [P, 2, NG], I32)
        blks = sb("n_blks", [P, 2, NG], I32)
        sfx = sb("n_sfx", [P, 2, NG + 128], F32)
        sfi = sb("n_sfi", [P, NG], I32)
        sfs = sb("n_sfs", [P, NG], I32)
        packed = sb("n_packed", [P, 2, NG], F32)

        s_x = [sem(f"n_x{j}") for j in range(R5)]
        s_tab = [sem(f"n_tab{j}") for j in range(R5)]
        s_pad, s_src, s_dst, s_w, s_eps = sem("n_pad"), sem("n_src"), sem("n_dst"), sem("n_w"), sem("n_eps_in")
        s_self, s_epsc, s_const, s_id = sem("n_self"), sem("n_epsc"), sem("n_const"), sem("n_id")
        s_stat, s_var, s_std, s_rst, s_xn = sem("n_stat"), sem("n_var"), sem("n_std"), sem("n_rst"), sem("n_xn")
        s_hi, s_term, s_lo = sem("n_hi"), sem("n_term"), sem("n_lo")
        s_ext, s_all, s_rng = sem("n_ext_s"), sem("n_all"), sem("n_rng")

        with nc.Block() as block:
            @block.sync
            def _(sp):
                def load(q, j, rnd):
                    if not (isinstance(rnd, int) and rnd == 0):
                        sp.wait_ge(s_lo, q - R5 + 1)
                        sp.wait_ge(s_term, q - R5 + 1)
                    if isinstance(q, int) and q == NQ - 1:
                        sp.dma_start(xin[:, j, 0, :], x[q * QN:q * QN + P, :]).then_inc(s_x[j], 16)
                        sp.dma_start(xin[0:N - q * QN - P, j, 1, :], x[q * QN + P:N, :]).then_inc(s_x[j], 16)
                    else:
                        sp.dma_start(xin[:, j, :, :],
                                     x[at(q, QN), :].rearrange("(t p) d -> p t d", p=P)).then_inc(s_x[j], 16)

                def store(q, j, rnd):
                    sp.wait_ge(s_lo, q + 1)
                    sp.dma_start(table[at(q, QN), :].rearrange("(t p) d -> p t d", p=P),
                                 pair[:, j, :, :]).then_inc(s_tab[j], 16)

                sp.dma_start(epsb[:, :], eps.unsqueeze(0).broadcast_to((P, 1))).then_inc(s_eps, 16)
                for q in range(2):
                    load(q, q, 0)
                sp.wait_ge(s_pad, 2)
                sp.dma_start(dsti[:, 0:EFULL], dst).then_inc(s_dst, 16)
                sp.dma_start(dsti[0:ETAIL, EFULL:EFULL + 1], dst_tail).then_inc(s_dst, 16)
                for q in range(2, R5):
                    load(q, q, 0)
                sp.dma_start(src_all[:, 0:EFULL], src).then_inc(s_src, 16)
                sp.dma_start(src_all[0:ETAIL, EFULL:EFULL + 1], src_tail).then_inc(s_src, 16)
                with sp.Fori(1, NQ // R5 - 1) as it:
                    for j in range(R5):
                        store(it * R5 + j - R5, j, it - 1)
                        load(it * R5 + j, j, it)
                for q in range(NQ - R5, NQ):
                    store(q - R5, q % R5, q // R5 - 1)
                    load(q, q % R5, q // R5)
                for q in range(NQ - R5, NQ):
                    store(q, q % R5, q // R5)
                for j in range(R5):
                    sp.wait_ge(s_tab[j], 16 * (NQ // R5))
                sp.wait_ge(s_src, 32)

            @block.gpsimd
            def _(pool):
                nc.gpsimd.memset(src_all[:, EFULL:EP], 0).then_inc(s_pad, 1)
                nc.gpsimd.memset(ctl[:, NG:NG + 1], 0)
                nc.gpsimd.memset(dsti[:, EFULL:EP], PAD_DST).then_inc(s_pad, 1)
                nc.gpsimd.memset(epsl[:, :], EPS / X_SCALE**2).then_inc(s_epsc, 1)
                nc.gpsimd.memset(epsc[:, :], EPS).then_inc(s_const, 1)
                nc.gpsimd.memset(ident[:, :], 0.0).then_inc(s_id, 1)
                nc.gpsimd.iota(base[:, :], pattern=[[P, NB]], base=0, channel_multiplier=0,
                               allow_small_or_imprecise_dtypes=True).then_inc(s_const, 1)
                nc.gpsimd.iota(iota[:, :], pattern=[[1, P]], base=0, channel_multiplier=0,
                               allow_small_or_imprecise_dtypes=True).then_inc(s_const, 1)
                pool.wait_ge(s_id, 1)
                nc.gpsimd.affine_select(out=ident[:, :], in_=ident[:, :], compare_op=ALU.not_equal, fill=1.0,
                                        base=0, pattern=[[-1, P]], channel_multiplier=1).then_inc(s_id, 1)

                def term(q, j, rnd):
                    wait_count(pool, s_xn, q + 1, normed)
                    nc.gpsimd.tensor_tensor(nodes[:, at(q), :].rearrange("p a b -> p (a b)"),
                                            xin[:, j, :, :].rearrange("p t d -> p (t d)"),
                                            selfs[:, 0:1].broadcast_to((P, QT * D)), ALU.mult).then_inc(s_term, 1)

                def extremes(q, j, rnd):
                    if isinstance(q, int) and q == R5 - 1:
                        pool.wait_ge(s_ext, 3)
                        nc.gpsimd.partition_all_reduce(allx[:, :, :].rearrange("p a g -> p (a g)"),
                                                       ext[:, :, :].rearrange("p a g -> p (a g)"), P,
                                                       RMAX).then_inc(s_all, 1)

                normed = counter(pool, "n_normed", R5 + 1)
                pool.wait_ge(s_self, 1)
                walk(pool, [(term, 0), (extremes, 0)], NQ, R5)
                pool.wait_ge(s_id, 2)
                pool.wait_ge(s_const, 3)

            @block.scalar
            def _(act):
                act.dma_start(W1s[:, :, :], W1.rearrange("(k p) f -> p k f", p=P)).then_inc(s_w, 16)
                act.dma_start(W2s[:, :, :], W2.rearrange("(k p) f -> p k f", p=P)).then_inc(s_w, 16)
                with nc.allow_non_contiguous_dma(reason="small vectors"):
                    for tile, vector in ((b1s, b1), (b2s, b2), (gam, gamma), (bet, beta)):
                        act.dma_start(tile[:, :], vector.rearrange("(c p) -> p c", p=P)).then_inc(s_w, 16)

                def std(q, j, rnd):
                    act.wait_ge(s_var, q + 1)
                    nc.scalar.activation(sd[:, j, :], mv[:, j, :, 1], ACT.Sqrt, scale=1.0 / X_SCALE**2,
                                         bias=epsl[:, 0:1]).then_inc(s_std, 1)

                def parts(q, j, rnd):
                    act.wait_ge(s_rst, q * 2 + 2)
                    for t in range(QT):
                        ins = nc.scalar.activation(xin[:, j, t, :], xin[:, j, t, :], ACT.Identity,
                                                   bias=off[:, j, t:t + 1], scale=rsl[:, j, t:t + 1])
                    ins.then_inc(s_xn, 1)
                    if not (isinstance(rnd, int) and rnd == 0):
                        act.wait_ge(s_tab[j], rnd * 16)
                    act.wait_ge(s_xn, q + 1)
                    nc.scalar.activation(pair[:, j, :, 0:D], xin[:, j, :, :], ACT.Identity).then_inc(s_hi, 1)

                act.wait_ge(s_epsc, 1)
                walk(act, [(std, 0), (parts, 1)], NQ, R5)
                act.wait_ge(s_w, 96)

            @block.vector
            def _(dve):
                dve.wait_ge(s_eps, 16)
                nc.vector.tensor_scalar(selfs[:, :], epsb[:, :], 1.0, 1.0 / X_SCALE, ALU.add,
                                        ALU.mult).then_inc(s_self, 1)

                stat_seen = counter(dve, "n_stat_seen", R5 + 1)

                def stat(q, j, rnd):
                    if isinstance(q, int) and q == NQ - 1:
                        dve.wait_ge(s_x[j], 16 * rnd + 32)
                    else:
                        dve.wait_ge(s_x[j], rnd * 16 + 16)
                    for t in range(QT):
                        ins = nc.vector.bn_stats(st[:, j, t, :], xin[:, j, t, :])
                    ins.then_inc(s_stat, 1)
                    wait_count(dve, s_stat, q + 1, stat_seen)
                    for t in range(QT):
                        ins = nc.vector.bn_aggr(mv[:, j, t, :], st[:, j, t, :])
                    ins.then_inc(s_var, 1)

                def norm(q, j, rnd):
                    dve.wait_ge(s_std, q + 1)
                    nc.vector.reciprocal(rsl[:, j, :], sd[:, j, :]).then_inc(s_rst, 1)
                    dve.wait_ge(s_rst, q * 2 + 1)
                    nc.vector.scalar_tensor_tensor(out=off[:, j, :], in0=mv[:, j, :, 0], scalar=-1.0,
                                                   in1=rsl[:, j, :], op0=ALU.mult, op1=ALU.mult).then_inc(s_rst, 1)

                def low(q, j, rnd):
                    dve.wait_ge(s_hi, q + 1)
                    nc.vector.tensor_tensor(pair[:, j, :, D:2 * D], xin[:, j, :, :], pair[:, j, :, 0:D],
                                            ALU.subtract).then_inc(s_lo, 1)

                def ranges(q, j, rnd):
                    if not isinstance(q, int):
                        return
                    if q == 3:
                        dve.wait_ge(s_dst, 32)
                        nc.vector.tensor_copy(dst_all[:, :], dsti[:, :]).then_inc(s_rng, 1)
                        dve.wait_ge(s_rng, 1)
                        by_group = dst_all[:, :].rearrange("p (g t) -> p g t", t=GT)
                        nc.vector.tensor_reduce(low_of[:, :], by_group, AX.X, ALU.min).then_inc(s_ext, 1)
                        nc.vector.tensor_reduce(ext[:, 1, :], by_group, AX.X, ALU.max).then_inc(s_ext, 1)
                        dve.wait_ge(s_ext, 2)
                        nc.vector.tensor_scalar(ext[:, 0, :], low_of[:, :], -1.0, None, ALU.mult).then_inc(s_ext, 1)
                    if q == NQ - R5:
                        link = [1]

                        def then(ins):
                            link[0] += 1
                            ins.then_inc(s_rng, 1)
                            dve.wait_ge(s_rng, link[0])

                        dve.wait_ge(s_all, 1)
                        nc.vector.tensor_scalar(blki[:, 0, :], allx[:, 0, :], -1.0, None, ALU.mult).then_inc(s_rng, 1)
                        nc.vector.tensor_copy(blki[:, 1, :], allx[:, 1, :]).then_inc(s_rng, 1)
                        link[0] += 2
                        dve.wait_ge(s_rng, link[0])
                        then(nc.vector.tensor_scalar(blks[:, :, :], blki[:, :, :], 7, None, ALU.arith_shift_right))
                        then(nc.vector.memset(sfx[:, :, :], float(NB)))
                        then(nc.vector.tensor_copy(sfx[:, 0, 0:NG - 1], blks[:, 0, 1:NG]))
                        for k in range(8):
                            then(nc.vector.tensor_tensor(sfx[:, (k + 1) % 2, 0:NG], sfx[:, k % 2, 0:NG],
                                                         sfx[:, k % 2, 1 << k:(1 << k) + NG], ALU.min))
                        then(nc.vector.tensor_copy(sfi[:, :], sfx[:, 0, 0:NG]))
                        then(nc.vector.tensor_scalar(sfs[:, :], sfi[:, :], 2, None, ALU.arith_shift_right))
                        then(nc.vector.tensor_scalar(packed[:, 0, :], blks[:, 1, :], 128.0, 128.0, ALU.mult, ALU.add))
                        then(nc.vector.scalar_tensor_tensor(out=packed[:, 1, :], in0=sfs[:, :], scalar=16384.0,
                                                            in1=packed[:, 0, :], op0=ALU.mult, op1=ALU.add))
                        nc.vector.tensor_tensor(ctl[:, 0:NG], packed[:, 1, :], blks[:, 0, :], ALU.add)

                walk(dve, [(stat, 0), (norm, 1), (low, 2), (ranges, 0)], NQ, R5)


def stage_edges(nc, table, buf, ident, nodes, src_all, dst_all, ctl, base, iota, stats, W1s, W2s, b1s, b2s):
    with ExitStack() as ctx:
        def sb(name, shape, dt):
            return ctx.enter_context(nc.sbuf_tensor(name, shape, dt))

        def psum(name, shape, dt):
            return ctx.enter_context(nc.psum_tensor(name, shape, dt))

        def sem(name):
            return ctx.enter_context(nc.semaphore(name))

        HR = 4
        LAG = 2
        ZR = 8
        got = sb("e_got", [P, RG, GT, 2 * D], F16)
        idx = sb("e_idx", [P, RG, GT], I32)
        hot = sb("e_hot", [P, HR, GT, P], F16)
        hrow = sb("e_hrow", [P, QT, D], F32)
        hT = sb("e_hT", [P, DK, QN], F32)
        mid = sb("e_mid", [P, H1C, QN], F32)
        zero = sb("e_zero", [P, ZR * ROW], F32)
        sums = psum("e_sums", [P, HR, 2 * D], F32)
        turned = psum("e_turned", [P, DK, QN], F32)
        up = psum("e_up", [P, 2, QN], F32)

        s_flush = sem("e_flush")
        s_free, s_zero, s_zeroed = sem("e_free"), sem("e_zero_s"), sem("e_zeroed")
        s_idx = [sem(f"e_idx{h}") for h in range(2)]
        s_got = [sem(f"e_got{r}") for r in range(RG)]
        s_hot, s_sum, s_add = sem("e_hot_s"), sem("e_sum"), sem("e_add")
        s_hrow, s_turn, s_hT, s_up, s_mid, s_down, s_h2 = (
            sem("e_hrow_s"), sem("e_turn"), sem("e_hT_s"), sem("e_up_s"), sem("e_mid_s"), sem("e_down_s"),
            sem("e_h2"))

        blocks_of = nodes[:, :, :].rearrange("p q (t d) -> p (q t) d", d=D)

        with nc.Block() as block:
            @block.sync
            def _(sp):
                ZERO = NX * SLOTS // (P * ZR)

                def indices(n, h):
                    sp.dma_start(idx[:, 2 * h:2 * h + 2, :],
                                 src_all[:, at(n * 2 + h, 2 * GT)]).then_inc(s_idx[h], 16)

                def next_indices(it):
                    for h in range(2):
                        for r in range(2 * h, 2 * h + 2):
                            sp.wait_ge(s_got[r], it * (16 * GT) + 16 * GT)
                        indices(it + 1, h)

                for h in range(2):
                    indices(0, h)
                sp.wait_ge(s_zero, 1)
                with sp.Fori(0, ZERO) as it:
                    next_indices(it)
                    sp.dma_start(buf[at(it, P * ZR), :].rearrange("(p r) d -> p (r d)", p=P),
                                 zero[:, :]).then_inc(s_zeroed, 16)
                with sp.Fori(ZERO, NG // RG - 1) as it:
                    next_indices(it)
                sp.wait_ge(s_zeroed, 16 * ZERO)

            @block.gpsimd
            def _(pool):
                free = counter(pool, "free", 1)
                have = [counter(pool, f"have{h}", 16) for h in range(2)]
                nc.gpsimd.memset(zero[:, :], 0.0).then_inc(s_zero, 1)
                with pool.Fori(0, NG // RG):
                    for r in range(RG):
                        if r % 2 == 0:
                            pool.wait_ge(s_idx[r // 2], have[r // 2])
                            pool.reg_add(have[r // 2], have[r // 2], 16)
                        pool.wait_ge(s_free, free)
                        pool.reg_add(free, free, 1)
                        for t in range(GT):
                            pool.indirect_dma_start(
                                got[:, r, t, :], None, table,
                                bass.IndirectOffsetOnAxis(ap=idx[:, r, t:t + 1], axis=0)).then_inc(s_got[r], 16)

            @block.tensor
            def _(pe):
                turn = pe.alloc_register("turn")
                done = pe.alloc_register("done")
                pe.reg_mov(turn, 1)
                made = pe.alloc_register("made")
                pe.reg_mov(done, 0)
                pe.reg_mov(made, 0)
                pe.sem_inc(s_free, RG)

                pe.sem_inc(s_turn, 1)

                def transposes(q):
                    pe.wait_ge(s_hrow, q + 1)
                    for k in range(DK):
                        for t in range(QT):
                            ins = nc.tensor.transpose(turned[:, k, t * P:(t + 1) * P],
                                                      hrow[:, t, k * P:(k + 1) * P], ident[:, :])
                    ins.then_inc(s_turn, 1)

                def products(q):
                    pe.wait_ge(s_hT, q + 1)
                    for c in range(H1C):
                        if c >= 2:
                            pe.wait_ge(s_mid, q * H1C + c - 1)
                        for k in range(DK):
                            ins = nc.tensor.matmul(up[:, c % 2, :], W1s[:, k, c * P:(c + 1) * P], hT[:, k, :],
                                                   start=(k == 0), stop=(k == DK - 1))
                        ins.then_inc(s_up, 1)
                    pe.wait_ge(s_mid, q * H1C + H1C)
                    for c in range(DK):
                        for k in range(H1C):
                            ins = nc.tensor.matmul(up[:, c, :], W2s[:, k, c * P:(c + 1) * P], mid[:, k, :],
                                                   start=(k == 0), stop=(k == H1C - 1))
                    ins.then_inc(s_down, 1)

                def quad(number):
                    return nc.s_assert_within(number, 0, NQ - 1,
                                              skip_runtime_bounds_check_because="stage_norm packs it")

                first, end, whole = (pe.alloc_register(n) for n in ("first", "end", "whole"))

                def load_word(number):
                    return pe.value_load(ctl[0:1, number], min_val=0, max_val=1 << 20)

                def unpack(word):
                    pe.reg_mov(first, pe.snap(word % 128))
                    pe.reg_mov(end, pe.snap((word // 128) % 128))
                    pe.reg_mov(whole, pe.snap(word // 16384))

                unpack(load_word(at(0)))
                with pe.Fori(0, NG // RG) as it:
                    for r in range(RG):
                        with pe.Fori(first, end):
                            place = pe.snap(turn) % HR
                            pe.wait_ge(s_got[r], it * (16 * GT) + 16 * GT)
                            pe.wait_ge(s_hot, turn)
                            pe.wait_ge(s_add, turn)
                            pe.reg_add(turn, turn, 1)
                            for t in range(GT):
                                for part in range(2):
                                    ins = nc.tensor.matmul(sums[:, place, 0:D], hot[:, place, t, :],
                                                           got[:, r, t, part * D:(part + 1) * D],
                                                           start=(t == 0 and part == 0),
                                                           stop=(t == GT - 1 and part == 1))
                            ins.then_inc(s_sum, 1)
                        word = load_word(at(it * RG + (r + 1)))
                        pe.wait_ge(s_sum, pe.snap(pe.snap(turn) + 1))
                        pe.sem_inc(s_free, 1)
                        with pe.If(pe.snap(done) < pe.snap(whole)):
                            with pe.Fori(done, whole) as number:
                                with pe.If(number > 0):
                                    products(quad(pe.snap(made)))
                                    pe.reg_add(made, made, 1)
                                transposes(quad(number))
                        pe.reg_mov(done, whole)
                        unpack(word)
                products(NQ - 1)

            @block.scalar
            def _(act):
                def mlp(q):
                    act.wait_ge(s_turn, q + 2)
                    nc.scalar.activation(hT[:, :, :], turned[:, :, :], ACT.Identity).then_inc(s_hT, 1)
                    for c in range(H1C):
                        act.wait_ge(s_up, q * H1C + c + 1)
                        nc.scalar.activation(mid[:, c, :], up[:, c % 2, :], ACT.Relu,
                                             bias=b1s[:, c:c + 1]).then_inc(s_mid, 1)
                    act.wait_ge(s_down, q + 1)
                    for c in range(DK):
                        nc.scalar.activation(
                            nodes[:, at(q), c * QN:(c + 1) * QN].rearrange("p a b -> p (a b)"), up[:, c, :],
                            ACT.Identity, bias=b2s[:, c:c + 1]).then_inc(s_h2, 1)

                with act.Fori(0, NQ) as q:
                    mlp(q)

            @block.vector
            def _(dve):
                turn = dve.alloc_register("turn")
                done = dve.alloc_register("done")
                last = dve.alloc_register("last")
                older = dve.alloc_register("older")
                flushed = dve.alloc_register("flushed")
                dve.reg_mov(turn, 1)
                dve.reg_mov(done, 0)
                measured = dve.alloc_register("measured")
                dve.reg_mov(last, 0)
                dve.reg_mov(older, 0)
                dve.reg_mov(measured, 0)
                dve.reg_mov(flushed, 1)
                nc.vector.memset(sums[:, :, 0:D], 0.0).then_inc(s_sum, LAG)
                dve.wait_ge(s_sum, LAG)
                dve.sem_inc(s_add, 1)

                def place_of(back):
                    return dve.snap(dve.snap(turn) + (HR - back)) % HR

                def add_sums(back, b):
                    place = dve.snap(place_of(back))
                    row = blocks_of[:, b, :].rearrange("p a d -> p (a d)")
                    return nc.vector.scalar_tensor_tensor(out=row, in0=sums[:, place, 0:D], scalar=1.0 / X_SCALE,
                                                          in1=row, op0=ALU.mult, op1=ALU.add)

                def batch_stats(q, width=QN):
                    dve.wait_ge(s_h2, q * DK + DK)
                    for c in range(DK):
                        nc.vector.bn_stats(stats[:, c, at(q, 6)], nodes[:, at(q), c * QN:c * QN + width].rearrange(
                            "p a b -> p (a b)"))

                def quad(number):
                    return nc.s_assert_within(number, 0, NQ - 1,
                                              skip_runtime_bounds_check_because="stage_norm packs it")

                def block_no(register):
                    return at(nc.s_assert_within(dve.snap(register), 0, NB - 1,
                                                 skip_runtime_bounds_check_because="stage_norm packs it"))

                with dve.Fori(0, NG // RG) as it:
                    for r in range(RG):
                        word = dve.value_load(ctl[0:1, at(it * RG + r)], min_val=0, max_val=1 << 20)
                        first = dve.snap(word % 128)
                        end = dve.snap((word // 128) % 128)
                        whole = dve.snap(word // 16384)
                        with dve.Fori(first, end) as number:
                            place = dve.snap(place_of(0))
                            b, before = block_no(number), block_no(older)
                            nc.vector.scalar_tensor_tensor(
                                out=hot[:, place, :, :],
                                in0=dst_all[:, at(it * RG + r, GT)].unsqueeze(2).broadcast_to((P, GT, P)),
                                scalar=base[:, b], in1=iota[:, :].unsqueeze(1).broadcast_to((P, GT, P)),
                                op0=ALU.subtract, op1=ALU.is_equal).then_inc(s_hot, 1)
                            dve.wait_ge(s_sum, turn)
                            dve.wait_ge(s_add, turn)
                            add_sums(LAG, before).then_inc(s_add, 1)
                            dve.reg_mov(older, last)
                            dve.reg_mov(last, number)
                            dve.reg_add(turn, turn, 1)
                        with dve.If(dve.snap(done) < whole):
                            before, newest = block_no(older), block_no(last)
                            dve.wait_ge(s_sum, dve.snap(dve.snap(turn) + 1))
                            dve.wait_ge(s_add, turn)

                            def then(ins):
                                ins.then_inc(s_flush, 1)
                                dve.wait_ge(s_flush, flushed)
                                dve.reg_add(flushed, flushed, 1)

                            then(add_sums(2, before))
                            then(add_sums(1, newest))
                            nc.vector.memset(sums[:, :, 0:D], 0.0).then_inc(s_flush, 1)
                            open_block = dve.snap(whole * QT)
                            dve.reg_mov(last, open_block)
                            dve.reg_mov(older, open_block)
                            with dve.Fori(done, whole) as number:
                                q = quad(number)
                                dve.wait_ge(s_turn, q + 1)
                                nc.vector.tensor_scalar(hrow[:, :, :].rearrange("p t d -> p (t d)"),
                                                        nodes[:, at(q), :].rearrange("p a b -> p (a b)"),
                                                        1.0, None, ALU.mult).then_inc(s_hrow, 1)
                                with dve.If(number > 1):
                                    batch_stats(quad(dve.snap(measured)))
                                    dve.reg_add(measured, measured, 1)
                            dve.wait_ge(s_flush, flushed)
                            dve.reg_add(flushed, flushed, 1)
                        dve.reg_mov(done, whole)
                batch_stats(NQ - 2)
                batch_stats(NQ - 1, N - (NQ - 1) * QN)


def stage_route(nc, x, gate_w, gate_b, buf, out, ident, epsc, nodes, stats, gam, bet):
    with ExitStack() as ctx:
        def sb(name, shape, dt):
            return ctx.enter_context(nc.sbuf_tensor(name, shape, dt))

        def psum(name, shape, dt):
            return ctx.enter_context(nc.psum_tensor(name, shape, dt))

        def sem(name):
            return ctx.enter_context(nc.semaphore(name))

        bnv = sb("r_bnv", [P, DK, 2], F32)
        bns = sb("r_bns", [P, DK], F32)
        bnr = sb("r_bnr", [P, DK], F32)
        scale = sb("r_scale", [P, DK], F32)
        ms = sb("r_ms", [P, DK], F32)
        shift = sb("r_shift", [P, DK], F32)
        gw = sb("r_gw", [P, DK, NX], F32)
        gb = sb("r_gb", [P, NX], F32)
        gwh = sb("r_gwh", [P, DK, NX], F16)
        gwl = sb("r_gwl", [P, DK, NX], F16)
        ones = sb("r_ones", [P, P], F16)
        tri = sb("r_tri", [P, P], F16)
        rev = sb("r_rev", [P, NX], F32)
        node1 = sb("r_node1", [P, NB], F32)
        xin = sb("r_xin", [P, R5, QT, D], F32)
        row = sb("r_row", [P, R5, QT, ROW], F32)
        hbn = sb("r_hbn", [P, DK, QN], F32)
        xn = sb("r_xn", [P, QT, D], F32)
        xTh = sb("r_xTh", [P, DK, QN], F16)
        xTl = sb("r_xTl", [P, DK, QN], F16)
        st = sb("r_st", [P, R5, QT, 6], F32)
        mv = sb("r_mv", [P, R5, QT, 2], F32)
        sd = sb("r_sd", [P, R5, QT], F32)
        lg = sb("r_lg", [P, QT, NX], F32)
        mx = sb("r_mx", [P, QT], F32)
        cand = sb("r_cand", [P, QT, NX], F32)
        best = sb("r_best", [P, QT], F32)
        hot = sb("r_hot", [P, QT, NX], F16)
        more = sb("r_more", [P, NX], F32)
        seen = sb("r_seen", [P, R5, NX], F16)
        mine = sb("r_mine", [P, QT, NX], F32)
        pos = sb("r_pos", [P, QT], F32)
        slot = sb("r_slot", [P, QT], F32)
        over = sb("r_over", [P, QT], F32)
        slot2 = sb("r_slot2", [P, QT], F32)
        pad = sb("r_pad", [P, NB], F32)
        offset = sb("r_offset", [P, NB], F32)
        slots = sb("r_slots", [P, R5, QT], I32)
        turned = psum("r_turned", [P, QT, D], F32)
        back = psum("r_back", [P, DK, QN], F32)
        logit = psum("r_logit", [P, QT, NX], F32)
        count = psum("r_count", [P, QT, NX], F32)

        s_gw, s_const, s_tri, s_rows, s_bn = sem("r_gw_s"), sem("r_const"), sem("r_tri_s"), sem("r_rows"), sem("r_bn")
        s_bnsd, s_gwh, s_gwl, s_xlo, s_ones, s_offset = (
            sem("r_bnsd"), sem("r_gwh_s"), sem("r_gwl_s"), sem("r_xlo"), sem("r_ones_s"), sem("r_offset_s"))
        s_x = [sem(f"r_x{j}") for j in range(R5)]
        s_out = [sem(f"r_out{j}") for j in range(R5)]
        s_scat = [sem(f"r_scat{j}") for j in range(R5)]
        s_hbn, s_turn, s_x2, s_var, s_std, s_rstd, s_xn, s_back, s_xT, s_logit = (
            sem("r_hbn_s"), sem("r_turn"), sem("r_x2_s"), sem("r_var"), sem("r_std"), sem("r_rstd"), sem("r_xn_s"),
            sem("r_back_s"), sem("r_xT_s"), sem("r_logit_s"))
        s_stat, s_hotv, s_hot, s_count, s_slotv, s_slot, s_node = (
            sem("r_stat"), sem("r_hotv"), sem("r_hot_s"), sem("r_count_s"), sem("r_slotv"), sem("r_slot_s"),
            sem("r_node_s"))

        with nc.Block() as block:
            @block.sync
            def _(sp):
                sp.dma_start(gw[:, :, :], gate_w.rearrange("(k p) e -> p k e", p=P)).then_inc(s_gw, 16)
                sp.dma_start(gb[:, :], gate_b.unsqueeze(0).broadcast_to((P, NX))).then_inc(s_gw, 16)

                def load(q, j, rnd):
                    if not (isinstance(rnd, int) and rnd == 0):
                        sp.wait_ge(s_x2, q - R5 + 1)
                    if isinstance(q, int) and q == NQ - 1:
                        sp.dma_start(xin[:, j, 0, :], x[q * QN:q * QN + P, :]).then_inc(s_x[j], 16)
                        sp.dma_start(xin[0:N - q * QN - P, j, 1, :], x[q * QN + P:N, :]).then_inc(s_x[j], 16)
                    else:
                        sp.dma_start(xin[:, j, :, :],
                                     x[at(q, QN), :].rearrange("(t p) d -> p t d", p=P)).then_inc(s_x[j], 16)

                def store(q, j, rnd):
                    sp.wait_ge(s_x2, q + 1)
                    if isinstance(q, int) and q == NQ - 1:
                        sp.dma_start(out[q * QN:q * QN + P, :], row[:, j, 0, 0:D]).then_inc(s_out[j], 16)
                        sp.dma_start(out[q * QN + P:N, :], row[0:N - q * QN - P, j, 1, 0:D]).then_inc(s_out[j], 16)
                    else:
                        sp.dma_start(out[at(q, QN), :].rearrange("(t p) d -> p t d", p=P),
                                     row[:, j, :, 0:D]).then_inc(s_out[j], 16)

                walk(sp, [(load, 0), (store, 3)], NQ, R5)
                for j in range(R5):
                    sp.wait_ge(s_out[j], 16 * (NQ // R5) + (16 if j == (NQ - 1) % R5 else 0))

            @block.gpsimd
            def _(pool):
                ready = counter(pool, "r_ready", R5 + 1)
                nc.gpsimd.memset(row[:, :, :, D + 3:D + 4], 0.0).then_inc(s_rows, 1)
                nc.gpsimd.memset(seen[:, :, :], 0.0).then_inc(s_const, 1)
                nc.gpsimd.iota(rev[:, :], pattern=[[-1, NX]], base=NX, channel_multiplier=0,
                               allow_small_or_imprecise_dtypes=True).then_inc(s_const, 1)
                nc.gpsimd.iota(node1[:, :], pattern=[[P, NB]], base=1, channel_multiplier=1,
                               allow_small_or_imprecise_dtypes=True).then_inc(s_const, 1)
                nc.gpsimd.memset(ones[:, :], 1.0).then_inc(s_ones, 1)
                pool.wait_ge(s_ones, 1)
                nc.gpsimd.affine_select(out=tri[:, :], in_=ones[:, :], compare_op=ALU.is_ge, fill=0.0,
                                        base=0, pattern=[[1, P]], channel_multiplier=-1).then_inc(s_tri, 1)
                bound = pool.to_reg(NX * SLOTS - 1)

                def scatter(q, j, rnd):
                    wait_count(pool, s_slot, q + 1, ready)
                    for t in range(QT):
                        pool.indirect_dma_start(
                            buf, bass.IndirectOffsetOnAxis(ap=slots[:, j, t:t + 1], axis=0), row[:, j, t, :], None,
                            bounds_check=bound, oob_is_err=False).then_inc(s_scat[j], 16)

                pool.wait_ge(s_rows, 1)
                walk(pool, [(scatter, 0)], NQ, R5)
                for j in range(R5):
                    pool.wait_ge(s_scat[j], 16 * QT * (NQ // R5))

            @block.tensor
            def _(pe):
                def turn(q, j, rnd):
                    pe.wait_ge(s_hbn, q + 1)
                    if not (isinstance(q, int) and q == 0):
                        pe.wait_ge(s_x2, q)
                    for t in range(QT):
                        for k in range(DK):
                            ins = nc.tensor.transpose(turned[:, t, k * P:(k + 1) * P],
                                                      hbn[:, k, t * P:(t + 1) * P], ident[:, :])
                    ins.then_inc(s_turn, 1)

                def turn_back(q, j, rnd):
                    pe.wait_ge(s_xn, q + 1)
                    if not (isinstance(q, int) and q == 0):
                        pe.wait_ge(s_xlo, q)
                    for k in range(DK):
                        for t in range(QT):
                            ins = nc.tensor.transpose(back[:, k, t * P:(t + 1) * P],
                                                      xn[:, t, k * P:(k + 1) * P], ident[:, :])
                    ins.then_inc(s_back, 1)

                def gate(q, j, rnd):
                    pe.wait_ge(s_xlo, q + 1)
                    if not (isinstance(q, int) and q == 0):
                        pe.wait_ge(s_hot, q)
                    for t in range(QT):
                        passes = [(x, w, k) for k in range(DK) for x, w in ((xTh, gwh), (xTh, gwl), (xTl, gwh))]
                        for n, (x, w, k) in enumerate(passes):
                            ins = nc.tensor.matmul(logit[:, t, :], x[:, k, t * P:(t + 1) * P], w[:, k, :],
                                                   start=(n == 0), stop=(n == len(passes) - 1))
                    ins.then_inc(s_logit, 1)

                def counts(q, j, rnd):
                    pe.wait_ge(s_hot, q + 1)
                    if not (isinstance(q, int) and q == 0):
                        pe.wait_ge(s_slot, q)
                    nc.tensor.matmul(count[:, :, :], tri[:, :], hot[:, :, :], start=True, stop=False)
                    nc.tensor.matmul(count[:, :, :], ones[:, :], seen[:, j, :].unsqueeze(1).broadcast_to((P, QT, NX)),
                                     start=False, stop=False)
                    for t in range(QT - 1):
                        ins = nc.tensor.matmul(count[:, t + 1:QT, :], ones[:, :],
                                               hot[:, t, :].unsqueeze(1).broadcast_to((P, QT - 1 - t, NX)),
                                               start=False, stop=(t == QT - 2))
                    ins.then_inc(s_count, 1)

                pe.wait_ge(s_gwl, 1)
                pe.wait_ge(s_tri, 1)
                walk(pe, [(turn, 1), (counts, 4), (gate, 3), (turn_back, 2)], NQ, R5)

            @block.scalar
            def _(act):
                act.wait_ge(s_bn, 1)
                nc.scalar.activation(bns[:, :], bnv[:, :, 1], ACT.Sqrt, bias=epsc[:, 0:1]).then_inc(s_bnsd, 1)
                act.wait_ge(s_gw, 32)
                nc.scalar.activation(gwh[:, :, :], gw[:, :, :], ACT.Identity, scale=W_SCALE).then_inc(s_gwh, 1)
                act.wait_ge(s_bn, 2)

                def norm(q, j, rnd):
                    if not (isinstance(q, int) and q == 0):
                        act.wait_ge(s_turn, q)
                    for k in range(DK):
                        ins = nc.scalar.activation(
                            hbn[:, k, :], nodes[:, at(q), k * QN:(k + 1) * QN].rearrange("p a b -> p (a b)"),
                            ACT.Identity, bias=shift[:, k:k + 1], scale=scale[:, k:k + 1])
                    ins.then_inc(s_hbn, 1)

                def rows(q, j, rnd):
                    act.wait_ge(s_rstd, q * 2 + 2)
                    if not (isinstance(q, int) and q == 0):
                        act.wait_ge(s_back, q)
                    for t in range(QT):
                        ins = nc.scalar.activation(xn[:, t, :], row[:, j, t, 0:D], ACT.Identity,
                                                   bias=row[:, j, t, D + 1:D + 2], scale=row[:, j, t, D:D + 1])
                    ins.then_inc(s_xn, 1)

                def std(q, j, rnd):
                    act.wait_ge(s_var, q + 1)
                    nc.scalar.activation(sd[:, j, :], mv[:, j, :, 1], ACT.Sqrt, bias=epsc[:, 0:1]).then_inc(s_std, 1)

                def columns(q, j, rnd):
                    act.wait_ge(s_back, q + 1)
                    if not (isinstance(q, int) and q == 0):
                        act.wait_ge(s_logit, q)
                    nc.scalar.activation(xTh[:, :, :], back[:, :, :], ACT.Identity, scale=X_SCALE).then_inc(s_xT, 1)

                walk(act, [(columns, 3), (rows, 2), (norm, 0), (std, 1)], NQ, R5)

            @block.vector
            def _(dve):
                for k in range(DK):
                    ins = nc.vector.bn_aggr(bnv[:, k, :], stats[:, k, :])
                ins.then_inc(s_bn, 1)
                dve.wait_ge(s_bnsd, 1)
                nc.vector.reciprocal(bnr[:, :], bns[:, :]).then_inc(s_node, 1)
                dve.wait_ge(s_node, 1)
                nc.vector.tensor_tensor(scale[:, :], bnr[:, :], gam[:, :], ALU.mult).then_inc(s_node, 1)
                dve.wait_ge(s_node, 2)
                nc.vector.tensor_tensor(ms[:, :], bnv[:, :, 0], scale[:, :], ALU.mult).then_inc(s_node, 1)
                dve.wait_ge(s_node, 3)
                nc.vector.tensor_tensor(shift[:, :], bet[:, :], ms[:, :], ALU.subtract).then_inc(s_bn, 1)
                dve.wait_ge(s_gwh, 1)
                nc.vector.scalar_tensor_tensor(out=gwl[:, :, :], in0=gw[:, :, :], scalar=W_SCALE, in1=gwh[:, :, :],
                                               op0=ALU.mult, op1=ALU.subtract).then_inc(s_gwl, 1)
                dve.wait_ge(s_gw, 32)
                dve.wait_ge(s_const, 3)
                nc.vector.tensor_scalar(pad[:, :], node1[:, :], float(N), SKIP, ALU.is_gt,
                                        ALU.mult).then_inc(s_offset, 1)
                dve.wait_ge(s_offset, 1)
                nc.vector.tensor_scalar(offset[:, :], pad[:, :], float(NX * SLOTS - 1), None,
                                        ALU.add).then_inc(s_offset, 1)
                dve.wait_ge(s_offset, 2)
                dve.wait_ge(s_rows, 1)

                stat_seen = counter(dve, "r_stat_seen", R5)

                def add(q, j, rnd):
                    dve.wait_ge(s_turn, q + 1)
                    if isinstance(q, int) and q == NQ - 1:
                        dve.wait_ge(s_x[j], 16 * rnd + 32)
                    else:
                        dve.wait_ge(s_x[j], rnd * 16 + 16)
                    if not (isinstance(rnd, int) and rnd == 0):
                        dve.wait_ge(s_out[j], rnd * 16)
                        dve.wait_ge(s_scat[j], rnd * (16 * QT))
                    nc.vector.tensor_tensor(row[:, j, :, 0:D], turned[:, :, :], xin[:, j, :, :],
                                            ALU.add).then_inc(s_x2, 1)
                    dve.wait_ge(s_x2, q + 1)
                    for t in range(QT):
                        ins = nc.vector.bn_stats(st[:, j, t, :], row[:, j, t, 0:D])
                    ins.then_inc(s_stat, 1)
                    wait_count(dve, s_stat, q + 1, stat_seen)
                    for t in range(QT):
                        ins = nc.vector.bn_aggr(mv[:, j, t, :], st[:, j, t, :])
                    ins.then_inc(s_var, 1)

                def low_columns(q, j, rnd):
                    dve.wait_ge(s_xT, q + 1)
                    nc.vector.scalar_tensor_tensor(out=xTl[:, :, :], in0=back[:, :, :], scalar=X_SCALE,
                                                   in1=xTh[:, :, :], op0=ALU.mult, op1=ALU.subtract
                                                   ).then_inc(s_xlo, 1)

                def norm(q, j, rnd):
                    dve.wait_ge(s_std, q + 1)
                    nc.vector.reciprocal(row[:, j, :, D], sd[:, j, :]).then_inc(s_rstd, 1)
                    dve.wait_ge(s_rstd, q * 2 + 1)
                    nc.vector.scalar_tensor_tensor(out=row[:, j, :, D + 1], in0=mv[:, j, :, 0], scalar=-1.0,
                                                   in1=row[:, j, :, D], op0=ALU.mult, op1=ALU.mult
                                                   ).then_inc(s_rstd, 1)

                PICK, PLACE = 7, 6

                def picked(q, k, ins=None):
                    if ins is None:
                        dve.wait_ge(s_hotv, q * PICK + k)
                    else:
                        ins.then_inc(s_hotv, 1)

                def placed(q, k, ins=None):
                    if ins is None:
                        dve.wait_ge(s_slotv, q * PLACE + k)
                    else:
                        ins.then_inc(s_slotv, 1)

                def route(q, j, rnd):
                    before = not (isinstance(q, int) and q == 0)
                    p, i = q - 1, (j - 1) % R5
                    dve.wait_ge(s_logit, q + 1)
                    picked(q, 1, nc.vector.scalar_tensor_tensor(
                        out=lg[:, :, :], in0=logit[:, :, :], scalar=1.0 / (X_SCALE * W_SCALE),
                        in1=gb[:, :].unsqueeze(1).broadcast_to((P, QT, NX)), op0=ALU.mult, op1=ALU.add))
                    if before:
                        dve.wait_ge(s_count, q)
                        dve.wait_ge(s_hot, q)
                        placed(p, 1, nc.vector.tensor_tensor(mine[:, :, :], count[:, :, :], hot[:, :, :], ALU.mult))
                    picked(q, 1)
                    picked(q, 2, nc.vector.tensor_reduce(mx[:, :], lg[:, :, :], AX.X, ALU.max))
                    if before:
                        placed(p, 1)
                        placed(p, 2, nc.vector.tensor_reduce(pos[:, :], mine[:, :, :], AX.X, ALU.add))
                    picked(q, 2)
                    picked(q, 3, nc.vector.tensor_tensor(row[:, j, :, D + 4:ROW], lg[:, :, :],
                                                         mx[:, :].unsqueeze(2).broadcast_to((P, QT, NX)), ALU.subtract))
                    if before:
                        placed(p, 2)
                        placed(p, 3, nc.vector.scalar_tensor_tensor(out=slot[:, :], in0=best[:, :], scalar=-float(SLOTS),
                                                                    in1=pos[:, :], op0=ALU.mult, op1=ALU.add))
                    picked(q, 3)
                    picked(q, 4, nc.vector.scalar_tensor_tensor(
                        out=cand[:, :, :], in0=row[:, j, :, D + 4:ROW], scalar=0.0,
                        in1=rev[:, :].unsqueeze(1).broadcast_to((P, QT, NX)), op0=ALU.is_ge, op1=ALU.mult))
                    if before:
                        placed(p, 4, nc.vector.tensor_scalar(over[:, :], pos[:, :], float(CAP), SKIP, ALU.is_gt, ALU.mult))
                        placed(p, 3)
                    picked(q, 4)
                    picked(q, 5, nc.vector.tensor_reduce(best[:, :], cand[:, :, :], AX.X, ALU.max))
                    if before:
                        placed(p, 4)
                        placed(p, 5, nc.vector.tensor_tensor(slot2[:, :], slot[:, :], over[:, :], ALU.add))
                    picked(q, 5)
                    picked(q, 6, nc.vector.tensor_tensor(hot[:, :, :], rev[:, :].unsqueeze(1).broadcast_to((P, QT, NX)),
                                                         best[:, :].unsqueeze(2).broadcast_to((P, QT, NX)),
                                                         ALU.is_equal))
                    if before:
                        placed(p, 6, nc.vector.tensor_scalar(row[:, i, :, D + 2], node1[:, at(p, QT)], 1.0, None, ALU.mult))
                        placed(p, 6)
                        nc.vector.tensor_tensor(slots[:, i, :], slot2[:, :], offset[:, at(p, QT)],
                                                ALU.add).then_inc(s_slot, 1)
                    picked(q, 6)
                    picked(q, 7, nc.vector.tensor_reduce(more[:, :], hot[:, :, :].rearrange("p t e -> p e t"), AX.X, ALU.add))
                    picked(q, 7)
                    nc.vector.tensor_tensor(seen[:, (j + 1) % R5, :], seen[:, j, :], more[:, :],
                                            ALU.add).then_inc(s_hot, 1)

                def last_slots(p, i):
                    dve.wait_ge(s_count, p + 1)
                    dve.wait_ge(s_hot, p + 1)
                    placed(p, 1, nc.vector.tensor_tensor(mine[:, :, :], count[:, :, :], hot[:, :, :], ALU.mult))
                    placed(p, 1)
                    placed(p, 2, nc.vector.tensor_reduce(pos[:, :], mine[:, :, :], AX.X, ALU.add))
                    placed(p, 2)
                    placed(p, 3, nc.vector.scalar_tensor_tensor(out=slot[:, :], in0=best[:, :], scalar=-float(SLOTS),
                                                                in1=pos[:, :], op0=ALU.mult, op1=ALU.add))
                    placed(p, 4, nc.vector.tensor_scalar(over[:, :], pos[:, :], float(CAP), SKIP, ALU.is_gt, ALU.mult))
                    placed(p, 4)
                    placed(p, 5, nc.vector.tensor_tensor(slot2[:, :], slot[:, :], over[:, :], ALU.add))
                    placed(p, 6, nc.vector.tensor_scalar(row[:, i, :, D + 2], node1[:, at(p, QT)], 1.0, None, ALU.mult))
                    placed(p, 6)
                    nc.vector.tensor_tensor(slots[:, i, :], slot2[:, :], offset[:, at(p, QT)],
                                            ALU.add).then_inc(s_slot, 1)

                walk(dve, [(low_columns, 3), (add, 1), (route, 3), (norm, 1)], NQ, R5)
                last_slots(NQ - 1, (NQ - 1) % R5)


def stage_experts(nc, buf, w1, xb1, w2, xb2, out, ident):
    with ExitStack() as ctx:
        def sb(name, shape, dt):
            return ctx.enter_context(nc.sbuf_tensor(name, shape, dt))

        def psum(name, shape, dt):
            return ctx.enter_context(nc.psum_tensor(name, shape, dt))

        def sem(name):
            return ctx.enter_context(nc.semaphore(name))

        NS = NX * SG
        R8 = 2 * SG
        RR = 4
        RW = R8
        MB = 4
        w1f = sb("x_w1f", [P, DK, F], F32)
        w2f = sb("x_w2f", [P, FC, D], F32)
        b1f = sb("x_b1f", [P, FC], F32)
        w1h = sb("x_w1h", [P, 2, DK, F], F16)
        w1l = sb("x_w1l", [P, 2, DK, F], F16)
        w2h = sb("x_w2h", [P, 2, FC, D], F16)
        w2l = sb("x_w2l", [P, 2, FC, D], F16)
        b1s = sb("x_b1s", [P, 2, FC], F32)
        b2s = sb("x_b2s", [P, 2, D], F32)
        row = sb("x_row", [P, RW, QT, ROW], F32)
        xn = sb("x_xn", [P, QT, D], F32)
        xTh = sb("x_xTh", [P, 2, DK, QN], F16)
        xTl = sb("x_xTl", [P, 2, DK, QN], F16)
        midf = sb("x_midf", [P, MB, QN], F32)
        midh = sb("x_midh", [P, 2, FC, QN], F16)
        midl = sb("x_midl", [P, 2, FC, QN], F16)
        ex = sb("x_ex", [P, QT, NX], F32)
        tot = sb("x_tot", [P, QT], F32)
        prob = sb("x_prob", [P, RW, QT], F32)
        gone = sb("x_gone", [P, QT], F32)
        nodei = sb("x_nodei", [P, RW, QT], I32)
        yb = sb("x_yb", [P, QT, D], F32)
        y = sb("x_y", [P, QT, D], F32)
        up1 = sb("x_up1", [P, QT, D], F32)
        dn1 = sb("x_dn1", [P, QT, D], F32)
        fine = sb("x_fine", [P, QT, D], I32)
        res = sb("x_res", [P, RR, QT, D], F32)
        first_row = sb("x_first_row", [1, NX, SG * QT], F32)
        taken = sb("x_taken", [1, NX, SG * QT], F32)
        tiles = sb("x_tiles", [1, NX // 2, 2], F32)
        words = sb("x_words", [1, NX // 2], I32)
        turned = psum("x_turned", [P, DK, QN], F32)
        up = psum("x_up", [P, MB, QN], F32)
        down = psum("x_down", [P, QT, D], F32)

        s_row = [sem(f"x_row{j}") for j in range(RW)]
        s_scat = [sem(f"x_scat{j}") for j in range(RW)]
        s_zero, s_first, s_tiles, s_w, s_whi, s_split = (
            sem("x_zero"), sem("x_first"), sem("x_tiles_s"), sem("x_w"), sem("x_whi"), sem("x_split"))
        s_xn, s_turn, s_xT, s_xlo, s_up, s_mid, s_mlo, s_down, s_exp, s_meta, s_yv, s_res = (
            sem("x_xn_s"), sem("x_turn"), sem("x_xT_s"), sem("x_xlo"), sem("x_up_s"), sem("x_mid_s"), sem("x_mlo"),
            sem("x_down_s"), sem("x_exp"), sem("x_meta"), sem("x_yv"), sem("x_res_s"))

        def expert(j, rnd):
            return rnd * 2 + j // SG

        def tile_counts(engine):
            word = engine.alloc_register("round_word")
            engine.wait_ge(s_tiles, 3)

            def take(s, j, rnd):
                if j == 0:
                    engine.reg_mov(word, engine.value_load(words[0:1, at(rnd)], min_val=0, max_val=1023))

            def branch(own, j, work, skip, narrow=False):
                if j == 0:
                    engine.reg_mov(own, word)
                used = engine.snap(engine.snap(own) % 32) if j < SG else engine.snap(engine.snap(own) // 32)
                with engine.If(used > j % SG * QT):
                    if narrow:
                        with engine.If(used > j % SG * QT + QT // 2):
                            work(QT)
                        with engine.Else():
                            work(QT // 2)
                    else:
                        work()
                with engine.Else():
                    skip()

            return take, branch

        with nc.Block() as block:
            @block.sync
            def _(sp):
                def weights(s, j, rnd):
                    e = expert(j, rnd)
                    if j % SG or (isinstance(s, int) and e + 1 >= NX):
                        return
                    if isinstance(s, int) and e == 0:
                        sp.wait_ge(s_split, 1)
                    else:
                        sp.wait_ge(s_res, e * SG)
                    fetch(e + 1, (j // SG + 1) % 2)

                def fetch(e, h):
                    sp.dma_start(w1f[:, :, :], w1[at(e), :, :].rearrange("a (k p) f -> p (a k) f", p=P)).then_inc(s_w, 16)
                    sp.dma_start(w2f[:, :, :], w2[at(e), :, :].rearrange("a (k p) d -> p (a k) d", p=P)).then_inc(s_w, 16)
                    with nc.allow_non_contiguous_dma(reason="small vector"):
                        sp.dma_start(b1f[:, :], xb1[at(e), :].rearrange("a (c p) -> p (a c)", p=P)).then_inc(s_w, 16)
                    sp.dma_start(b2s[:, h, :], xb2[at(e), :].broadcast_to((P, D))).then_inc(s_w, 16)

                def load(s, j, rnd):
                    if not (isinstance(s, int) and s < RW):
                        sp.wait_ge(s_res, s - RW + 1)
                    sp.dma_start(row[:, j, :, :],
                                 buf[at(s, QN), :].rearrange("(t p) d -> p t d", p=P)).then_inc(s_row[j], 16)

                with nc.allow_non_contiguous_dma(reason="one word of the first slot of each tile"):
                    sp.dma_start(first_row[:, :, :], buf.rearrange("(e g n) d -> n e g d", g=SG * QT, n=P)[0:1, :, :, D + 2]
                                 ).then_inc(s_first, 16)
                fetch(0, 0)
                walk(sp, [(load, 0), (weights, 3)], NS, R8)

            @block.gpsimd
            def _(pool):
                take, branch = tile_counts(pool)
                lows = pool.alloc_register("lows_word")
                ready = counter(pool, "x_ready", R8 + 1 - 3)
                bound = pool.to_reg(N - 1)

                def low_hidden(s, j, rnd):
                    def work():
                        if not (isinstance(s, int) and s < 2):
                            pool.wait_ge(s_down, s - 1)
                        for c in range(FC):
                            pool.wait_ge(s_mid, s * FC + c + 1)
                            nc.gpsimd.tensor_tensor(midl[:, j % 2, c, :], midf[:, c % MB, :], midh[:, j % 2, c, :],
                                                    ALU.subtract).then_inc(s_mlo, 1)

                    def skip():
                        if not (isinstance(s, int) and s == 0):
                            pool.wait_ge(s_mlo, s * FC)
                        pool.sem_inc(s_mlo, FC)

                    branch(lows, j, work, skip)

                def scatter(s, j, rnd):
                    r = j % RR
                    wait_count(pool, s_res, s + 1, ready)
                    for t in range(QT):
                        pool.indirect_dma_start(
                            out, bass.IndirectOffsetOnAxis(ap=nodei[:, j, t:t + 1], axis=0),
                            res[:, r, t, :], None, bounds_check=bound, oob_is_err=False).then_inc(s_scat[j], 16)

                nc.gpsimd.memset(res[:, :, :, :], 0.0).then_inc(s_zero, 1)
                walk(pool, [(take, 0), (low_hidden, 1), (scatter, 3)], NS, R8)
                for j in range(RW):
                    pool.wait_ge(s_scat[j], 16 * QT * (NS // RW))

            @block.tensor
            def _(pe):
                take, branch = tile_counts(pe)
                ups = pe.alloc_register("ups_word")
                downs = pe.alloc_register("downs_word")

                def turn(s, j, rnd):
                    pe.wait_ge(s_xn, s + 1)
                    if not (isinstance(s, int) and s == 0):
                        pe.wait_ge(s_xlo, s)
                    for k in range(DK):
                        for t in range(QT):
                            ins = nc.tensor.transpose(turned[:, k, t * P:(t + 1) * P],
                                                      xn[:, t, k * P:(k + 1) * P], ident[:, :])
                    ins.then_inc(s_turn, 1)

                def product_up(s, j, rnd):
                    h = j // SG

                    def work(tiles):
                        pe.wait_ge(s_split, expert(j, rnd) + 1)
                        pe.wait_ge(s_xlo, s + 1)
                        for c in range(FC):
                            cols = slice(c * P, (c + 1) * P)
                            if not (isinstance(s, int) and s == 0 and c < MB):
                                pe.wait_ge(s_mid, s * FC + c + 1 - MB)
                            passes = [(w, x, k) for k in range(DK) for w, x in ((w1h, xTh), (w1h, xTl), (w1l, xTh))]
                            for n, (w, x, k) in enumerate(passes):
                                ins = nc.tensor.matmul(up[:, c % MB, 0:tiles * P], w[:, h, k, cols],
                                                       x[:, j % 2, k, 0:tiles * P],
                                                       start=(n == 0), stop=(n == len(passes) - 1))
                            ins.then_inc(s_up, 1)

                    def skip():
                        if not (isinstance(s, int) and s == 0):
                            pe.wait_ge(s_up, s * FC)
                        pe.sem_inc(s_up, FC)

                    branch(ups, j, work, skip, narrow=True)

                def product_down(s, j, rnd):
                    h = j // SG

                    def work(tiles):
                        pe.wait_ge(s_mlo, s * FC + FC)
                        if not (isinstance(s, int) and s == 0):
                            pe.wait_ge(s_yv, s * 7 - 6)
                        for t in range(tiles):
                            rows = slice(t * P, (t + 1) * P)
                            passes = [(m, w, k) for k in range(FC)
                                      for m, w in ((midh, w2h), (midh, w2l), (midl, w2h))]
                            for n, (m, w, k) in enumerate(passes):
                                ins = nc.tensor.matmul(down[:, t, :], m[:, j % 2, k, rows], w[:, h, k, :],
                                                       start=(n == 0), stop=(n == len(passes) - 1))
                        ins.then_inc(s_down, 1)

                    def skip():
                        if not (isinstance(s, int) and s == 0):
                            pe.wait_ge(s_down, s)
                        pe.sem_inc(s_down, 1)

                    branch(downs, j, work, skip, narrow=True)

                walk(pe, [(take, 0), (turn, 0), (product_up, 1), (product_down, 2)], NS, R8)

            @block.scalar
            def _(act):
                take, branch = tile_counts(act)
                mids = act.alloc_register("mids_word")

                def columns(s, j, rnd):
                    act.wait_ge(s_turn, s + 1)
                    if not (isinstance(s, int) and s < 2):
                        act.wait_ge(s_up, s * FC - FC)
                    nc.scalar.activation(xTh[:, j % 2, :, :], turned[:, :, :], ACT.Identity,
                                         scale=X_SCALE).then_inc(s_xT, 1)

                def expo(s, j, rnd):
                    act.wait_ge(s_row[j], rnd * 16 + 16)
                    if not (isinstance(s, int) and s == 0):
                        act.wait_ge(s_meta, s * 3)
                    nc.scalar.activation(ex[:, :, :], row[:, j, :, D + 4:ROW], ACT.Exp).then_inc(s_exp, 1)

                def hidden(s, j, rnd):
                    h = j // SG

                    def work():
                        if not (isinstance(s, int) and s < 2):
                            act.wait_ge(s_down, s - 1)
                        act.wait_ge(s_split, expert(j, rnd) + 1)
                        for c in range(FC):
                            act.wait_ge(s_up, s * FC + c + 1)
                            if not (isinstance(s, int) and s == 0 and c < MB):
                                act.wait_ge(s_mlo, s * FC + c + 1 - MB)
                            for m in (midf[:, c % MB, :], midh[:, j % 2, c, :]):
                                ins = nc.scalar.activation(m, up[:, c % MB, :], ACT.Relu, bias=b1s[:, h, c:c + 1],
                                                           scale=MID_SCALE / (X_SCALE * W_SCALE))
                            ins.then_inc(s_mid, 1)

                    def skip():
                        if not (isinstance(s, int) and s == 0):
                            act.wait_ge(s_mid, s * FC)
                        act.sem_inc(s_mid, FC)

                    branch(mids, j, work, skip)

                def split(s, j, rnd):
                    e = expert(j, rnd) + 1
                    if j % SG or (isinstance(s, int) and e >= NX):
                        return
                    if not (isinstance(s, int) and e == 1):
                        act.wait_ge(s_down, (e - 1) * SG)
                    high_weights(e, (j // SG + 1) % 2)

                def high_weights(e, h):
                    act.wait_ge(s_w, e * 64 + 64)
                    nc.scalar.activation(w1h[:, h, :, :], w1f[:, :, :], ACT.Identity, scale=W_SCALE)
                    nc.scalar.activation(w2h[:, h, :, :], w2f[:, :, :], ACT.Identity, scale=W_SCALE
                                         ).then_inc(s_whi, 1)

                high_weights(0, 0)
                walk(act, [(take, 0), (expo, 0), (columns, 0), (hidden, 1), (split, 3)], NS, R8)

            @block.vector
            def _(dve):
                dve.wait_ge(s_first, 16)
                nc.vector.tensor_scalar(taken[:, :, :], first_row[:, :, :], 0.5, None, ALU.is_gt).then_inc(s_tiles, 1)
                dve.wait_ge(s_tiles, 1)
                nc.vector.tensor_reduce(tiles[:, :, :].rearrange("p a b -> p (a b)"), taken[:, :, :], AX.X,
                                        ALU.add).then_inc(s_tiles, 1)
                dve.wait_ge(s_tiles, 2)
                nc.vector.scalar_tensor_tensor(out=words[:, :], in0=tiles[:, :, 1], scalar=32.0, in1=tiles[:, :, 0],
                                               op0=ALU.mult, op1=ALU.add).then_inc(s_tiles, 1)
                take, branch = tile_counts(dve)
                ends = dve.alloc_register("ends_word")

                def norm(s, j, rnd):
                    dve.wait_ge(s_row[j], rnd * 16 + 16)
                    if not (isinstance(s, int) and s == 0):
                        dve.wait_ge(s_turn, s)
                    for t in range(QT):
                        ins = nc.vector.tensor_scalar(xn[:, t, :], row[:, j, t, 0:D], row[:, j, t, D:D + 1],
                                                      row[:, j, t, D + 1:D + 2], ALU.mult, ALU.add)
                    ins.then_inc(s_xn, 1)

                def split(s, j, rnd):
                    e = expert(j, rnd) + 1
                    if j % SG or (isinstance(s, int) and e >= NX):
                        return
                    low_weights(e, (j // SG + 1) % 2)

                def low_weights(e, h):
                    dve.wait_ge(s_whi, e + 1)
                    nc.vector.tensor_scalar(b1s[:, h, :], b1f[:, :], MID_SCALE, None, ALU.mult)
                    nc.vector.scalar_tensor_tensor(out=w1l[:, h, :, :], in0=w1f[:, :, :], scalar=W_SCALE,
                                                   in1=w1h[:, h, :, :], op0=ALU.mult, op1=ALU.subtract)
                    nc.vector.scalar_tensor_tensor(out=w2l[:, h, :, :], in0=w2f[:, :, :], scalar=W_SCALE,
                                                   in1=w2h[:, h, :, :], op0=ALU.mult, op1=ALU.subtract
                                                   ).then_inc(s_split, 1)

                def low_columns(s, j, rnd):
                    dve.wait_ge(s_xT, s + 1)
                    nc.vector.scalar_tensor_tensor(out=xTl[:, j % 2, :, :], in0=turned[:, :, :], scalar=X_SCALE,
                                                   in1=xTh[:, j % 2, :, :], op0=ALU.mult, op1=ALU.subtract
                                                   ).then_inc(s_xlo, 1)

                def meta(s, j, rnd):
                    dve.wait_ge(s_exp, s + 1)
                    if not (isinstance(s, int) and s < RW):
                        dve.wait_ge(s_scat[j], rnd * (16 * QT))
                    nc.vector.tensor_reduce(tot[:, :], ex[:, :, :], AX.X, ALU.add).then_inc(s_meta, 1)
                    nc.vector.tensor_scalar(gone[:, :], row[:, j, :, D + 2], 0.5, SKIP, ALU.is_lt,
                                            ALU.mult).then_inc(s_meta, 1)
                    dve.wait_ge(s_meta, s * 3 + 2)
                    nc.vector.reciprocal(prob[:, j, :], tot[:, :])
                    nc.vector.scalar_tensor_tensor(out=nodei[:, j, :], in0=row[:, j, :, D + 2], scalar=-1.0,
                                                   in1=gone[:, :], op0=ALU.add, op1=ALU.add).then_inc(s_meta, 1)

                guard_seen = counter(dve, "x_guard_seen", (R8 - 3) * 7 + 6)

                def finish(s, j, rnd):
                    r = j % RR

                    def then(k, ins):
                        ins.then_inc(s_yv, 1)
                        dve.wait_ge(s_yv, s * 7 + k)

                    def work():
                        dve.wait_ge(s_down, s + 1)
                        dve.wait_ge(s_w, expert(j, rnd) * 64 + 64)
                        then(1, nc.vector.scalar_tensor_tensor(
                            out=yb[:, :, :], in0=down[:, :, :], scalar=1.0 / (MID_SCALE * W_SCALE),
                            in1=b2s[:, j // SG, :].unsqueeze(1).broadcast_to((P, QT, D)), op0=ALU.mult, op1=ALU.add))
                        then(2, nc.vector.tensor_tensor(y[:, :, :], yb[:, :, :],
                                                        prob[:, j, :].unsqueeze(2).broadcast_to((P, QT, D)), ALU.mult))
                        nc.vector.tensor_scalar(up1[:, :, :], y[:, :, :], 0.0, 1e4, ALU.is_gt, ALU.mult).then_inc(s_yv, 1)
                        nc.vector.tensor_scalar(dn1[:, :, :], y[:, :, :], 0.0, -1e4, ALU.is_lt, ALU.mult).then_inc(s_yv, 1)
                        then(5, nc.vector.tensor_scalar(fine[:, :, :], y[:, :, :], 0.0, 0.0, ALU.mult, ALU.is_equal))
                        nc.vector.tensor_tensor(up1[:, :, :], up1[:, :, :], dn1[:, :, :], ALU.add).then_inc(s_yv, 1)
                        wait_count(dve, s_yv, s * 7 + 6, guard_seen, 7)
                        then(7, nc.vector.copy_predicated(up1[:, :, :], fine[:, :, :], y[:, :, :]))
                        if not (isinstance(s, int) and s < RR):
                            dve.wait_ge(s_scat[(j - RR) % RW], (rnd + j // RR) * (16 * QT))
                        nc.vector.tensor_tensor(res[:, r, :, :], up1[:, :, :], row[:, j, :, 0:D],
                                                ALU.add).then_inc(s_res, 1)

                    def skip():
                        if not isinstance(s, int):
                            dve.reg_add(guard_seen, guard_seen, 7)
                        if not (isinstance(s, int) and s == 0):
                            dve.wait_ge(s_yv, s * 7)
                            dve.wait_ge(s_res, s)
                        dve.sem_inc(s_yv, 7)
                        dve.sem_inc(s_res, 1)

                    branch(ends, j, work, skip)

                low_weights(0, 0)
                dve.wait_ge(s_zero, 1)
                walk(dve, [(take, 0), (norm, 0), (meta, 0), (split, 4), (finish, 3), (low_columns, 0)], NS, R8)


def kernel(x, src, dst, L0_gnn_eps, L0_gnn_W1, L0_gnn_b1, L0_gnn_W2, L0_gnn_b2, L0_gnn_gamma, L0_gnn_beta,
           L0_ffn_gate_w, L0_ffn_gate_b, L0_ffn_w1, L0_ffn_b1, L0_ffn_w2, L0_ffn_b2):
    import concourse.bacc as bacc
    from concourse.bass_utils import run_bass_kernel_spmd

    def edge_tiles(a):
        a = np.asarray(a)
        return np.ascontiguousarray(a[:EFULL * P].reshape(EFULL, P).T), np.ascontiguousarray(a[EFULL * P:, None])

    src_full, src_tail = edge_tiles(src)
    dst_full, dst_tail = edge_tiles(dst)
    arrays = {
        "x": x, "src": src_full, "dst": dst_full, "src_tail": src_tail, "dst_tail": dst_tail, "eps": L0_gnn_eps,
        "W1": L0_gnn_W1, "b1": L0_gnn_b1, "W2": L0_gnn_W2, "b2": L0_gnn_b2, "gamma": L0_gnn_gamma,
        "beta": L0_gnn_beta, "gate_w": L0_ffn_gate_w, "gate_b": L0_ffn_gate_b, "w1": L0_ffn_w1, "xb1": L0_ffn_b1,
        "w2": L0_ffn_w2, "xb2": L0_ffn_b2,
    }
    nc = bacc.Bacc("TRN2", target_bir_lowering=False, num_devices=1)
    ins, aps = {}, {}
    for name, a in arrays.items():
        a = np.ascontiguousarray(a)
        ins[f"in_{name}"] = a
        aps[name] = nc.dram_tensor(f"in_{name}", a.shape, mybir.dt.from_np(a.dtype), kind="ExternalInput").ap()
    out = nc.dram_tensor("out", (N, D), F32, kind="ExternalOutput").ap()
    kernel_program(nc, out=out, **aps)
    return run_bass_kernel_spmd(nc, [ins], core_ids=[0]).results[0]["out"]
```
